# Optimizing a Trainium2 kernel written in Bass

```python
import numpy as np
import jax
import jax.numpy as jnp

def _softmax(x, axis=-1):
    return jax.nn.softmax(x, axis=axis)

def _gelu(x):
    return jax.nn.gelu(x, approximate=True)

def _silu(x):
    return jax.nn.silu(x)

def _sigmoid(x):
    return jax.nn.sigmoid(x)

def _layernorm(x, axis=-1, eps=1e-05):
    m = jnp.mean(x, axis=axis, keepdims=True)
    v = jnp.var(x, axis=axis, keepdims=True)
    return (x - m) / jnp.sqrt(v + eps)

def _scatter_add(tgt, idx, src, axis=0):
    return tgt.at[idx].add(src)

def _segment_sum(src, seg, n):
    return jax.ops.segment_sum(src, seg, n)
kernel_name = 'mk_adaln_d1_jaxref_r8_4bd825'

def setup_inputs(seed: int=0):
    np.random.seed(seed)
    _w = jnp.asarray

    def _L0_attn_setup():
        import math
        import jax, jax.numpy as jnp
        import numpy as np
        B, T, D, H, L = (8, 256, 128, 16, 4)
        DK = D // H
        EPS_LN = 1e-05
        EPS_ATTN = 1e-06

        def _layernorm(x, scale, bias):
            mu = jnp.mean(x, axis=-1, keepdims=True)
            var = jnp.mean(jnp.square(x - mu), axis=-1, keepdims=True)
            return (x - mu) * jax.lax.rsqrt(var + EPS_LN) * scale + bias

        def _sinusoidal_pos_emb(t, d):
            half = d // 2
            freq = jnp.exp(jnp.arange(half, dtype=jnp.float32) * (-math.log(10000.0) / (half - 1)))
            pos = (jnp.arange(t, dtype=jnp.float32) + 1.0)[:, None] * freq[None, :]
            return jnp.concatenate([jnp.sin(pos), jnp.cos(pos)], axis=-1)

        def _linear_attention(q, k, v):
            qp = jax.nn.elu(q) + 1.0
            kp = jax.nn.elu(k) + 1.0
            kv = jnp.einsum('bshd,bshm->bhmd', kp, v)
            ksum = jnp.sum(kp, axis=1)
            z = 1.0 / (jnp.einsum('blhd,bhd->blh', qp, ksum) + EPS_ATTN)
            return jnp.einsum('blhd,bhmd,blh->blhm', qp, kv, z)

        def _encoder_layer(x, Wq, bq, Wk, bk, Wv, bv, Wo, bo, W1, b1, W2, b2, ln1_s, ln1_b, ln2_s, ln2_b):
            b, t, d = x.shape
            h = _layernorm(x, ln1_s, ln1_b)
            q = (h @ Wq + bq).reshape(b, t, H, DK)
            k = (h @ Wk + bk).reshape(b, t, H, DK)
            v = (h @ Wv + bv).reshape(b, t, H, DK)
            attn = _linear_attention(q, k, v).reshape(b, t, d)
            x = x + (attn @ Wo + bo)
            h = _layernorm(x, ln2_s, ln2_b)
            h = jax.nn.relu(h @ W1 + b1) @ W2 + b2
            return x + h
        key = jax.random.key(seed)
        ks = jax.random.split(key, 8)
        w = lambda k, shape: jax.random.normal(k, shape, dtype=jnp.float32) * 0.02
        return {'x_in': jax.random.normal(ks[0], (B, T, D), dtype=jnp.float32), 'Wq': w(ks[1], (L, D, D)), 'bq': jnp.zeros((L, D), jnp.float32), 'Wk': w(ks[2], (L, D, D)), 'bk': jnp.zeros((L, D), jnp.float32), 'Wv': w(ks[3], (L, D, D)), 'bv': jnp.zeros((L, D), jnp.float32), 'Wo': w(ks[4], (L, D, D)), 'bo': jnp.zeros((L, D), jnp.float32), 'W1': w(ks[5], (L, D, 4 * D)), 'b1': jnp.zeros((L, 4 * D), jnp.float32), 'W2': w(ks[6], (L, 4 * D, D)), 'b2': jnp.zeros((L, D), jnp.float32), 'ln1_s': jnp.ones((L, D), jnp.float32), 'ln1_b': jnp.zeros((L, D), jnp.float32), 'ln2_s': jnp.ones((L, D), jnp.float32), 'ln2_b': jnp.zeros((L, D), jnp.float32), 'lnf_s': jnp.ones((D,), jnp.float32), 'lnf_b': jnp.zeros((D,), jnp.float32)}
    _L0_attn_in = _L0_attn_setup()

    def _L0_ffn_setup():
        import jax, jax.numpy as jnp
        import numpy as np
        TOP_K = 2
        NUM_EXPERTS = 8
        key = jax.random.key(seed)
        ks = jax.random.split(key, 8)
        h, d, ds, E = (128, 64, 128, NUM_EXPERTS)
        s = 1.0 / np.sqrt(h)
        return {'x': jax.random.normal(ks[0], (2, 256, h), jnp.float32), 'router': jax.random.normal(ks[1], (h, E), jnp.float32) * s, 'experts_gate': jax.random.normal(ks[2], (E, h, d), jnp.float32) * s, 'experts_up': jax.random.normal(ks[3], (E, h, d), jnp.float32) * s, 'experts_down': jax.random.normal(ks[4], (E, d, h), jnp.float32) * (1.0 / np.sqrt(d)), 'shared_gate': jax.random.normal(ks[5], (h, ds), jnp.float32) * s, 'shared_up': jax.random.normal(ks[6], (h, ds), jnp.float32) * s, 'shared_down': jax.random.normal(ks[7], (ds, h), jnp.float32) * (1.0 / np.sqrt(ds))}
    _L0_ffn_in = _L0_ffn_setup()
    _L0_c = _w((lambda *s: np.random.randn(*s).astype(np.float32) * 0.05)(16, 128))
    _L0_wmod = _w((lambda *s: np.random.randn(*s).astype(np.float32) * 0.05)(128, 6 * 128) * 128 ** (-0.5))
    _d = {'L0_attn_x_in': _L0_attn_in['x_in'], 'L0_attn_Wq': _L0_attn_in['Wq'], 'L0_attn_bq': _L0_attn_in['bq'], 'L0_attn_Wk': _L0_attn_in['Wk'], 'L0_attn_bk': _L0_attn_in['bk'], 'L0_attn_Wv': _L0_attn_in['Wv'], 'L0_attn_bv': _L0_attn_in['bv'], 'L0_attn_Wo': _L0_attn_in['Wo'], 'L0_attn_bo': _L0_attn_in['bo'], 'L0_attn_W1': _L0_attn_in['W1'], 'L0_attn_b1': _L0_attn_in['b1'], 'L0_attn_W2': _L0_attn_in['W2'], 'L0_attn_b2': _L0_attn_in['b2'], 'L0_attn_ln1_s': _L0_attn_in['ln1_s'], 'L0_attn_ln1_b': _L0_attn_in['ln1_b'], 'L0_attn_ln2_s': _L0_attn_in['ln2_s'], 'L0_attn_ln2_b': _L0_attn_in['ln2_b'], 'L0_attn_lnf_s': _L0_attn_in['lnf_s'], 'L0_attn_lnf_b': _L0_attn_in['lnf_b'], 'L0_ffn_router': _L0_ffn_in['router'], 'L0_ffn_experts_gate': _L0_ffn_in['experts_gate'], 'L0_ffn_experts_up': _L0_ffn_in['experts_up'], 'L0_ffn_experts_down': _L0_ffn_in['experts_down'], 'L0_ffn_shared_gate': _L0_ffn_in['shared_gate'], 'L0_ffn_shared_up': _L0_ffn_in['shared_up'], 'L0_ffn_shared_down': _L0_ffn_in['shared_down'], 'L0_c': _L0_c, 'L0_wmod': _L0_wmod}
    _x0 = _d['L0_attn_x_in']
    _d['L0_attn_x_in'] = jax.random.normal(jax.random.fold_in(jax.random.key(seed), 1), (16, 256, 128), dtype=_x0.dtype)
    del _x0
    return _d

def reference(L0_attn_x_in, L0_attn_Wq, L0_attn_bq, L0_attn_Wk, L0_attn_bk, L0_attn_Wv, L0_attn_bv, L0_attn_Wo, L0_attn_bo, L0_attn_W1, L0_attn_b1, L0_attn_W2, L0_attn_b2, L0_attn_ln1_s, L0_attn_ln1_b, L0_attn_ln2_s, L0_attn_ln2_b, L0_attn_lnf_s, L0_attn_lnf_b, L0_ffn_router, L0_ffn_experts_gate, L0_ffn_experts_up, L0_ffn_experts_down, L0_ffn_shared_gate, L0_ffn_shared_up, L0_ffn_shared_down, L0_c, L0_wmod):

    def _L0_attn_ref(x_in, Wq, bq, Wk, bk, Wv, bv, Wo, bo, W1, b1, W2, b2, ln1_s, ln1_b, ln2_s, ln2_b, lnf_s, lnf_b):
        import math
        import jax, jax.numpy as jnp
        import numpy as np
        B, T, D, H, L = (8, 256, 128, 16, 4)
        DK = D // H
        EPS_LN = 1e-05
        EPS_ATTN = 1e-06

        def _layernorm(x, scale, bias):
            mu = jnp.mean(x, axis=-1, keepdims=True)
            var = jnp.mean(jnp.square(x - mu), axis=-1, keepdims=True)
            return (x - mu) * jax.lax.rsqrt(var + EPS_LN) * scale + bias

        def _sinusoidal_pos_emb(t, d):
            half = d // 2
            freq = jnp.exp(jnp.arange(half, dtype=jnp.float32) * (-math.log(10000.0) / (half - 1)))
            pos = (jnp.arange(t, dtype=jnp.float32) + 1.0)[:, None] * freq[None, :]
            return jnp.concatenate([jnp.sin(pos), jnp.cos(pos)], axis=-1)

        def _linear_attention(q, k, v):
            qp = jax.nn.elu(q) + 1.0
            kp = jax.nn.elu(k) + 1.0
            kv = jnp.einsum('bshd,bshm->bhmd', kp, v)
            ksum = jnp.sum(kp, axis=1)
            z = 1.0 / (jnp.einsum('blhd,bhd->blh', qp, ksum) + EPS_ATTN)
            return jnp.einsum('blhd,bhmd,blh->blhm', qp, kv, z)

        def _encoder_layer(x, Wq, bq, Wk, bk, Wv, bv, Wo, bo, W1, b1, W2, b2, ln1_s, ln1_b, ln2_s, ln2_b):
            b, t, d = x.shape
            h = _layernorm(x, ln1_s, ln1_b)
            q = (h @ Wq + bq).reshape(b, t, H, DK)
            k = (h @ Wk + bk).reshape(b, t, H, DK)
            v = (h @ Wv + bv).reshape(b, t, H, DK)
            attn = _linear_attention(q, k, v).reshape(b, t, d)
            x = x + (attn @ Wo + bo)
            h = _layernorm(x, ln2_s, ln2_b)
            h = jax.nn.relu(h @ W1 + b1) @ W2 + b2
            return x + h
        b, t, d = x_in.shape
        x = math.sqrt(d) * x_in + _sinusoidal_pos_emb(t, d)[None, :, :]
        for i in range(L):
            x = _encoder_layer(x, Wq[i], bq[i], Wk[i], bk[i], Wv[i], bv[i], Wo[i], bo[i], W1[i], b1[i], W2[i], b2[i], ln1_s[i], ln1_b[i], ln2_s[i], ln2_b[i])
        return _layernorm(x, lnf_s, lnf_b)

    def _L0_ffn_ref(x, router, experts_gate, experts_up, experts_down, shared_gate, shared_up, shared_down):
        import jax, jax.numpy as jnp
        import numpy as np
        TOP_K = 2
        NUM_EXPERTS = 8
        b, s, h = x.shape
        E = router.shape[1]
        shared_act = jax.nn.silu(jnp.einsum('bsh,hd->bsd', x, shared_gate))
        shared_up_out = jnp.einsum('bsh,hd->bsd', x, shared_up)
        shared_out = jnp.einsum('bsd,dh->bsh', shared_act * shared_up_out, shared_down)
        router_probs = jax.nn.softmax(jnp.einsum('bsh,he->bse', x, router), axis=-1)
        topk_probs, topk_idx = jax.lax.top_k(router_probs, TOP_K)
        coef = jnp.sum(jax.nn.one_hot(topk_idx, E, dtype=x.dtype) * topk_probs[..., None], axis=2)
        coef = coef.reshape(b * s, E)
        x_flat = x.reshape(b * s, h)
        gate = jnp.einsum('th,ehd->etd', x_flat, experts_gate)
        up = jnp.einsum('th,ehd->etd', x_flat, experts_up)
        expert_out = jnp.einsum('etd,edh->eth', jax.nn.silu(gate) * up, experts_down)
        routed = jnp.einsum('eth,te->th', expert_out, coef)
        return routed.reshape(b, s, h) + shared_out
    x = L0_attn_x_in
    mod = (_silu(L0_c) @ L0_wmod).reshape(L0_c.shape[0], 6, 1, -1)
    sa, ca, ga, sb, cb, gb = (mod[:, 0], mod[:, 1], mod[:, 2], mod[:, 3], mod[:, 4], mod[:, 5])
    ga = (2 * (ga >= 0) - 1) * jnp.maximum(jnp.abs(ga), 0.25)
    gb = (2 * (gb >= 0) - 1) * jnp.maximum(jnp.abs(gb), 0.25)
    h = _layernorm(x, axis=-1) * (1 + ca) + sa
    x = x + ga * _L0_attn_ref(h, L0_attn_Wq, L0_attn_bq, L0_attn_Wk, L0_attn_bk, L0_attn_Wv, L0_attn_bv, L0_attn_Wo, L0_attn_bo, L0_attn_W1, L0_attn_b1, L0_attn_W2, L0_attn_b2, L0_attn_ln1_s, L0_attn_ln1_b, L0_attn_ln2_s, L0_attn_ln2_b, L0_attn_lnf_s, L0_attn_lnf_b)
    h = _layernorm(x, axis=-1) * (1 + cb) + sb
    x = x + gb * _L0_ffn_ref(h, L0_ffn_router, L0_ffn_experts_gate, L0_ffn_experts_up, L0_ffn_experts_down, L0_ffn_shared_gate, L0_ffn_shared_up, L0_ffn_shared_down)
    return x

_drawn_inputs = setup_inputs


def setup_inputs(seed=0):
    import zlib

    import numpy as np

    out = dict(_drawn_inputs(seed))
    spreads = {'L0_attn_bq': (0.0, 2.0),
     'L0_attn_bk': (0.0, 2.0),
     'L0_attn_bv': (0.0, 0.8),
     'L0_attn_bo': (0.0, 2.0),
     'L0_attn_b1': (0.0, 0.8),
     'L0_attn_b2': (0.0, 2.0),
     'L0_attn_ln1_s': (1.0, 0.6),
     'L0_attn_ln1_b': (0.0, 0.8),
     'L0_attn_ln2_s': (1.0, 0.6),
     'L0_attn_ln2_b': (0.0, 0.8),
     'L0_attn_lnf_s': (1.0, 0.2),
     'L0_attn_lnf_b': (0.0, 0.309)}
    factors = {'L0_attn_Wq': 31.591,
     'L0_attn_Wk': 23.164,
     'L0_attn_Wv': 8.0,
     'L0_attn_Wo': 8.0,
     'L0_attn_W1': 8.0,
     'L0_attn_W2': 8.0}
    for name, (base, spread) in spreads.items():
        noise = np.random.default_rng([zlib.crc32(name.encode()), seed]).standard_normal(out[name].shape)
        drawn = base * np.exp(spread * noise) if base else spread * noise
        out[name] = jnp.asarray(drawn.astype(out[name].dtype))
    for name, factor in factors.items():
        out[name] = (out[name] * factor).astype(out[name].dtype)
    return out
```

```python
from contextlib import ExitStack

import numpy as np

import concourse.bass as bass
from concourse import mybir
from concourse.alu_op_type import AluOpType as ALU

F32 = mybir.dt.float32
BF16 = mybir.dt.bfloat16
ACT = mybir.ActivationFunctionType
AXX = mybir.AxisListType.X

BATCH, T, D = 16, 256, 128
LAYERS, HEADS, FF = 4, 16, 512
DK = D // HEADS
EXPERTS, DE, TOP = 8, 64, 2
P = 128
CHAINS = 2
TILES = 4
SEQS = TILES * P // T
HALF = TILES // SEQS
GT = TILES * P
STEPS = BATCH // (SEQS * CHAINS)
CH = FF // P
VW = D + HEADS
QKV = 3 * D
MOD = 5 * D
EPS = 1e-5
EPS_ATTN = 1e-6
NORMS = 2 * LAYERS + 3

C_ID = 0
C_MASK = C_ID + P
C_TRI = C_MASK + VW
C_POS = C_TRI + EXPERTS * EXPERTS
C_BASE = C_POS + T // P * D
C_SEL = C_BASE + P
C_HOT = C_SEL + CH * P
C_ROW = C_HOT + BATCH * P
C_ALL = C_ROW + P


def constants():
    k = np.zeros((P, C_ALL), np.float32)
    p = np.arange(P)
    k[:, C_ID:C_ID + P] = np.eye(P)
    k[:, C_MASK:C_MASK + D] = p[:, None] // DK == p[None, :] // DK
    k[:, C_MASK + D:C_MASK + VW] = p[:, None] // DK == np.arange(HEADS)[None, :]
    e = np.arange(EXPERTS)
    k[:, C_TRI:C_TRI + EXPERTS ** 2] = (e[None, :] < e[:, None]).reshape(1, -1)
    half = D // 2
    freq = np.exp(np.arange(half, dtype=np.float32) * np.float32(-np.log(10000.0) / (half - 1)))
    pos = (np.arange(T, dtype=np.float32) + np.float32(1))[:, None] * freq[None, :]
    pos = np.concatenate([np.sin(pos), np.cos(pos)], axis=-1)
    k[:, C_POS:C_POS + T // P * D] = pos.reshape(T // P, P, D).transpose(1, 0, 2).reshape(P, -1)
    base = np.eye(P)
    base[P - 1, :] = -1
    k[:, C_BASE:C_BASE + P] = base
    for c in range(CH):
        for m in range(P):
            k[2 * c + m // DE + EXPERTS * np.arange(3), C_SEL + c * P + m] = 1
    for s in range(BATCH):
        k[s, C_HOT + s * P:C_HOT + (s + 1) * P] = 1
    k[0, C_ROW + P - 1] = 1
    return k


class Signal:

    def __init__(self, sem, per):
        self.sem, self.per = sem, per

    def value(self, i, n):
        return i * self.per + n


def program(nc, x_in, Wq, bq, Wk, bk, Wv, bv, Wo, bo, W1, b1, W2, b2, ln1_s, ln1_b, ln2_s, ln2_b, lnf_s, lnf_b,
            router, e_gate, e_up, e_down, s_gate, s_up, s_down, cond, wmod, consts, out):
    nc.disable_value_cache = True
    ctx = ExitStack()
    with ctx:
        def sb(name, shape, dt=F32):
            return ctx.enter_context(nc.sbuf_tensor(name, shape, dt))

        def sem(name):
            return ctx.enter_context(nc.semaphore(name))

        K = sb("K", [P, C_ALL])
        ident, base = K[:, C_ID:C_ID + P], K[:, C_BASE:C_BASE + P]
        headmask = K[:, C_MASK:C_MASK + VW]
        tri = K[:, C_TRI:C_TRI + EXPERTS ** 2].rearrange("p (j k) -> p j k", k=EXPERTS)
        pos = K[:, C_POS:C_POS + T // P * D]
        last_row = K[0:1, C_ROW:C_ROW + P]
        ident16 = sb("ident16", [P, P], BF16)
        sel16 = sb("sel16", [3 * EXPERTS, CH * P], BF16)
        X = sb("X", [P, BATCH * T // P * D])
        rows = sb("rows", [1, LAYERS * (QKV + FF)])
        par = sb("par", [4 * LAYERS + BATCH, D])
        parT = sb("parT", [P, 4 * LAYERS + BATCH])
        condT = sb("condT", [P, BATCH])
        wqkv = sb("wqkv", [P, LAYERS, QKV])
        w1 = sb("w1", [P, LAYERS, FF])
        w2 = sb("w2", [P, LAYERS, CH, D])
        wo = sb("wo", [P, LAYERS, D])
        bo_all = sb("bo_all", [P, LAYERS, D])
        b2_all = sb("b2_all", [P, LAYERS, D])
        fold = sb("fold", [P, 2, P])
        wm = sb("wm", [P, 6 * D])
        lnf = sb("lnf", [BATCH, 2 * D])
        mod = sb("mod", [BATCH, 6 * D])
        modp = sb("modp", [BATCH, MOD])
        sgn = sb("sgn", [BATCH, 2 * D])
        M = sb("M", [P, BATCH, MOD])
        shiftT = sb("shiftT", [P, BATCH])
        scaleT = sb("scaleT", [P, BATCH])
        wr = sb("wr", [P, EXPERTS])
        wg = sb("wg", [P, CH + 1, P])
        wu = sb("wu", [P, CH + 1, P])
        wd = sb("wd", [P, CH + 1, D])
        neghalf = sb("neghalf", [P, HALF])
        epsilon = sb("epsilon", [P, HALF])

        class Chain:
            pass

        chains = []
        for c in range(CHAINS):
            b = Chain()
            b.c = c
            n = "AB"[c]
            b.x = sb("x" + n, [P, TILES, D])
            b.stat = sb("stat" + n, [P, TILES, 6])
            b.mv = sb("mv" + n, [P, TILES, 2])
            b.ve = sb("ve" + n, [P, TILES])
            b.rstd = sb("rstd" + n, [P, TILES])
            b.xn = sb("xn" + n, [P, TILES, D])
            b.z = sb("z" + n, [P, TILES, D])
            b.xT = sb("xT" + n, [P, GT])
            b.eq = sb("eq" + n, [P, GT])
            b.ek = sb("ek" + n, [P, TILES, D])
            b.qp = sb("qp" + n, [P, GT])
            b.kp = sb("kp" + n, [P, TILES, D])
            b.v = sb("v" + n, [P, TILES, VW])
            b.kv = sb("kv" + n, [P, SEQS, VW])
            b.den = sb("den" + n, [P, TILES, HEADS])
            b.rden = sb("rden" + n, [P, TILES, HEADS])
            b.att = sb("att" + n, [P, TILES, D])
            b.attT = sb("attT" + n, [P, GT])
            b.h = sb("h" + n, [P, CH, GT])
            b.y = b.att
            b.sig = [b.eq[:, :], b.ek[:, :, :].rearrange("p t f -> p (t f)")]
            b.hs = b.qp
            b.gu = [b.attT[:, :], b.z[:, :, :].rearrange("p t f -> p (t f)")]
            b.lg = sb("lg" + n, [P, TILES, EXPERTS])
            b.mx = sb("mx" + n, [P, TILES])
            b.ls = sb("ls" + n, [P, TILES, EXPERTS])
            b.ex = sb("ex" + n, [P, TILES, EXPERTS])
            b.gt = sb("gt" + n, [P, TILES, EXPERTS, EXPERTS])
            b.tie = sb("tie" + n, [P, TILES, EXPERTS, EXPERTS])
            b.rank = sb("rank" + n, [P, TILES, EXPERTS])
            b.sum = sb("sum" + n, [P, TILES])
            b.rsum = sb("rsum" + n, [P, TILES])
            b.coef = sb("coef" + n, [P, TILES, EXPERTS])
            b.rest = sb("rest" + n, [P, TILES, EXPERTS])
            b.rest2 = sb("rest2" + n, [P, TILES, EXPERTS])
            b.parts = sb("parts" + n, [P, TILES, 3, EXPERTS], BF16)
            b.coefT = sb("coefT" + n, [3 * EXPERTS, GT], BF16)
            b.ps = ctx.enter_context(nc.psum_tensor("ps" + n, [P, 4, 512], F32))

            def sig(name, per, n=n):
                return Signal(sem(name + n), per)

            b.s_moved = sig("moved", 2 * 2 * LAYERS + 2 + 2)
            b.s_moments = sig("moments", NORMS * TILES)
            b.s_ve = sig("ve", NORMS * 2)
            b.s_rstd = sig("rstd", NORMS * 2)
            b.s_normed = sig("normed", NORMS * 2)
            b.s_biased = sig("biased", 2 * LAYERS)
            b.s_tps = sig("tps", 2 * (2 * LAYERS + 1))
            b.s_xT = sig("xT", 2 * (2 * LAYERS + 1))
            b.s_kvps = sig("kvps", 2 * LAYERS)
            b.s_qps = sig("qps", LAYERS)
            b.s_v = sig("v", 2 * LAYERS)
            b.s_kp = sig("kp", 2 * LAYERS)
            b.s_eq = sig("eq", LAYERS)
            b.s_qp = sig("qp", LAYERS)
            b.s_sumps = sig("sumps", 2 * LAYERS)
            b.s_kv = sig("kv", 2 * LAYERS)
            b.s_attps = sig("attps", 2 * LAYERS)
            b.s_den = sig("den", 2 * LAYERS)
            b.s_rden = sig("rden", 2 * LAYERS)
            b.s_att = sig("att", 2 * LAYERS)
            b.s_atps = sig("atps", 2 * LAYERS)
            b.s_attT = sig("attT", 2 * LAYERS)
            b.s_wops = sig("wops", 2 * LAYERS)
            b.s_w1ps = sig("w1ps", CH * LAYERS)
            b.s_h = sig("h", CH * LAYERS)
            b.s_w2ps = sig("w2ps", 2 * LAYERS)
            b.s_mod = sig("mod", 4 * 2)
            b.s_rps = sig("rps", 1)
            b.s_route = sig("route", 17)
            b.s_ex = sig("ex", 1)
            b.s_cps = sig("cps", 1)
            b.s_coefT = sig("coefT", 1)
            b.s_gps = sig("gps", CH + 1)
            b.s_ups = sig("ups", CH + 1)
            b.s_cbps = sig("cbps", CH)
            b.s_sig = sig("sig", CH + 1)
            b.s_gu = sig("gu", CH + 1)
            b.s_hid = sig("hid", CH)
            b.s_downps = sig("downps", 2)
            b.s_gated = sig("gated", 2)
            b.s_out = sig("out", 2)
            chains.append(b)
        A, B = chains

        s_k, s_par, s_rows, s_lnf, s_wm = sem("k"), sem("par"), sem("rowsin"), sem("lnf"), sem("wm")
        s_wqkv, s_w1, s_rest, s_wmoe = sem("wqkv"), sem("w1in"), sem("wrest"), sem("wmoe")
        s_x = sem("xin")
        s_stored = sem("stored")
        s_const = sem("const")
        s_c16 = sem("c16")
        s_plus = sem("plus")
        s_parps = sem("parps")
        s_parT = sem("parT")
        s_condT = sem("condT")
        s_modps = sem("modps")
        s_modsb = sem("modsb")
        s_rowps = sem("rowps")
        s_rowsb = sem("rowsb")
        s_fold = sem("fold")
        s_foldps = sem("foldps")
        s_folded = sem("folded")

        block = ctx.enter_context(nc.Block())

        def seq_of(b, i, h):
            return (i * CHAINS + b.c) * SEQS + h

        def x_cols(b, i, t, n=1):
            return bass.ds(((i * CHAINS + b.c) * TILES + t) * D, n * D)

        def mod_row(b, i, h, k):
            r = M[:, bass.ds(seq_of(b, i, h), 1), k * D:(k + 1) * D]
            return r.to_broadcast([P, HALF, D])

        def bank_of(item):
            return item % 4

        items = [(kind, c) for c in range(CH) for kind in ("gate", "up", "coef")] + [("gate", CH), ("up", CH)]
        items += [("down", 0), ("down", 1)]

        def left(b, item):
            kind, c = items[item]
            return {"gate": b.s_sig, "up": b.s_gu, "coef": b.s_hid}[kind], c + 1

        @block.sync
        def _(sync):
            sync.dma_start(K[:, :], consts).then_inc(s_k, 16)
            for n, a in enumerate((ln1_s, ln1_b, ln2_s, ln2_b)):
                sync.dma_start(par[n * LAYERS:(n + 1) * LAYERS, :], a).then_inc(s_par, 16)
            sync.dma_start(par[4 * LAYERS:, :], cond).then_inc(s_par, 16)
            tiles_in = x_in.rearrange("b (t p) f -> p (b t) f", p=P)
            Xv = X[:, :].rearrange("p (n f) -> p n f", f=D)
            for n in range(STEPS):
                k = CHAINS * TILES
                sync.dma_start(Xv[:, n * k:(n + 1) * k, :], tiles_in[:, n * k:(n + 1) * k, :]).then_inc(s_x, 16)
            sync.dma_start(wo[:, :, :], Wo.rearrange("l k n -> k l n")).then_inc(s_rest, 16)
            sync.dma_start(w2[:, :, :, :].rearrange("p l c n -> p (l c) n"),
                           W2.rearrange("l (c p) n -> p (l c) n", p=P)).then_inc(s_rest, 16)
            sync.dma_start(bo_all[:, :, :].rearrange("p l n -> p (l n)"),
                           bo.rearrange("(a l) n -> a (l n)", a=1).to_broadcast([P, LAYERS * D])).then_inc(s_rest, 16)
            sync.dma_start(b2_all[:, :, :].rearrange("p l n -> p (l n)"),
                           b2.rearrange("(a l) n -> a (l n)", a=1).to_broadcast([P, LAYERS * D])).then_inc(s_rest, 16)
            out_tiles = out.rearrange("b (t p) f -> (b t) p f", p=P)
            with sync.Fori(0, STEPS) as i:
                for b in chains:
                    for h in range(SEQS):
                        sync.wait_ge(b.s_out.sem, b.s_out.value(i, h + 1))
                        first = (i * CHAINS + b.c) * TILES + h * HALF
                        sync.dma_start(out_tiles[bass.ds(first, HALF), :, :].rearrange("t p f -> p t f"),
                                       X[:, x_cols(b, i, h * HALF, HALF)].rearrange("p (t f) -> p t f", f=D))\
                            .then_inc(s_stored, 16)
            sync.wait_ge(s_stored, 16 * STEPS * CHAINS * SEQS)

        @block.scalar
        def _(act):
            for n, a in enumerate((Wq, Wk, Wv)):
                act.dma_start(wqkv[:, :, n * D:(n + 1) * D], a.rearrange("l k n -> k l n")).then_inc(s_wqkv, 16)
            rq = rows[:, 0:LAYERS * QKV].rearrange("a (l n) -> a l n", n=QKV)
            for n, a in enumerate((bq, bk, bv)):
                act.dma_start(rq[:, :, n * D:(n + 1) * D], a.rearrange("(a l) n -> a l n", a=1)).then_inc(s_rows, 16)
            act.dma_start(rows[:, LAYERS * QKV:], b1.rearrange("(a l) n -> a (l n)", a=1)).then_inc(s_rows, 16)
            act.dma_start(w1[:, :, :], W1.rearrange("l k n -> k l n")).then_inc(s_w1, 16)
            act.dma_start(wm[:, :], wmod).then_inc(s_wm, 16)
            for n, a in enumerate((lnf_s, lnf_b)):
                act.dma_start(lnf[:, n * D:(n + 1) * D],
                              a.rearrange("(a n) -> a n", a=1).to_broadcast([BATCH, D])).then_inc(s_lnf, 16)
            act.dma_start(wr[:, :], router).then_inc(s_wmoe, 16)
            for w, e, s in ((wg, e_gate, s_gate), (wu, e_up, s_up)):
                act.dma_start(w[:, 0:CH, :].rearrange("p c (e d) -> p (c e) d", d=DE),
                              e.rearrange("e h d -> h e d")).then_inc(s_wmoe, 16)
                act.dma_start(w[:, CH, :], s).then_inc(s_wmoe, 16)
            act.dma_start(wd[:, 0:CH, :], e_down.rearrange("(c e) d n -> (e d) c n", e=2)).then_inc(s_wmoe, 16)
            act.dma_start(wd[:, CH, :], s_down).then_inc(s_wmoe, 16)

            act.wait_ge(s_parT, 1)
            act.activation(condT[:, :], parT[:, 4 * LAYERS:], ACT.Silu).then_inc(s_condT, 1)
            for n in range(2 * LAYERS):
                w = wqkv[:, n // 2, :] if n % 2 == 0 else w1[:, n // 2, :]
                act.wait_ge(s_foldps, n + 1)
                act.activation(w, B.ps[:, n % 2, 0:w.shape[-1]], ACT.Copy).then_inc(s_folded, 1)
            for s in range(BATCH):
                act.wait_ge(s_rowps, s + 1)
                bank = 2 * (s % 2)
                act.activation(M[:, s, :], A.ps[:, bank:bank + 2, :].rearrange("p k n -> p (k n)")[:, 0:MOD],
                               ACT.Copy).then_inc(s_rowsb, 1)

            def transposed(b, i, n):
                first = 0 if n % 2 == 0 else 2
                for h in range(2):
                    act.wait_ge(b.s_tps.sem, b.s_tps.value(i, 2 * n + h + 1))
                    act.activation(b.xT[:, h * T:(h + 1) * T], b.ps[:, first + h, 0:T], ACT.Copy)\
                        .then_inc(b.s_xT.sem, 1)

            def exps(b, i, l):
                for h in range(2):
                    act.wait_ge(b.s_kvps.sem, b.s_kvps.value(i, 2 * l + h + 1))
                    both = b.ps[:, 2 + h, :].rearrange("p (t n) -> p t n", n=2 * D)
                    t = slice(h * HALF, (h + 1) * HALF)
                    act.activation(b.ek[:, t, :], both[:, :, 0:D], ACT.Exp, bias=-1.0)
                    act.activation(b.v[:, t, 0:D], both[:, :, D:], ACT.Copy).then_inc(b.s_v.sem, 1)
                act.wait_ge(b.s_qps.sem, b.s_qps.value(i, l + 1))
                act.activation(b.eq[:, :], b.ps[:, 0, :], ACT.Exp, bias=-1.0).then_inc(b.s_eq.sem, 1)

            def att_transposed(b, i, l):
                for h in range(2):
                    act.wait_ge(b.s_atps.sem, b.s_atps.value(i, 2 * l + h + 1))
                    act.activation(b.attT[:, h * T:(h + 1) * T], b.ps[:, 2 + h, 0:T], ACT.Copy)\
                        .then_inc(b.s_attT.sem, 1)

            def relus(b, i, l, some):
                for c in some:
                    act.wait_ge(b.s_w1ps.sem, b.s_w1ps.value(i, l * CH + c + 1))
                    act.activation(b.h[:, c, :], b.ps[:, c, :], ACT.Relu).then_inc(b.s_h.sem, 1)

            def router_exp(b, i):
                act.wait_ge(b.s_route.sem, b.s_route.value(i, 3))
                act.activation(b.ex[:, :, :], b.ls[:, :, :], ACT.Exp).then_inc(b.s_ex.sem, 1)

            def coefs(b, i):
                act.wait_ge(b.s_cps.sem, b.s_cps.value(i, 1))
                act.activation(b.coefT[:, :], b.ps[0:3 * EXPERTS, 3, 0:GT // 2].bitcast(BF16), ACT.Copy)\
                    .then_inc(b.s_coefT.sem, 1)

            def silus(b, i, some):
                for c in some:
                    act.wait_ge(b.s_gps.sem, b.s_gps.value(i, c + 1))
                    if c >= 2:
                        act.wait_ge(b.s_gu.sem, b.s_gu.value(i, c - 1))
                    act.activation(b.sig[c % 2], b.ps[:, bank_of(items.index(("gate", c))), :], ACT.Silu)\
                        .then_inc(b.s_sig.sem, 1)

            with act.Fori(0, STEPS) as i:
                for n in range(2 * LAYERS + 2):
                    a, f = (A, B) if n % 2 == 0 else (B, A)
                    l, m = n // 2, (n - 1) // 2
                    attends = l < LAYERS
                    feeds = 0 <= m < LAYERS
                    if attends:
                        transposed(a, i, 2 * l)
                    if feeds:
                        transposed(f, i, 2 * m + 1)
                    if attends:
                        exps(a, i, l)
                    if feeds:
                        relus(f, i, m, range(CH))
                    if attends:
                        att_transposed(a, i, l)
                    if not attends:
                        router_exp(a, i)
                        silus(a, i, range(1))
                        coefs(a, i)
                        silus(a, i, range(1, CH + 1))

        @block.gpsimd
        def _(pool):
            pool.memset(neghalf[:, :], -0.5).then_inc(s_const, 1)
            pool.memset(epsilon[:, :], EPS).then_inc(s_const, 1)
            for b in chains:
                pool.memset(b.xn[:, :, D - 1:D], 1.0).then_inc(s_const, 1)
                pool.memset(b.v[:, :, D:], 1.0).then_inc(s_const, 1)
            pool.wait_ge(s_const, 6)

            def rstd(b, i, n):
                for h in range(2):
                    t = slice(h * HALF, (h + 1) * HALF)
                    pool.wait_ge(b.s_moments.sem, b.s_moments.value(i, n * TILES + (h + 1) * HALF))
                    pool.tensor_tensor(b.ve[:, t], b.mv[:, t, 1], epsilon[:, :], ALU.add).then_inc(b.s_ve.sem, 1)
                    pool.wait_ge(b.s_ve.sem, b.s_ve.value(i, 2 * n + h + 1))
                    pool.tensor_tensor(b.rstd[:, t], b.ve[:, t], neghalf[:, :], ALU.pow).then_inc(b.s_rstd.sem, 1)

            def add_bias(b, i, l, k):
                n = 1 + 2 * l + k
                w = (bo_all, b2_all)[k]
                if l == 0 and k == 0:
                    pool.wait_ge(s_rest, 16 * 4)
                pool.wait_ge(b.s_normed.sem, b.s_normed.value(i, 2 * n + 2))
                pool.tensor_tensor(b.x[:, :, :], b.x[:, :, :], w[:, l:l + 1, :].to_broadcast([P, TILES, D]), ALU.add)\
                    .then_inc(b.s_biased.sem, 1)

            with pool.Fori(0, STEPS) as i:
                rstd(A, i, 0)
                rstd(A, i, 1)
                add_bias(A, i, 0, 0)
                for n in range(2 * LAYERS + 2):
                    a, f = (A, B) if n % 2 == 0 else (B, A)
                    l, m = n // 2, (n - 1) // 2
                    if n == 0:
                        rstd(B, i, 0)
                    if 0 <= m < LAYERS or n == 0:
                        nf = 2 * m + 3 if n else 1
                        b = f
                        rstd(b, i, nf)
                        if nf <= 2 * LAYERS:
                            add_bias(b, i, (nf - 1) // 2, 0)
                        else:
                            rstd(b, i, nf + 1)
                    if l < LAYERS:
                        rstd(a, i, 2 * l + 2)
                        add_bias(a, i, l, 1)

        @block.vector
        def _(dve):
            dve.wait_ge(s_k, 16)
            dve.tensor_copy(ident16[:, :], ident)
            dve.tensor_copy(sel16[:, :], K[0:3 * EXPERTS, C_SEL:C_SEL + CH * P]).then_inc(s_c16, 1)
            dve.wait_ge(s_rows, 64)
            rq = rows[:, 0:LAYERS * QKV].rearrange("a (l n) -> a l n", n=QKV)[:, :, 0:2 * D]
            dve.tensor_scalar(rq, rq, 1.0, None, ALU.add).then_inc(s_plus, 1)
            dve.wait_ge(s_parps, 1)
            dve.tensor_copy(parT[:, :], A.ps[:, 0, 0:4 * LAYERS + BATCH]).then_inc(s_parT, 1)
            dve.wait_ge(s_parT, 1)
            for n in range(2 * LAYERS):
                l, k = n // 2, n % 2
                if n >= 2:
                    dve.wait_ge(s_foldps, n - 1)
                sc = parT[:, 2 * k * LAYERS + l:2 * k * LAYERS + l + 1]
                sh = parT[:, (2 * k + 1) * LAYERS + l:(2 * k + 1) * LAYERS + l + 1]
                dve.tensor_scalar(fold[:, k, 0:P - 1], base[:, 0:P - 1], sc, None, ALU.mult)
                dve.tensor_copy(fold[:, k, P - 1:P], sh).then_inc(s_fold, 1)

            steps = [0]

            def done(ins):
                ins.then_inc(s_modsb, 1)
                steps[0] += 1
                dve.wait_ge(s_modsb, steps[0])

            dve.wait_ge(s_modps, 1)
            done(dve.tensor_copy(mod[:, :], A.ps[0:BATCH, 0:2, :].rearrange("p k n -> p (k n)")[:, 0:6 * D]))
            dve.tensor_copy(shiftT[:, :], A.ps[:, 2, 0:BATCH])
            done(dve.tensor_scalar(scaleT[:, :], A.ps[:, 2, BATCH:2 * BATCH], 1.0, None, ALU.add))
            root = float(D) ** 0.5
            dve.tensor_scalar(modp[:, 0:D], mod[:, D:2 * D], 1.0, root, ALU.add, ALU.mult)
            done(dve.tensor_scalar(modp[:, D:2 * D], mod[:, 0:D], root, None, ALU.mult))
            for k, o in ((0, 2), (1, 5)):
                g = mod[:, o * D:(o + 1) * D]
                s = sgn[:, k * D:(k + 1) * D]
                done(dve.tensor_scalar(s, g, 0.0, 2.0, ALU.is_ge, ALU.mult))
                done(dve.tensor_scalar(s, s, -1.0, None, ALU.add))
                done(dve.tensor_tensor(g, g, s, ALU.mult))
                done(dve.scalar_tensor_tensor(s, g, 0.25, s, ALU.max, ALU.mult))
            dve.wait_ge(s_lnf, 32)
            dve.tensor_tensor(modp[:, 2 * D:3 * D], sgn[:, 0:D], lnf[:, 0:D], ALU.mult)
            dve.tensor_tensor(modp[:, 3 * D:4 * D], sgn[:, 0:D], lnf[:, D:2 * D], ALU.mult)
            done(dve.tensor_copy(modp[:, 4 * D:5 * D], sgn[:, D:2 * D]))

            dve.wait_ge(s_const, 6)

            def norm(b, i, n, src, dst, width, halves=range(2)):
                for h in halves:
                    ts = range(h * HALF, (h + 1) * HALF)
                    if n > 0:
                        dve.wait_ge(b.s_moved.sem, b.s_moved.value(i, 2 * n - 1 + h))
                    for t in ts:
                        dve.bn_stats(b.stat[:, t, :], src(t))
                    dve.drain()
                    for t in ts:
                        dve.bn_aggr(b.mv[:, t, :], b.stat[:, t, :]).then_inc(b.s_moments.sem, 1)

                def scaled():
                    for h in halves:
                        dve.wait_ge(b.s_rstd.sem, b.s_rstd.value(i, 2 * n + h + 1))
                        for t in range(h * HALF, (h + 1) * HALF):
                            last = dve.tensor_scalar(dst[:, t, 0:width], src(t)[:, 0:width], b.mv[:, t, 0:1],
                                                     b.rstd[:, t:t + 1], ALU.subtract, ALU.mult)
                        last.then_inc(b.s_normed.sem, 1)
                return scaled

            def norm_x(b, i, n, halves=range(2)):
                norm(b, i, n, lambda t: b.x[:, t, :], b.xn if n <= 2 * LAYERS else b.z,
                     D - 1 if n <= 2 * LAYERS else D, halves)()

            def enter(b, i):
                norm(b, i, 0, lambda t: X[:, x_cols(b, i, t)], b.z, D)()
                zs = [b.z[:, h * HALF:(h + 1) * HALF, :] for h in range(2)]
                for h in range(2):
                    dve.wait_ge(b.s_normed.sem, b.s_normed.value(i, h + 1))
                    dve.tensor_tensor(zs[h], zs[h], mod_row(b, i, h, 0), ALU.mult).then_inc(b.s_mod.sem, 1)
                for h in range(2):
                    dve.wait_ge(b.s_mod.sem, b.s_mod.value(i, h + 1))
                    dve.tensor_tensor(zs[h], zs[h], mod_row(b, i, h, 1), ALU.add).then_inc(b.s_mod.sem, 1)
                for h in range(2):
                    dve.wait_ge(b.s_mod.sem, b.s_mod.value(i, 2 + h + 1))
                    dve.tensor_tensor(b.x[:, h * HALF:(h + 1) * HALF, :], zs[h],
                                      pos.rearrange("p (t f) -> p t f", f=D), ALU.add).then_inc(b.s_moved.sem, 1)

            def positive(b, i, l):
                for h in range(2):
                    dve.wait_ge(b.s_v.sem, b.s_v.value(i, 2 * l + h + 1))
                    t = slice(h * HALF, (h + 1) * HALF)
                    keys = b.ps[:, 2 + h, :].rearrange("p (t n) -> p t n", n=2 * D)[:, :, 0:D]
                    dve.scalar_tensor_tensor(b.kp[:, t, :], b.ek[:, t, :], 1.0, keys, ALU.min, ALU.max)\
                        .then_inc(b.s_kp.sem, 1)
                dve.wait_ge(b.s_eq.sem, b.s_eq.value(i, l + 1))
                dve.scalar_tensor_tensor(b.qp[:, :], b.eq[:, :], 1.0, b.ps[:, 0, :], ALU.min, ALU.max)\
                    .then_inc(b.s_qp.sem, 1)

            def masked(b, i, l):
                for s in range(SEQS):
                    dve.wait_ge(b.s_sumps.sem, b.s_sumps.value(i, 2 * l + s + 1))
                    dve.tensor_tensor(b.kv[:, s, :], b.ps[:, 2 + s, 0:VW], headmask, ALU.mult).then_inc(b.s_kv.sem, 1)

            def divided(b, i, l):
                pairs = [b.ps[:, 1 - h, :].rearrange("p (t n) -> p t n", n=2 * D) for h in range(2)]
                for h in range(2):
                    t = slice(h * HALF, (h + 1) * HALF)
                    dve.wait_ge(b.s_attps.sem, b.s_attps.value(i, 2 * l + h + 1))
                    dve.tensor_scalar(b.den[:, t, :], pairs[h][:, :, D:VW], EPS_ATTN, None, ALU.add)\
                        .then_inc(b.s_den.sem, 1)
                    dve.wait_ge(b.s_den.sem, b.s_den.value(i, 2 * l + h + 1))
                    dve.reciprocal(b.rden[:, t, :], b.den[:, t, :]).then_inc(b.s_rden.sem, 1)
                    dve.wait_ge(b.s_rden.sem, b.s_rden.value(i, 2 * l + h + 1))
                    num = pairs[h][:, :, 0:D].rearrange("p t (h k) -> p t h k", k=DK)
                    dve.tensor_tensor(b.att[:, t, :].rearrange("p t (h k) -> p t h k", k=DK), num,
                                      b.rden[:, t, :].unsqueeze(3).to_broadcast([P, HALF, HEADS, DK]), ALU.mult)\
                        .then_inc(b.s_att.sem, 1)

            def move(b, i, l, k, h):
                ps, bank = ((b.s_wops, 1 - h), (b.s_w2ps, h))[k]
                dve.wait_ge(ps.sem, ps.value(i, 2 * l + h + 1))
                dve.wait_ge(b.s_biased.sem, b.s_biased.value(i, 2 * l + k + 1))
                xh = b.x[:, h * HALF:(h + 1) * HALF, :]
                dve.tensor_tensor(xh, b.ps[:, bank, 0:T].rearrange("p (t f) -> p t f", f=D), xh, ALU.add)\
                    .then_inc(b.s_moved.sem, 1)

            def leave(b, i):
                zs = [b.z[:, h * HALF:(h + 1) * HALF, :] for h in range(2)]
                for h in range(2):
                    dve.wait_ge(b.s_normed.sem, b.s_normed.value(i, 2 * (2 * LAYERS + 1) + h + 1))
                    dve.tensor_tensor(zs[h], zs[h], mod_row(b, i, h, 2), ALU.mult).then_inc(b.s_mod.sem, 1)
                for h in range(2):
                    dve.wait_ge(b.s_mod.sem, b.s_mod.value(i, 4 + h + 1))
                    dve.tensor_tensor(zs[h], zs[h], mod_row(b, i, h, 3), ALU.add).then_inc(b.s_mod.sem, 1)
                for h in range(2):
                    dve.wait_ge(b.s_mod.sem, b.s_mod.value(i, 6 + h + 1))
                    dve.tensor_tensor(b.y[:, h * HALF:(h + 1) * HALF, :], zs[h],
                                      X[:, x_cols(b, i, h * HALF, HALF)].rearrange("p (t f) -> p t f", f=D), ALU.add)\
                        .then_inc(b.s_moved.sem, 1)
                norm(b, i, 2 * LAYERS + 2, lambda t: b.y[:, t, :], b.z, D)()

            def tokensT(b, i):
                for h in range(2):
                    dve.wait_ge(b.s_tps.sem, b.s_tps.value(i, 4 * LAYERS + h + 1))
                    s = seq_of(b, i, h)
                    dve.tensor_scalar(b.xT[:, h * T:(h + 1) * T], b.ps[:, h, 0:T], scaleT[:, bass.ds(s, 1)],
                                      shiftT[:, bass.ds(s, 1)], ALU.mult, ALU.add).then_inc(b.s_xT.sem, 1)

            def route(b, i):
                n = [0]

                def step(ins):
                    n[0] += 1
                    ins.then_inc(b.s_route.sem, 1)
                    return n[0]

                def after(k):
                    dve.wait_ge(b.s_route.sem, b.s_route.value(i, k))

                dve.wait_ge(b.s_rps.sem, b.s_rps.value(i, 1))
                after(step(dve.tensor_copy(b.lg[:, :, :], b.ps[:, 2, 0:TILES * EXPERTS].rearrange(
                    "p (t e) -> p t e", e=EXPERTS))))
                after(step(dve.tensor_reduce(b.mx[:, :], b.lg[:, :, :], AXX, ALU.max)))
                step(dve.tensor_tensor(b.ls[:, :, :], b.lg[:, :, :],
                                       b.mx[:, :].unsqueeze(2).to_broadcast([P, TILES, EXPERTS]), ALU.subtract))
                four = [P, TILES, EXPERTS, EXPERTS]
                other = b.lg[:, :, :].unsqueeze(2).to_broadcast(four)
                mine = b.lg[:, :, :].unsqueeze(3).to_broadcast(four)
                step(dve.tensor_tensor(b.gt[:, :, :, :], other, mine, ALU.is_gt))
                after(step(dve.tensor_tensor(b.tie[:, :, :, :], other, mine, ALU.is_equal)))
                after(step(dve.tensor_tensor(b.tie[:, :, :, :], b.tie[:, :, :, :],
                                             tri.unsqueeze(1).to_broadcast(four), ALU.mult)))
                after(step(dve.tensor_tensor(b.gt[:, :, :, :], b.gt[:, :, :, :], b.tie[:, :, :, :], ALU.add)))
                after(step(dve.tensor_reduce(b.rank[:, :, :], b.gt[:, :, :, :], AXX, ALU.add)))
                dve.wait_ge(b.s_ex.sem, b.s_ex.value(i, 1))
                after(step(dve.tensor_reduce(b.sum[:, :], b.ex[:, :, :], AXX, ALU.add)))
                step(dve.reciprocal(b.rsum[:, :], b.sum[:, :]))
                after(step(dve.scalar_tensor_tensor(b.coef[:, :, :], b.rank[:, :, :], float(TOP), b.ex[:, :, :],
                                                    ALU.is_lt, ALU.mult)))
                after(step(dve.tensor_tensor(b.coef[:, :, :], b.coef[:, :, :],
                                             b.rsum[:, :].unsqueeze(2).to_broadcast([P, TILES, EXPERTS]), ALU.mult)))
                after(step(dve.tensor_copy(b.parts[:, :, 0, :], b.coef[:, :, :])))
                after(step(dve.tensor_tensor(b.rest[:, :, :], b.coef[:, :, :], b.parts[:, :, 0, :], ALU.subtract)))
                after(step(dve.tensor_copy(b.parts[:, :, 1, :], b.rest[:, :, :])))
                after(step(dve.tensor_tensor(b.rest2[:, :, :], b.rest[:, :, :], b.parts[:, :, 1, :], ALU.subtract)))
                step(dve.tensor_copy(b.parts[:, :, 2, :], b.rest2[:, :, :]))
                assert n[0] == b.s_route.per

            def hidden(b, i, some):
                for c in some:
                    dve.wait_ge(b.s_sig.sem, b.s_sig.value(i, c + 1))
                    dve.wait_ge(b.s_ups.sem, b.s_ups.value(i, c + 1))
                    if 2 <= c < CH:
                        dve.wait_ge(b.s_hid.sem, b.s_hid.value(i, c - 1))
                    dst = b.gu[c % 2] if c < CH else b.hs[:, :]
                    dve.tensor_tensor(dst, b.sig[c % 2], b.ps[:, bank_of(items.index(("up", c))), :], ALU.mult)\
                        .then_inc(b.s_gu.sem, 1)
                    if c < CH:
                        dve.wait_ge(b.s_gu.sem, b.s_gu.value(i, c + 1))
                        dve.wait_ge(b.s_cbps.sem, b.s_cbps.value(i, c + 1))
                        dve.tensor_tensor(b.h[:, c, :], b.gu[c % 2], b.ps[:, bank_of(items.index(("coef", c))), :],
                                          ALU.mult).then_inc(b.s_hid.sem, 1)

            def finish(b, i):
                for h in range(2):
                    dve.wait_ge(b.s_downps.sem, b.s_downps.value(i, h + 1))
                    t = slice(h * HALF, (h + 1) * HALF)
                    dve.tensor_tensor(b.z[:, t, :],
                                      b.ps[:, bank_of(items.index(("down", h))), 0:T].rearrange("p (t f) -> p t f", f=D),
                                      mod_row(b, i, h, 4), ALU.mult).then_inc(b.s_gated.sem, 1)
                for h in range(2):
                    t = slice(h * HALF, (h + 1) * HALF)
                    dve.wait_ge(b.s_gated.sem, b.s_gated.value(i, h + 1))
                    dve.tensor_tensor(X[:, x_cols(b, i, h * HALF, HALF)].rearrange("p (t f) -> p t f", f=D),
                                      b.z[:, t, :], b.y[:, t, :], ALU.add).then_inc(b.s_out.sem, 1)

            dve.wait_ge(s_rowsb, BATCH)
            dve.wait_ge(s_x, 16 * STEPS)
            with dve.Fori(0, STEPS) as i:
                enter(A, i)
                norm_x(A, i, 1)
                for n in range(2 * LAYERS + 2):
                    a, f = (A, B) if n % 2 == 0 else (B, A)
                    l, m = n // 2, (n - 1) // 2
                    attends, feeds = l < LAYERS, 0 <= m < LAYERS
                    if n == 0:
                        enter(B, i)
                        norm_x(B, i, 1)
                    if attends:
                        positive(a, i, l)
                        masked(a, i, l)
                        divided(a, i, l)
                    else:
                        tokensT(a, i)
                        route(a, i)
                        hidden(a, i, range(CH + 1))
                        finish(a, i)
                    if feeds:
                        for h in range(2):
                            move(f, i, m, 1, h)
                        norm_x(f, i, 2 * m + 3)
                        if m == LAYERS - 1:
                            leave(f, i)
                    if attends:
                        for h in range(2):
                            move(a, i, l, 0, h)
                        norm_x(a, i, 2 * l + 2)

        @block.tensor
        def _(pe):
            def mm(o, lhsT, rhs, start=True, stop=True):
                return pe.matmul(o, lhsT, rhs, start=start, stop=stop)

            pe.wait_ge(s_k, 16)
            pe.wait_ge(s_par, 16 * 5)
            n_par = 4 * LAYERS + BATCH
            pe.transpose(A.ps[:, 0, 0:n_par], par[:, :], ident[0:n_par, 0:n_par]).then_inc(s_parps, 1)
            pe.wait_ge(s_condT, 1)
            pe.wait_ge(s_wm, 16)
            mm(A.ps[0:BATCH, 0, :], condT[:, :], wm[:, 0:512])
            mm(A.ps[0:BATCH, 1, 0:6 * D - 512], condT[:, :], wm[:, 512:6 * D])
            mm(A.ps[:, 2, 0:BATCH], wm[:, 3 * D:4 * D], condT[:, :])
            mm(A.ps[:, 2, BATCH:2 * BATCH], wm[:, 4 * D:5 * D], condT[:, :]).then_inc(s_modps, 1)
            pe.wait_ge(s_wqkv, 48)
            pe.wait_ge(s_plus, 1)
            for n in range(2 * LAYERS):
                l, k = n // 2, n % 2
                if n == 1:
                    pe.wait_ge(s_w1, 16)
                w = wqkv[:, l, :] if k == 0 else w1[:, l, :]
                width = QKV if k == 0 else FF
                row = rows[:, l * QKV:(l + 1) * QKV] if k == 0 else \
                    rows[:, LAYERS * QKV + l * FF:LAYERS * QKV + (l + 1) * FF]
                pe.wait_ge(s_fold, n + 1)
                if n >= 2:
                    pe.wait_ge(s_folded, n - 1)
                mm(B.ps[:, k, 0:width], fold[:, k, :], w, stop=False)
                mm(B.ps[:, k, 0:width], last_row, row, start=False).then_inc(s_foldps, 1)
            pe.wait_ge(s_modsb, 12)
            for s in range(BATCH):
                if s >= 2:
                    pe.wait_ge(s_rowsb, s - 1)
                hot = K[0:BATCH, C_HOT + s * P:C_HOT + (s + 1) * P]
                bank = 2 * (s % 2)
                mm(A.ps[:, bank, :], hot, modp[:, 0:512])
                mm(A.ps[:, bank + 1, 0:MOD - 512], hot, modp[:, 512:MOD]).then_inc(s_rowps, 1)
            pe.wait_ge(s_folded, 2 * LAYERS)
            pe.wait_ge(s_rowsb, BATCH)
            pe.wait_ge(s_rest, 64)
            pe.wait_ge(s_wmoe, 16 * 7)
            pe.wait_ge(s_const, 6)
            pe.wait_ge(s_c16, 1)

            def transposes(b, i, n, src):
                first = 0 if n % 2 == 0 else 2
                norm = n + 1 if n < 2 * LAYERS else n + 2
                for h in range(2):
                    pe.wait_ge(b.s_normed.sem, b.s_normed.value(i, 2 * norm + h + 1))
                    for t in range(HALF):
                        last = pe.transpose(b.ps[:, first + h, t * P:(t + 1) * P], src[:, h * HALF + t, :], ident)
                    last.then_inc(b.s_tps.sem, 1)

            def project(b, i, l):
                for h in range(2):
                    pe.wait_ge(b.s_xT.sem, b.s_xT.value(i, 4 * l + h + 1))
                    for t in range(HALF):
                        last = mm(b.ps[:, 2 + h, t * 2 * D:(t + 1) * 2 * D],
                                  b.xT[:, (h * HALF + t) * P:(h * HALF + t + 1) * P], wqkv[:, l, D:QKV])
                    last.then_inc(b.s_kvps.sem, 1)
                mm(b.ps[:, 0, :], wqkv[:, l, 0:D], b.xT[:, :]).then_inc(b.s_qps.sem, 1)

            def sums(b, i, l):
                for s in range(SEQS):
                    pe.wait_ge(b.s_kp.sem, b.s_kp.value(i, 2 * l + s + 1))
                    for t in range(HALF):
                        last = mm(b.ps[:, 2 + s, 0:VW], b.kp[:, s * HALF + t, :], b.v[:, s * HALF + t, :],
                                  start=t == 0, stop=t == HALF - 1)
                    last.then_inc(b.s_sumps.sem, 1)

            def attend(b, i, l):
                pe.wait_ge(b.s_qp.sem, b.s_qp.value(i, l + 1))
                for s in range(SEQS):
                    pe.wait_ge(b.s_kv.sem, b.s_kv.value(i, 2 * l + s + 1))
                    for t in range(HALF):
                        last = mm(b.ps[:, 1 - s, t * 2 * D:t * 2 * D + VW],
                                  b.qp[:, (s * HALF + t) * P:(s * HALF + t + 1) * P], b.kv[:, s, :])
                    last.then_inc(b.s_attps.sem, 1)

            def att_transposes(b, i, l):
                for h in range(2):
                    pe.wait_ge(b.s_att.sem, b.s_att.value(i, 2 * l + h + 1))
                    for t in range(HALF):
                        last = pe.transpose(b.ps[:, 2 + h, t * P:(t + 1) * P], b.att[:, h * HALF + t, :], ident)
                    last.then_inc(b.s_atps.sem, 1)

            def out_project(b, i, l):
                for h in range(2):
                    pe.wait_ge(b.s_attT.sem, b.s_attT.value(i, 2 * l + h + 1))
                    for t in range(HALF):
                        last = mm(b.ps[:, 1 - h, t * P:(t + 1) * P],
                                  b.attT[:, (h * HALF + t) * P:(h * HALF + t + 1) * P], wo[:, l, :])
                    last.then_inc(b.s_wops.sem, 1)

            def expand(b, i, l, some):
                for c in some:
                    if c == 0:
                        pe.wait_ge(b.s_xT.sem, b.s_xT.value(i, 4 * l + 4))
                    mm(b.ps[:, c, :], w1[:, l, c * P:(c + 1) * P], b.xT[:, :]).then_inc(b.s_w1ps.sem, 1)

            def contract(b, i, l, h):
                for t in range(h * HALF, (h + 1) * HALF):
                    for c in range(CH):
                        if h == 0 and t == 0:
                            pe.wait_ge(b.s_h.sem, b.s_h.value(i, l * CH + CH))
                        last = mm(b.ps[:, h, (t - h * HALF) * P:(t - h * HALF + 1) * P],
                                  b.h[:, c, t * P:(t + 1) * P], w2[:, l, c, :], start=c == 0, stop=c == CH - 1)
                last.then_inc(b.s_w2ps.sem, 1)

            def logits(b, i):
                pe.wait_ge(b.s_xT.sem, b.s_xT.value(i, 4 * LAYERS + 2))
                for t in range(TILES):
                    last = mm(b.ps[:, 2, t * EXPERTS:(t + 1) * EXPERTS], b.xT[:, t * P:(t + 1) * P], wr[:, :])
                last.then_inc(b.s_rps.sem, 1)

            def coef_transposes(b, i):
                pe.wait_ge(b.s_route.sem, b.s_route.value(i, b.s_route.per))
                cps = b.ps[0:3 * EXPERTS, 3, 0:GT // 2].bitcast(BF16)
                for t in range(TILES):
                    last = pe.transpose(cps[:, t * P:(t + 1) * P],
                                        b.parts[:, t, :, :].rearrange("p k e -> p (k e)"), ident16[:, :])
                last.then_inc(b.s_cps.sem, 1)

            def free_bank(b, i, item):
                if item >= 4:
                    signal, n = left(b, item - 4)
                    pe.wait_ge(signal.sem, signal.value(i, n))

            def up_gate(b, i, c):
                for kind, w, signal in (("gate", wg, b.s_gps), ("up", wu, b.s_ups)):
                    item = items.index((kind, c))
                    free_bank(b, i, item)
                    mm(b.ps[:, bank_of(item), :], w[:, c, :], b.xT[:, :]).then_inc(signal.sem, 1)

            def coef_rows(b, i, c):
                item = items.index(("coef", c))
                if c == 0:
                    pe.wait_ge(b.s_coefT.sem, b.s_coefT.value(i, 1))
                free_bank(b, i, item)
                mm(b.ps[:, bank_of(item), :], sel16[:, c * P:(c + 1) * P], b.coefT[:, :]).then_inc(b.s_cbps.sem, 1)

            def down(b, i):
                pe.wait_ge(b.s_gu.sem, b.s_gu.value(i, CH + 1))
                for h in range(2):
                    item = items.index(("down", h))
                    free_bank(b, i, item)
                    for t in range(HALF):
                        tok = slice((h * HALF + t) * P, (h * HALF + t + 1) * P)
                        for c in range(CH + 1):
                            hid = b.h[:, c, tok] if c < CH else b.hs[:, tok]
                            last = mm(b.ps[:, bank_of(item), t * P:(t + 1) * P], hid, wd[:, c, :],
                                      start=c == 0, stop=c == CH)
                    last.then_inc(b.s_downps.sem, 1)

            with pe.Fori(0, STEPS) as i:
                for n in range(2 * LAYERS + 2):
                    a, f = (A, B) if n % 2 == 0 else (B, A)
                    l, m = n // 2, (n - 1) // 2
                    attends, feeds = l < LAYERS, 0 <= m < LAYERS
                    if attends:
                        transposes(a, i, 2 * l, a.xn)
                        if feeds:
                            transposes(f, i, 2 * m + 1, f.xn)
                        project(a, i, l)
                        if feeds:
                            expand(f, i, m, (0, 1))
                        sums(a, i, l)
                        if feeds:
                            expand(f, i, m, (2, 3))
                        attend(a, i, l)
                        if feeds:
                            contract(f, i, m, 0)
                        att_transposes(a, i, l)
                        if feeds:
                            contract(f, i, m, 1)
                        out_project(a, i, l)
                    else:
                        transposes(a, i, 2 * LAYERS, a.z)
                        if feeds:
                            transposes(f, i, 2 * m + 1, f.xn)
                        logits(a, i)
                        up_gate(a, i, 0)
                        if feeds:
                            expand(f, i, m, range(CH))
                            for h in range(2):
                                contract(f, i, m, h)
                        coef_transposes(a, i)
                        for c in range(CH):
                            coef_rows(a, i, c)
                            up_gate(a, i, c + 1)
                        down(a, i)


_INS = ["attn_x_in", "attn_Wq", "attn_bq", "attn_Wk", "attn_bk", "attn_Wv", "attn_bv", "attn_Wo", "attn_bo",
        "attn_W1", "attn_b1", "attn_W2", "attn_b2", "attn_ln1_s", "attn_ln1_b", "attn_ln2_s", "attn_ln2_b",
        "attn_lnf_s", "attn_lnf_b", "ffn_router", "ffn_experts_gate", "ffn_experts_up", "ffn_experts_down",
        "ffn_shared_gate", "ffn_shared_up", "ffn_shared_down", "c", "wmod"]


def build(nc, inputs):
    arrays, args = {}, []
    for name in _INS:
        arrays["in_" + name] = np.ascontiguousarray(inputs["L0_" + name])
    arrays["in_consts"] = constants()
    for name, a in arrays.items():
        args.append(nc.dram_tensor(name, a.shape, mybir.dt.from_np(a.dtype), kind="ExternalInput").ap())
    args.append(nc.dram_tensor("out", (BATCH, T, D), F32, kind="ExternalOutput").ap())
    program(nc, *args)
    return arrays


def kernel(**inputs):
    from concourse.bacc import Bacc
    from concourse.bass_utils import run_bass_kernel_spmd

    nc = Bacc("TRN2", target_bir_lowering=False, num_devices=1)
    arrays = build(nc, inputs)
    return run_bass_kernel_spmd(nc, [arrays], core_ids=[0]).results[0]["out"]
```

```python
from contextlib import ExitStack

import numpy as np

import concourse.bass as bass
from concourse import mybir
from concourse.alu_op_type import AluOpType as ALU

F32 = mybir.dt.float32
BF16 = mybir.dt.bfloat16
ACT = mybir.ActivationFunctionType
AXX = mybir.AxisListType.X

BATCH, T, D = 16, 256, 128
LAYERS, HEADS, FF = 4, 16, 512
DK = D // HEADS
EXPERTS, DE, TOP = 8, 64, 2
P = 128
CHAINS = 4
TILES = T // P
STEPS = BATCH // CHAINS
CH = FF // P
PAIRS = CH // 2
VW = D + HEADS
QKV = 3 * D
MOD = 5 * D
EPS = 1e-5
EPS_ATTN = 1e-6
NORMS = 2 * LAYERS + 3
LAST = 2 * LAYERS + 1
EXPERT_PS = ("logits", "gate0", "up0", "coefT", "spread0", "gate1", "up1", "spread1", "gate2", "up2", "down")
EXPERT_ACT = ("exp", "silu0", "coefT", "silu1", "silu2")
EXPERT_UNITS = ("product0", "weighed0", "product1", "weighed1", "product2")
ROUTE_STEPS = 17
PHASES = 2 * LAYERS + 2

C_ID = 0
C_MASK = C_ID + P
C_TRI = C_MASK + VW
C_POS = C_TRI + EXPERTS * EXPERTS
C_BASE = C_POS + T // P * D
C_ALL = C_BASE + P
S_SEL = 0
S_HOT = S_SEL + CH * P
S_ALL = S_HOT + BATCH * P
S_ROWS = 3 * EXPERTS


def constants():
    k = np.zeros((P, C_ALL), np.float32)
    p = np.arange(P)
    k[:, C_ID:C_ID + P] = np.eye(P)
    k[:, C_MASK:C_MASK + D] = p[:, None] // DK == p[None, :] // DK
    k[:, C_MASK + D:C_MASK + VW] = p[:, None] // DK == np.arange(HEADS)[None, :]
    e = np.arange(EXPERTS)
    k[:, C_TRI:C_TRI + EXPERTS ** 2] = (e[None, :] < e[:, None]).reshape(1, -1)
    half = D // 2
    freq = np.exp(np.arange(half, dtype=np.float32) * np.float32(-np.log(10000.0) / (half - 1)))
    pos = (np.arange(T, dtype=np.float32) + np.float32(1))[:, None] * freq[None, :]
    pos = np.concatenate([np.sin(pos), np.cos(pos)], axis=-1)
    k[:, C_POS:C_POS + T // P * D] = pos.reshape(T // P, P, D).transpose(1, 0, 2).reshape(P, -1)
    base = np.eye(P)
    base[P - 1, :] = -1
    k[:, C_BASE:C_BASE + P] = base
    return k


def selectors():
    k = np.zeros((S_ROWS, S_ALL), np.float32)
    for c in range(CH):
        for m in range(P):
            k[2 * c + m // DE + EXPERTS * np.arange(3), S_SEL + c * P + m] = 1
    for s in range(BATCH):
        k[s, S_HOT + s * P:S_HOT + (s + 1) * P] = 1
    return k


class Signal:

    def __init__(self, sem, per):
        self.sem, self.per = sem, per

    def value(self, i, n):
        return i * self.per + n

    def of(self, names, name, i):
        return self.value(i, names.index(name) + 1)


def program(nc, x_in, Wq, bq, Wk, bk, Wv, bv, Wo, bo, W1, b1, W2, b2, ln1_s, ln1_b, ln2_s, ln2_b, lnf_s, lnf_b,
            router, e_gate, e_up, e_down, s_gate, s_up, s_down, cond, wmod, consts, select, out):
    nc.disable_value_cache = True
    ctx = ExitStack()
    with ctx:
        def sb(name, shape, dt=F32):
            return ctx.enter_context(nc.sbuf_tensor(name, shape, dt))

        def sem(name):
            return ctx.enter_context(nc.semaphore(name))

        def flat(ap):
            return ap.rearrange("p a b -> p (a b)")

        K = sb("K", [P, C_ALL])
        ident, base = K[:, C_ID:C_ID + P], K[:, C_BASE:C_BASE + P]
        headmask = K[:, C_MASK:C_MASK + VW]
        tri = K[:, C_TRI:C_TRI + EXPERTS ** 2].rearrange("p (j k) -> p j k", k=EXPERTS)
        pos = K[:, C_POS:C_POS + TILES * D].rearrange("p (t f) -> p t f", f=D)
        ident16 = sb("ident16", [P, P], BF16)
        sel16 = sb("sel16", [S_ROWS, CH * P], BF16)
        hot16 = sb("hot16", [96, BATCH * P], BF16)
        mod16 = sb("mod16", [96, MOD], BF16)
        X = sb("X", [P, BATCH * TILES * D])
        par = sb("par", [4 * LAYERS + BATCH, D])
        parT = sb("parT", [P, 4 * LAYERS + BATCH])
        condT = sb("condT", [P, BATCH])
        wqkv = sb("wqkv", [P, LAYERS, QKV])
        w1 = sb("w1", [P, LAYERS, FF])
        w2 = sb("w2", [P, LAYERS, CH, D])
        wo = sb("wo", [P, LAYERS, D])
        bo_all = sb("bo_all", [P, LAYERS, D])
        b2_all = sb("b2_all", [P, LAYERS, D])
        fold = sb("fold", [P, 2 * LAYERS, P])
        wm = sb("wm", [P, 6 * D])
        lnf = sb("lnf", [BATCH, 2 * D])
        mod = sb("mod", [BATCH, 6 * D])
        modp = sb("modp", [BATCH, MOD])
        modr = sb("modr", [BATCH, MOD])
        mid16 = sb("mid16", [BATCH, MOD], BF16)
        sgn = sb("sgn", [BATCH, 2 * D])
        M = sb("M", [P, BATCH, MOD])
        H = sb("H", [P, CHAINS * CH * T])
        S = flat(M[:, :, :])[0:S_ROWS, BATCH * MOD - S_ALL:]
        bias = H[:, 0:LAYERS * (QKV + FF)].rearrange("p (l n) -> p l n", n=QKV + FF)
        shiftT = sb("shiftT", [P, BATCH])
        scaleT = sb("scaleT", [P, BATCH])
        wr = sb("wr", [P, EXPERTS])
        wg = sb("wg", [P, CH + 1, P])
        wu = sb("wu", [P, CH + 1, P])
        wd = sb("wd", [P, CH + 1, D])
        neghalf = sb("neghalf", [P, TILES])
        epsilon = sb("epsilon", [P, TILES])

        class Chain:
            pass

        chains = []
        for c in range(CHAINS):
            b = Chain()
            b.c = c
            n = "ABCD"[c]
            b.x = sb("x" + n, [P, TILES, D])
            b.stat = sb("stat" + n, [P, TILES, 6])
            b.mv = sb("mv" + n, [P, TILES, 2])
            b.ve = sb("ve" + n, [P, TILES])
            b.rstd = sb("rstd" + n, [P, TILES])
            b.xn = sb("xn" + n, [P, TILES, D])
            b.gu = sb("gu" + n, [P, 2, T])
            b.z = b.gu[:, 0, :].rearrange("p (t f) -> p t f", f=D)
            b.attT = b.gu[:, 1, :]
            b.xT = sb("xT" + n, [P, T])
            b.eqk = sb("eqk" + n, [P, 2, T])
            b.eq, b.ek = b.eqk[:, 0, :], b.eqk[:, 1, :].rearrange("p (t f) -> p t f", f=D)
            b.qp = sb("qp" + n, [P, T])
            b.kp = sb("kp" + n, [P, TILES, D])
            b.v = sb("v" + n, [P, TILES, VW])
            b.kv = sb("kv" + n, [P, VW])
            b.den = sb("den" + n, [P, TILES, HEADS])
            b.rden = sb("rden" + n, [P, TILES, HEADS])
            b.att = sb("att" + n, [P, TILES, D])
            b.y = b.att
            b.h = H[:, c * CH * T:(c + 1) * CH * T].rearrange("p (c t) -> p c t", t=T)
            b.hs = b.qp
            b.lg = sb("lg" + n, [P, TILES, EXPERTS])
            b.mx = sb("mx" + n, [P, TILES])
            b.ls = sb("ls" + n, [P, TILES, EXPERTS])
            b.ex = sb("ex" + n, [P, TILES, EXPERTS])
            b.gt = sb("gt" + n, [P, TILES, EXPERTS, EXPERTS])
            b.tie = sb("tie" + n, [P, TILES, EXPERTS, EXPERTS])
            b.rank = sb("rank" + n, [P, TILES, EXPERTS])
            b.sum = sb("sum" + n, [P, TILES])
            b.rsum = sb("rsum" + n, [P, TILES])
            b.coef = sb("coef" + n, [P, TILES, EXPERTS])
            b.rest = sb("rest" + n, [P, TILES, EXPERTS])
            b.rest2 = sb("rest2" + n, [P, TILES, EXPERTS])
            b.parts = sb("parts" + n, [P, TILES, 3, EXPERTS], BF16)
            b.coefT = sb("coefT" + n, [S_ROWS, T], BF16)
            b.ps = ctx.enter_context(nc.psum_tensor("ps" + n, [P, 2, 512], F32))

            def sig(name, per, n=n):
                return Signal(sem(name + n), per)

            b.s_moved = sig("moved", 2 * LAYERS + 2)
            b.s_moments = sig("moments", NORMS)
            b.s_rstd = sig("rstd", 2 * NORMS)
            b.s_normed = sig("normed", NORMS)
            b.s_biased = sig("biased", 2 * LAYERS)
            b.s_tps = sig("tps", 2 * LAYERS + 1)
            b.s_xT = sig("xT", 2 * LAYERS + 1)
            b.s_kvps = sig("kvps", LAYERS)
            b.s_qps = sig("qps", LAYERS)
            b.s_v = sig("v", LAYERS)
            b.s_kp = sig("kp", LAYERS)
            b.s_eq = sig("eq", LAYERS)
            b.s_qp = sig("qp", LAYERS)
            b.s_sumps = sig("sumps", LAYERS)
            b.s_kv = sig("kv", LAYERS)
            b.s_attps = sig("attps", LAYERS)
            b.s_att = sig("att", 3 * LAYERS)
            b.s_atps = sig("atps", LAYERS)
            b.s_attT = sig("attT", LAYERS)
            b.s_wops = sig("wops", LAYERS)
            b.s_w1ps = sig("w1ps", PAIRS * LAYERS)
            b.s_h = sig("h", PAIRS * LAYERS)
            b.s_w2ps = sig("w2ps", LAYERS)
            b.s_mod = sig("mod", 5)
            b.s_route = sig("route", ROUTE_STEPS)
            b.s_eps = sig("eps", len(EXPERT_PS))
            b.s_eact = sig("eact", len(EXPERT_ACT))
            b.s_units = sig("units", len(EXPERT_UNITS))
            b.s_out = sig("out", 1)
            chains.append(b)
        AB, CD = chains[:2], chains[2:]
        A, B = AB

        s_k, s_sel, s_par, s_bias, s_lnf, s_wm = sem("k"), sem("sel"), sem("par"), sem("biasin"), sem("lnf"), sem("wm")
        s_wqkv, s_w1, s_rest, s_wmoe = sem("wqkv"), sem("w1in"), sem("wrest"), sem("wmoe")
        s_x = sem("xin")
        s_stored = sem("stored")
        s_const = sem("const")
        s_zero = sem("zero")
        s_c16 = sem("c16")
        s_plus = sem("plus")
        s_parps = sem("parps")
        s_parT = sem("parT")
        s_condT = sem("condT")
        s_modps = sem("modps")
        s_modsb = sem("modsb")
        s_rowps = sem("rowps")
        s_rowsb = sem("rowsb")
        s_fold = sem("fold")
        s_foldps = sem("foldps")
        s_folded = sem("folded")

        block = ctx.enter_context(nc.Block())

        def seq_of(b, i):
            return (i % STEPS) * CHAINS + b.c

        def x_tile(b, i, t):
            return X[:, bass.ds(seq_of(b, i) * TILES * D + t * D, D)]

        def x_tiles(b, i):
            return X[:, bass.ds(seq_of(b, i) * TILES * D, TILES * D)].rearrange("p (t f) -> p t f", f=D)

        def mod_row(b, i, k):
            r = M[:, bass.ds(seq_of(b, i), 1), k * D:(k + 1) * D]
            return r.to_broadcast([P, TILES, D])

        def phase(n):
            first, second = (AB, CD) if n % 2 == 0 else (CD, AB)
            return first, n // 2, second, (n - 1) // 2

        @block.sync
        def _(sync):
            for n, a in enumerate((ln1_s, ln1_b, ln2_s, ln2_b)):
                sync.dma_start(par[n * LAYERS:(n + 1) * LAYERS, :], a).then_inc(s_par, 16)
            sync.dma_start(par[4 * LAYERS:, :], cond).then_inc(s_par, 16)
            sync.dma_start(K[:, :], consts).then_inc(s_k, 16)
            sync.dma_start(wm[:, :], wmod).then_inc(s_wm, 16)
            for n, a in enumerate((lnf_s, lnf_b)):
                sync.dma_start(lnf[:, n * D:(n + 1) * D],
                               a.rearrange("(a n) -> a n", a=1).to_broadcast([BATCH, D])).then_inc(s_lnf, 16)
            sync.dma_start(S, select).then_inc(s_sel, 16)
            tiles_in = x_in.rearrange("b (t p) f -> p (b t) f", p=P)
            Xv = X[:, :].rearrange("p (n f) -> p n f", f=D)
            k = CHAINS * TILES
            for n in range(STEPS):
                sync.dma_start(Xv[:, n * k:(n + 1) * k, :], tiles_in[:, n * k:(n + 1) * k, :]).then_inc(s_x, 16)
            sync.wait_ge(s_zero, 1)
            for n, a in enumerate((bq, bk, bv)):
                sync.dma_start(bias[P - 1:P, :, n * D:(n + 1) * D],
                               a.rearrange("(a l) n -> a l n", a=1)).then_inc(s_bias, 16)
            sync.dma_start(bias[P - 1:P, :, QKV:], b1.rearrange("(a l) n -> a l n", a=1)).then_inc(s_bias, 16)
            out_tiles = out.rearrange("b (t p) f -> b p t f", p=P)
            with sync.Fori(0, STEPS) as i:
                for b in chains:
                    sync.wait_ge(b.s_out.sem, b.s_out.value(i, 1))
                    sync.dma_start(out_tiles[bass.ds(seq_of(b, i), 1), :, :, :].rearrange("a p t f -> p (a t) f"),
                                   x_tiles(b, i)).then_inc(s_stored, 16)
            sync.wait_ge(s_stored, 16 * STEPS * CHAINS)

        @block.scalar
        def _(act):
            for n, a in enumerate((Wq, Wk, Wv)):
                act.dma_start(wqkv[:, :, n * D:(n + 1) * D], a.rearrange("l k n -> k l n")).then_inc(s_wqkv, 16)
            act.dma_start(w1[:, :, :], W1.rearrange("l k n -> k l n")).then_inc(s_w1, 16)

            act.wait_ge(s_parT, 1)
            act.activation(condT[:, :], parT[:, 4 * LAYERS:], ACT.Silu).then_inc(s_condT, 1)
            for s in range(BATCH):
                act.wait_ge(s_rowps, s + 1)
                act.activation(M[:, s, :], chains[s % 2].ps[:, :, :].rearrange("p k n -> p (k n)")[:, 0:MOD],
                               ACT.Copy).then_inc(s_rowsb, 1)

            def transposed(b, i, n):
                act.wait_ge(b.s_tps.sem, b.s_tps.value(i, n + 1))
                act.activation(b.xT[:, :], b.ps[:, n % 2, 0:T], ACT.Copy).then_inc(b.s_xT.sem, 1)

            def key_exps(b, i, l):
                act.wait_ge(b.s_kvps.sem, b.s_kvps.value(i, l + 1))
                both = b.ps[:, 1, :].rearrange("p (t n) -> p t n", n=2 * D)
                act.activation(b.ek, both[:, :, 0:D], ACT.Exp, bias=-1.0)
                act.activation(b.v[:, :, 0:D], both[:, :, D:], ACT.Copy).then_inc(b.s_v.sem, 1)

            def query_exps(b, i, l):
                act.wait_ge(b.s_qps.sem, b.s_qps.value(i, l + 1))
                act.activation(b.eq, b.ps[:, 0, 0:T], ACT.Exp, bias=-1.0).then_inc(b.s_eq.sem, 1)

            def att_transposed(b, i, l):
                act.wait_ge(b.s_atps.sem, b.s_atps.value(i, l + 1))
                act.activation(b.attT, b.ps[:, 1, 0:T], ACT.Copy).then_inc(b.s_attT.sem, 1)

            def relu(b, i, l, k):
                act.wait_ge(b.s_w1ps.sem, b.s_w1ps.value(i, l * PAIRS + k + 1))
                act.activation(b.h[:, 2 * k:2 * k + 2, :], b.ps[:, k, :].rearrange("p (c t) -> p c t", t=T),
                               ACT.Relu).then_inc(b.s_h.sem, 1)

            def router_exp(b, i):
                act.wait_ge(b.s_route.sem, b.s_route.value(i, 3))
                act.activation(b.ex[:, :, :], b.ls[:, :, :], ACT.Exp).then_inc(b.s_eact.sem, 1)

            def coefs(b, i):
                act.wait_ge(b.s_eps.sem, b.s_eps.of(EXPERT_PS, "coefT", i))
                act.activation(b.coefT[:, :], b.ps[0:S_ROWS, 1, 0:T // 2].bitcast(BF16), ACT.Copy)\
                    .then_inc(b.s_eact.sem, 1)

            def silu(b, i, k):
                act.wait_ge(b.s_eps.sem, b.s_eps.of(EXPERT_PS, f"gate{k}", i))
                if k > 0:
                    act.wait_ge(b.s_units.sem, b.s_units.of(EXPERT_UNITS, f"product{k - 1}", i))
                width = 2 * T if k < PAIRS else T
                act.activation(b.eqk[:, :, :].rearrange("p a t -> p (a t)")[:, 0:width], b.ps[:, k % 2, 0:width],
                               ACT.Silu).then_inc(b.s_eact.sem, 1)

            a, _, f, _ = phase(0)
            transposed(a[0], 0, 0)
            key_exps(a[0], 0, 0)
            query_exps(a[0], 0, 0)
            transposed(a[1], 0, 0)
            key_exps(a[1], 0, 0)
            query_exps(a[1], 0, 0)
            att_transposed(a[0], 0, 0)
            att_transposed(a[1], 0, 0)
            with act.Fori(0, STEPS) as i:
                for n in range(1, PHASES):
                    a, l, f, m = phase(n)
                    if n == 1:
                        transposed(f[0], i, 1)
                        relu(f[0], i, 0, 0)
                        relu(f[0], i, 0, 1)
                        transposed(f[1], i, 1)
                        transposed(a[0], i, 0)
                        key_exps(a[0], i, 0)
                        query_exps(a[0], i, 0)
                        transposed(a[1], i, 0)
                        relu(f[1], i, 0, 0)
                        key_exps(a[1], i, 0)
                        query_exps(a[1], i, 0)
                        att_transposed(a[0], i, l)
                        relu(f[1], i, m, 1)
                        att_transposed(a[1], i, l)
                    elif n < PHASES - 3:
                        transposed(a[0], i, 2 * l)
                        transposed(f[0], i, 2 * m + 1)
                        key_exps(a[0], i, l)
                        transposed(a[1], i, 2 * l)
                        query_exps(a[0], i, l)
                        transposed(f[1], i, 2 * m + 1)
                        key_exps(a[1], i, l)
                        query_exps(a[1], i, l)
                        relu(f[0], i, m, 0)
                        relu(f[0], i, m, 1)
                        relu(f[1], i, m, 0)
                        att_transposed(a[0], i, l)
                        relu(f[1], i, m, 1)
                        att_transposed(a[1], i, l)
                    elif l < LAYERS:
                        transposed(a[0], i, 2 * l)
                        transposed(f[0], i, 2 * m + 1)
                        key_exps(a[0], i, l)
                        transposed(a[1], i, 2 * l)
                        query_exps(a[0], i, l)
                        relu(f[0], i, m, 0)
                        relu(f[0], i, m, 1)
                        key_exps(a[1], i, l)
                        query_exps(a[1], i, l)
                        att_transposed(a[0], i, l)
                    elif m < LAYERS:
                        transposed(a[1], i, 2 * l - 1)
                        relu(a[1], i, l - 1, 0)
                        relu(a[1], i, l - 1, 1)
                        att_transposed(f[1], i, m)
                        transposed(f[0], i, 2 * m + 1)
                        router_exp(a[0], i)
                    else:
                        silu(f[0], i, 0)
                        router_exp(f[1], i)
                        relu(a[0], i, l - 1, 0)
                        transposed(a[1], i, 2 * l - 1)
                        silu(f[1], i, 0)
                        coefs(f[0], i)
                        coefs(f[1], i)
                        relu(a[1], i, l - 1, 0)
                        silu(f[1], i, 1)
                        silu(f[0], i, 1)
                        relu(a[0], i, l - 1, 1)
                        relu(a[1], i, l - 1, 1)
                        silu(f[0], i, 2)
                        silu(f[1], i, 2)
                        transposed(f[1], i + 1, 0)
                        router_exp(a[1], i)
                        transposed(f[0], i + 1, 0)
                        router_exp(a[0], i)
                        silu(a[0], i, 0)
                        silu(a[1], i, 0)
                        key_exps(f[0], i + 1, 0)
                        query_exps(f[0], i + 1, 0)
                        key_exps(f[1], i + 1, 0)
                        coefs(a[0], i)
                        coefs(a[1], i)
                        query_exps(f[1], i + 1, 0)
                        silu(a[1], i, 1)
                        silu(a[0], i, 1)
                        att_transposed(f[0], i + 1, 0)
                        att_transposed(f[1], i + 1, 0)
                        silu(a[0], i, 2)
                        silu(a[1], i, 2)

        @block.gpsimd
        def _(pool):
            pool.memset(bias[:, :, :], 0.0).then_inc(s_zero, 1)
            pool.memset(mod16[:, :], 0.0).then_inc(s_zero, 1)
            pool.memset(hot16[:, :], 0.0).then_inc(s_zero, 1)
            pool.memset(neghalf[:, :], -0.5).then_inc(s_const, 1)
            pool.memset(epsilon[:, :], EPS).then_inc(s_const, 1)
            for b in chains:
                pool.memset(b.xn[:, :, D - 1:D], 1.0).then_inc(s_const, 1)
                pool.memset(b.v[:, :, D:], 1.0).then_inc(s_const, 1)
            pool.dma_start(wo[:, :, :], Wo.rearrange("l k n -> k l n")).then_inc(s_rest, 16)
            pool.dma_start(w2[:, :, :, :].rearrange("p l c n -> p (l c) n"),
                           W2.rearrange("l (c p) n -> p (l c) n", p=P)).then_inc(s_rest, 16)
            for w, a in ((bo_all, bo), (b2_all, b2)):
                pool.dma_start(w[:, :, :].rearrange("p l n -> p (l n)"),
                               a.rearrange("(a l) n -> a (l n)", a=1).to_broadcast([P, LAYERS * D])).then_inc(s_rest, 16)
            pool.dma_start(wr[:, :], router).then_inc(s_wmoe, 16)
            for w, e, s in ((wg, e_gate, s_gate), (wu, e_up, s_up)):
                pool.dma_start(w[:, 0:CH, :].rearrange("p c (e d) -> p (c e) d", d=DE),
                               e.rearrange("e h d -> h e d")).then_inc(s_wmoe, 16)
                pool.dma_start(w[:, CH, :], s).then_inc(s_wmoe, 16)
            pool.dma_start(wd[:, 0:CH, :], e_down.rearrange("(c e) d n -> (e d) c n", e=2)).then_inc(s_wmoe, 16)
            pool.dma_start(wd[:, CH, :], s_down).then_inc(s_wmoe, 16)
            pool.wait_ge(s_const, 10)

            def rstd(b, i, n):
                pool.wait_ge(b.s_moments.sem, b.s_moments.value(i, n + 1))
                pool.tensor_tensor(b.ve[:, :], b.mv[:, :, 1], epsilon[:, :], ALU.add).then_inc(b.s_rstd.sem, 1)
                pool.wait_ge(b.s_rstd.sem, b.s_rstd.value(i, 2 * n + 1))
                pool.tensor_tensor(b.rstd[:, :], b.ve[:, :], neghalf[:, :], ALU.pow).then_inc(b.s_rstd.sem, 1)

            def add_bias(b, i, n):
                l, k = (n - 1) // 2, (n - 1) % 2
                w = (bo_all, b2_all)[k]
                pool.wait_ge(b.s_normed.sem, b.s_normed.value(i, n + 1))
                pool.tensor_tensor(b.x[:, :, :], b.x[:, :, :], w[:, l:l + 1, :].to_broadcast([P, TILES, D]), ALU.add)\
                    .then_inc(b.s_biased.sem, 1)

            a, _, f, _ = phase(0)
            rstd(a[0], 0, 0)
            rstd(a[1], 0, 0)
            rstd(a[0], 0, 1)
            rstd(f[1], 0, 0)
            pool.wait_ge(s_rest, 64)
            rstd(f[0], 0, 0)
            rstd(a[1], 0, 1)
            add_bias(a[1], 0, 1)
            add_bias(a[0], 0, 1)
            rstd(a[0], 0, 2)
            rstd(f[0], 0, 1)
            rstd(a[1], 0, 2)
            rstd(f[1], 0, 1)
            with pool.Fori(0, STEPS) as i:
                for n in range(1, PHASES):
                    a, l, f, m = phase(n)
                    if n == 1:
                        add_bias(a[1], i, 1)
                        add_bias(f[0], i, 2)
                        rstd(f[0], i, 3)
                        add_bias(a[0], i, 1)
                        add_bias(f[1], i, 2)
                        rstd(a[0], i, 2)
                        rstd(f[1], i, 3)
                        add_bias(f[0], i, 2 * m + 3)
                        rstd(a[1], i, 2)
                        add_bias(a[0], i, 2)
                        add_bias(a[1], i, 2 * l + 2)
                        rstd(a[0], i, 2 * l + 3)
                        add_bias(f[1], i, 2 * m + 3)
                        rstd(f[0], i, 2 * m + 4)
                    elif n < PHASES - 3:
                        add_bias(f[0], i, 2 * m + 3)
                        rstd(f[1], i, 2 * m + 3)
                        rstd(a[1], i, 2 * l + 2)
                        add_bias(a[0], i, 2 * l + 2)
                        rstd(a[0], i, 2 * l + 3)
                        add_bias(a[1], i, 2 * l + 2)
                        rstd(f[0], i, 2 * m + 4)
                        add_bias(f[1], i, 2 * m + 3)
                    elif l < LAYERS:
                        rstd(f[0], i, LAST + 1)
                        add_bias(a[0], i, 2 * l + 2)
                        rstd(f[1], i, 2 * m + 3)
                        rstd(a[1], i, 2 * l + 2)
                        rstd(f[1], i, LAST + 1)
                        add_bias(a[1], i, 2 * l + 2)
                        rstd(a[0], i, LAST)
                        rstd(a[1], i, LAST)
                        rstd(f[0], i + 1, 0)
                        rstd(a[0], i, LAST + 1)
                    elif m < LAYERS:
                        rstd(a[1], i + 1, 0)
                        rstd(f[1], i, LAST + 1)
                        rstd(a[0], i + 1, 1)
                        rstd(a[1], i + 1, 1)
                        add_bias(a[1], i + 1, 1)
                    else:
                        add_bias(f[0], i + 1, 1)
                        rstd(f[1], i + 1, 2)
                        rstd(f[0], i + 1, 2)
                        rstd(a[0], i + 1, 0)
                        rstd(a[1], i + 1, 0)
                        rstd(a[0], i + 1, 1)
                        rstd(a[1], i + 1, 1)

        @block.vector
        def _(dve):
            dve.wait_ge(s_parps, 1)
            dve.tensor_copy(parT[:, :], A.ps[:, 0, 0:4 * LAYERS + BATCH]).then_inc(s_parT, 1)
            dve.tensor_copy(ident16[:, :], ident)
            dve.wait_ge(s_parT, 1)
            for n in range(2 * LAYERS):
                l, k = n // 2, n % 2
                sc = parT[:, 2 * k * LAYERS + l:2 * k * LAYERS + l + 1]
                sh = parT[:, (2 * k + 1) * LAYERS + l:(2 * k + 1) * LAYERS + l + 1]
                dve.tensor_scalar(fold[:, n, 0:P - 1], base[:, 0:P - 1], sc, None, ALU.mult)
                dve.tensor_copy(fold[:, n, P - 1:P], sh).then_inc(s_fold, 1)

            steps = [0]

            def done(ins):
                ins.then_inc(s_modsb, 1)
                steps[0] += 1
                dve.wait_ge(s_modsb, steps[0])

            dve.wait_ge(s_modps, 1)
            done(dve.tensor_copy(mod[:, :], A.ps[0:BATCH, :, :].rearrange("p k n -> p (k n)")[:, 0:6 * D]))
            dve.tensor_copy(shiftT[:, :], B.ps[:, 0, 0:BATCH])
            done(dve.tensor_scalar(scaleT[:, :], B.ps[:, 0, BATCH:2 * BATCH], 1.0, None, ALU.add))
            root = float(D) ** 0.5
            dve.tensor_scalar(modp[:, 0:D], mod[:, D:2 * D], 1.0, root, ALU.add, ALU.mult)
            done(dve.tensor_scalar(modp[:, D:2 * D], mod[:, 0:D], root, None, ALU.mult))
            g = mod[:, :].rearrange("b (k n) -> b k n", n=3 * D)[:, :, 2 * D:]
            s = sgn[:, :].rearrange("b (k n) -> b k n", n=D)
            done(dve.tensor_scalar(s, g, 0.0, 2.0, ALU.is_ge, ALU.mult))
            done(dve.tensor_scalar(s, s, -1.0, None, ALU.add))
            done(dve.tensor_tensor(g, g, s, ALU.mult))
            done(dve.scalar_tensor_tensor(s, g, 0.25, s, ALU.max, ALU.mult))
            dve.wait_ge(s_lnf, 32)
            dve.tensor_tensor(modp[:, 2 * D:3 * D], sgn[:, 0:D], lnf[:, 0:D], ALU.mult)
            dve.tensor_tensor(modp[:, 3 * D:4 * D], sgn[:, 0:D], lnf[:, D:2 * D], ALU.mult)
            done(dve.tensor_copy(modp[:, 4 * D:5 * D], sgn[:, D:2 * D]))
            dve.wait_ge(s_zero, 3)
            done(dve.tensor_copy(mod16[0:BATCH, :], modp[:, :]))
            done(dve.tensor_tensor(modr[:, :], modp[:, :], mod16[0:BATCH, :], ALU.subtract))
            done(dve.tensor_copy(mid16[:, :], modr[:, :]))
            dve.tensor_copy(mod16[32:32 + BATCH, :], modr[:, :])
            done(dve.tensor_tensor(modr[:, :], modr[:, :], mid16[:, :], ALU.subtract))
            dve.tensor_copy(mod16[64:64 + BATCH, :], modr[:, :])
            dve.wait_ge(s_sel, 16)
            dve.tensor_copy(sel16[:, :], S[:, S_SEL:S_SEL + CH * P])
            for k in range(3):
                last = dve.tensor_copy(hot16[32 * k:32 * k + BATCH, :], S[0:BATCH, S_HOT:])
            last.then_inc(s_c16, 1)
            dve.wait_ge(s_bias, 64)
            dve.tensor_scalar(bias[:, :, 0:2 * D], bias[:, :, 0:2 * D], ident[:, P - 1:P], None, ALU.add)\
                .then_inc(s_plus, 1)
            dve.wait_ge(s_plus, 1)
            for n in range(2 * LAYERS):
                l, k = n // 2, n % 2
                w, part = (wqkv[:, l, :], bias[:, l, 0:QKV]) if k == 0 else (w1[:, l, :], bias[:, l, QKV:])
                dve.wait_ge(s_foldps, n + 1)
                dve.tensor_tensor(w, chains[2 + k].ps[:, l % 2, 0:w.shape[-1]], part, ALU.add).then_inc(s_folded, 1)
            dve.wait_ge(s_const, 10)

            def source(b, i, n):
                if n == 0:
                    return lambda t: x_tile(b, i, t)
                return (lambda t: b.y[:, t, :]) if n == LAST + 1 else (lambda t: b.x[:, t, :])

            def stats(b, i, n):
                src = source(b, i, n)
                if n > 0:
                    dve.wait_ge(b.s_moved.sem, b.s_moved.value(i, n))
                for t in range(TILES):
                    dve.bn_stats(b.stat[:, t, :], src(t))
                dve.drain()
                for t in range(TILES):
                    last = dve.bn_aggr(b.mv[:, t, :], b.stat[:, t, :])
                last.then_inc(b.s_moments.sem, 1)

            def scale(b, i, n):
                src = source(b, i, n)
                dst, width = (b.xn, D - 1) if 0 < n < LAST else (b.z, D)
                dve.wait_ge(b.s_rstd.sem, b.s_rstd.value(i, 2 * n + 2))
                for t in range(TILES):
                    last = dve.tensor_scalar(dst[:, t, 0:width], src(t)[:, 0:width], b.mv[:, t, 0:1],
                                             b.rstd[:, t:t + 1], ALU.subtract, ALU.mult)
                last.then_inc(b.s_normed.sem, 1)

            def enter(b, i, k):
                if k == 0:
                    dve.wait_ge(b.s_normed.sem, b.s_normed.value(i, 1))
                    dve.tensor_tensor(b.z[:, :, :], b.z[:, :, :], mod_row(b, i, 0), ALU.mult).then_inc(b.s_mod.sem, 1)
                elif k == 1:
                    dve.wait_ge(b.s_mod.sem, b.s_mod.value(i, 1))
                    dve.tensor_tensor(b.z[:, :, :], b.z[:, :, :], mod_row(b, i, 1), ALU.add).then_inc(b.s_mod.sem, 1)
                else:
                    dve.wait_ge(b.s_mod.sem, b.s_mod.value(i, 2))
                    dve.tensor_tensor(b.x[:, :, :], b.z[:, :, :], pos, ALU.add).then_inc(b.s_moved.sem, 1)

            def positive_keys(b, i, l):
                dve.wait_ge(b.s_v.sem, b.s_v.value(i, l + 1))
                keys = b.ps[:, 1, :].rearrange("p (t n) -> p t n", n=2 * D)[:, :, 0:D]
                dve.scalar_tensor_tensor(b.kp[:, :, :], b.ek, 1.0, keys, ALU.min, ALU.max).then_inc(b.s_kp.sem, 1)

            def positive_queries(b, i, l):
                dve.wait_ge(b.s_eq.sem, b.s_eq.value(i, l + 1))
                dve.scalar_tensor_tensor(b.qp[:, :], b.eq, 1.0, b.ps[:, 0, 0:T], ALU.min, ALU.max)\
                    .then_inc(b.s_qp.sem, 1)

            def masked(b, i, l):
                dve.wait_ge(b.s_sumps.sem, b.s_sumps.value(i, l + 1))
                dve.tensor_tensor(b.kv[:, :], b.ps[:, 1, 0:VW], headmask, ALU.mult).then_inc(b.s_kv.sem, 1)

            def divided(b, i, l):
                both = b.ps[:, 0, :].rearrange("p (t n) -> p t n", n=2 * D)
                dve.wait_ge(b.s_attps.sem, b.s_attps.value(i, l + 1))
                dve.tensor_scalar(b.den[:, :, :], both[:, :, D:VW], EPS_ATTN, None, ALU.add).then_inc(b.s_att.sem, 1)
                dve.wait_ge(b.s_att.sem, b.s_att.value(i, 3 * l + 1))
                dve.reciprocal(b.rden[:, :, :], b.den[:, :, :]).then_inc(b.s_att.sem, 1)
                dve.wait_ge(b.s_att.sem, b.s_att.value(i, 3 * l + 2))
                dve.tensor_tensor(b.att[:, :, :].rearrange("p t (h k) -> p t h k", k=DK),
                                  both[:, :, 0:D].rearrange("p t (h k) -> p t h k", k=DK),
                                  b.rden[:, :, :].unsqueeze(3).to_broadcast([P, TILES, HEADS, DK]), ALU.mult)\
                    .then_inc(b.s_att.sem, 1)

            def move(b, i, n):
                ps = (b.s_wops, b.s_w2ps)[(n - 1) % 2]
                dve.wait_ge(ps.sem, ps.value(i, (n - 1) // 2 + 1))
                dve.wait_ge(b.s_biased.sem, b.s_biased.value(i, n))
                dve.tensor_tensor(b.x[:, :, :], b.ps[:, 0, 0:T].rearrange("p (t f) -> p t f", f=D), b.x[:, :, :],
                                  ALU.add).then_inc(b.s_moved.sem, 1)

            def leave(b, i, k):
                if k == 0:
                    dve.wait_ge(b.s_normed.sem, b.s_normed.value(i, LAST + 1))
                    dve.tensor_tensor(b.z[:, :, :], b.z[:, :, :], mod_row(b, i, 2), ALU.mult).then_inc(b.s_mod.sem, 1)
                elif k == 1:
                    dve.wait_ge(b.s_mod.sem, b.s_mod.value(i, 3))
                    dve.tensor_tensor(b.z[:, :, :], b.z[:, :, :], mod_row(b, i, 3), ALU.add).then_inc(b.s_mod.sem, 1)
                else:
                    dve.wait_ge(b.s_mod.sem, b.s_mod.value(i, 4))
                    dve.tensor_tensor(b.y[:, :, :], b.z[:, :, :], x_tiles(b, i), ALU.add).then_inc(b.s_moved.sem, 1)

            def tokensT(b, i):
                dve.wait_ge(b.s_tps.sem, b.s_tps.value(i, 2 * LAYERS + 1))
                s = seq_of(b, i)
                dve.tensor_scalar(b.xT[:, :], b.ps[:, 0, 0:T], scaleT[:, bass.ds(s, 1)],
                                  shiftT[:, bass.ds(s, 1)], ALU.mult, ALU.add).then_inc(b.s_xT.sem, 1)

            def route(pair, i, part):
                n = [0 if part == 0 else 3]

                def step(op):
                    for b in pair:
                        op(b).then_inc(b.s_route.sem, 1)
                    n[0] += 1

                def then(op):
                    k = n[0]
                    for b in pair:
                        dve.wait_ge(b.s_route.sem, b.s_route.value(i, k))
                        op(b).then_inc(b.s_route.sem, 1)
                    n[0] += 1

                if part == 0:
                    for b in pair:
                        dve.wait_ge(b.s_eps.sem, b.s_eps.of(EXPERT_PS, "logits", i))
                        dve.tensor_copy(b.lg[:, :, :], b.ps[:, 1, 0:TILES * EXPERTS].rearrange(
                            "p (t e) -> p t e", e=EXPERTS)).then_inc(b.s_route.sem, 1)
                    n[0] += 1
                    then(lambda b: dve.tensor_reduce(b.mx[:, :], b.lg[:, :, :], AXX, ALU.max))
                    then(lambda b: dve.tensor_tensor(b.ls[:, :, :], b.lg[:, :, :],
                                                     b.mx[:, :].unsqueeze(2).to_broadcast([P, TILES, EXPERTS]),
                                                     ALU.subtract))
                    return
                four = [P, TILES, EXPERTS, EXPERTS]

                def other(b):
                    return b.lg[:, :, :].unsqueeze(2).to_broadcast(four)

                def mine(b):
                    return b.lg[:, :, :].unsqueeze(3).to_broadcast(four)

                step(lambda b: dve.tensor_tensor(b.tie[:, :, :, :], other(b), mine(b), ALU.is_equal))
                step(lambda b: dve.tensor_tensor(b.gt[:, :, :, :], other(b), mine(b), ALU.is_gt))
                then(lambda b: dve.tensor_tensor(b.tie[:, :, :, :], b.tie[:, :, :, :],
                                                 tri.unsqueeze(1).to_broadcast(four), ALU.mult))
                then(lambda b: dve.tensor_tensor(b.gt[:, :, :, :], b.gt[:, :, :, :], b.tie[:, :, :, :], ALU.add))
                then(lambda b: dve.tensor_reduce(b.rank[:, :, :], b.gt[:, :, :, :], AXX, ALU.add))
                for b in pair:
                    dve.wait_ge(b.s_eact.sem, b.s_eact.of(EXPERT_ACT, "exp", i))
                    dve.tensor_reduce(b.sum[:, :], b.ex[:, :, :], AXX, ALU.add).then_inc(b.s_route.sem, 1)
                n[0] += 1
                then(lambda b: dve.scalar_tensor_tensor(b.coef[:, :, :], b.rank[:, :, :], float(TOP), b.ex[:, :, :],
                                                        ALU.is_lt, ALU.mult))
                step(lambda b: dve.reciprocal(b.rsum[:, :], b.sum[:, :]))
                then(lambda b: dve.tensor_tensor(b.coef[:, :, :], b.coef[:, :, :],
                                                 b.rsum[:, :].unsqueeze(2).to_broadcast([P, TILES, EXPERTS]),
                                                 ALU.mult))
                then(lambda b: dve.tensor_copy(b.parts[:, :, 0, :], b.coef[:, :, :]))
                then(lambda b: dve.tensor_tensor(b.rest[:, :, :], b.coef[:, :, :], b.parts[:, :, 0, :], ALU.subtract))
                then(lambda b: dve.tensor_copy(b.parts[:, :, 1, :], b.rest[:, :, :]))
                then(lambda b: dve.tensor_tensor(b.rest2[:, :, :], b.rest[:, :, :], b.parts[:, :, 1, :], ALU.subtract))
                then(lambda b: dve.tensor_copy(b.parts[:, :, 2, :], b.rest2[:, :, :]))
                assert n[0] == ROUTE_STEPS

            def gate_up(b, i, k):
                dve.wait_ge(b.s_eact.sem, b.s_eact.of(EXPERT_ACT, f"silu{k}", i))
                dve.wait_ge(b.s_eps.sem, b.s_eps.of(EXPERT_PS, f"up{k}", i))
                if k < PAIRS:
                    if k > 0:
                        dve.wait_ge(b.s_units.sem, b.s_units.of(EXPERT_UNITS, f"weighed{k - 1}", i))
                    dve.tensor_tensor(flat(b.gu[:, :, :]), flat(b.eqk[:, :, :]), b.ps[:, 1 - k % 2, :], ALU.mult)\
                        .then_inc(b.s_units.sem, 1)
                else:
                    dve.tensor_tensor(b.hs[:, :], b.eqk[:, 0, :], b.ps[:, 1 - k % 2, 0:T], ALU.mult)\
                        .then_inc(b.s_units.sem, 1)

            def weigh(b, i, k):
                dve.wait_ge(b.s_units.sem, b.s_units.of(EXPERT_UNITS, f"product{k}", i))
                dve.wait_ge(b.s_eps.sem, b.s_eps.of(EXPERT_PS, f"spread{k}", i))
                dve.tensor_tensor(flat(b.h[:, 2 * k:2 * k + 2, :]), flat(b.gu[:, :, :]), b.ps[:, k % 2, :], ALU.mult)\
                    .then_inc(b.s_units.sem, 1)

            def finish(b, i, k):
                if k == 0:
                    dve.wait_ge(b.s_eps.sem, b.s_eps.of(EXPERT_PS, "down", i))
                    dve.tensor_tensor(b.z[:, :, :], b.ps[:, 0, 0:T].rearrange("p (t f) -> p t f", f=D),
                                      mod_row(b, i, 4), ALU.mult).then_inc(b.s_mod.sem, 1)
                else:
                    dve.wait_ge(b.s_mod.sem, b.s_mod.value(i, 5))
                    dve.tensor_tensor(x_tiles(b, i), b.z[:, :, :], b.y[:, :, :], ALU.add).then_inc(b.s_out.sem, 1)

            dve.wait_ge(s_rowsb, BATCH)
            dve.wait_ge(s_x, 16 * STEPS)
            a, _, f, _ = phase(0)
            stats(a[0], 0, 0)
            stats(a[1], 0, 0)
            stats(f[0], 0, 0)
            stats(f[1], 0, 0)
            scale(a[0], 0, 0)
            enter(a[0], 0, 0)
            enter(a[0], 0, 1)
            enter(a[0], 0, 2)
            stats(a[0], 0, 1)
            scale(a[0], 0, 1)
            scale(a[1], 0, 0)
            enter(a[1], 0, 0)
            enter(a[1], 0, 1)
            enter(a[1], 0, 2)
            stats(a[1], 0, 1)
            scale(a[1], 0, 1)
            positive_keys(a[0], 0, 0)
            scale(f[0], 0, 0)
            positive_queries(a[0], 0, 0)
            masked(a[0], 0, 0)
            enter(f[0], 0, 0)
            scale(f[1], 0, 0)
            divided(a[0], 0, 0)
            enter(f[1], 0, 0)
            enter(f[0], 0, 1)
            enter(f[0], 0, 2)
            positive_keys(a[1], 0, 0)
            positive_queries(a[1], 0, 0)
            masked(a[1], 0, 0)
            move(a[0], 0, 1)
            divided(a[1], 0, 0)
            stats(a[0], 0, 2)
            scale(a[0], 0, 2)
            stats(f[0], 0, 1)
            move(a[1], 0, 1)
            stats(a[1], 0, 2)
            scale(a[1], 0, 2)
            scale(f[0], 0, 1)
            enter(f[1], 0, 1)
            enter(f[1], 0, 2)
            stats(f[1], 0, 1)
            scale(f[1], 0, 1)
            with dve.Fori(0, STEPS) as i:
                for n in range(1, PHASES):
                    a, l, f, m = phase(n)
                    if n == 1:
                        positive_keys(a[0], i, 0)
                        positive_queries(a[0], i, 0)
                        masked(a[0], i, 0)
                        move(f[0], i, 2)
                        stats(f[0], i, 3)
                        divided(a[0], i, 0)
                        positive_keys(a[1], i, 0)
                        positive_queries(a[1], i, 0)
                        masked(a[1], i, 0)
                        move(a[0], i, 1)
                        stats(a[0], i, 2)
                        divided(a[1], i, 0)
                        scale(f[0], i, 3)
                    elif n < PHASES - 3:
                        scale(f[0], i, 2 * m + 2)
                        move(a[1], i, 2 * l)
                        stats(a[1], i, 2 * l + 1)
                        move(f[1], i, 2 * m + 1)
                        stats(f[1], i, 2 * m + 2)
                        scale(a[1], i, 2 * l + 1)
                        positive_keys(a[0], i, l)
                        scale(f[1], i, 2 * m + 2)
                        positive_queries(a[0], i, l)
                        masked(a[0], i, l)
                        positive_keys(a[1], i, l)
                        divided(a[0], i, l)
                        positive_queries(a[1], i, l)
                        masked(a[1], i, l)
                        move(f[0], i, 2 * m + 2)
                        stats(f[0], i, 2 * m + 3)
                        divided(a[1], i, l)
                        move(a[0], i, 2 * l + 1)
                        stats(a[0], i, 2 * l + 2)
                        scale(f[0], i, 2 * m + 3)
                    elif l < LAYERS:
                        scale(f[0], i, 2 * m + 2)
                        move(a[1], i, 2 * l)
                        stats(a[1], i, 2 * l + 1)
                        scale(a[1], i, 2 * l + 1)
                        move(f[1], i, 2 * m + 1)
                        positive_keys(a[0], i, l)
                        stats(f[1], i, 2 * m + 2)
                        positive_queries(a[0], i, l)
                        masked(a[0], i, l)
                        scale(f[1], i, 2 * m + 2)
                        positive_keys(a[1], i, l)
                        positive_queries(a[1], i, l)
                        divided(a[0], i, l)
                        move(f[0], i, 2 * m + 2)
                        masked(a[1], i, l)
                        stats(f[0], i, 2 * m + 3)
                        divided(a[1], i, l)
                        scale(f[0], i, 2 * m + 3)
                        move(a[0], i, 2 * l + 1)
                        leave(f[0], i, 0)
                        stats(a[0], i, 2 * l + 2)
                        leave(f[0], i, 1)
                        leave(f[0], i, 2)
                        stats(f[0], i, LAST + 1)
                        scale(a[0], i, 2 * l + 2)
                        move(f[1], i, 2 * m + 2)
                        stats(f[1], i, 2 * m + 3)
                        move(a[1], i, 2 * l + 1)
                        stats(a[1], i, 2 * l + 2)
                        scale(f[1], i, 2 * m + 3)
                        leave(f[1], i, 0)
                        leave(f[1], i, 1)
                        leave(f[1], i, 2)
                        stats(f[1], i, LAST + 1)
                        scale(f[0], i, LAST + 1)
                        scale(a[1], i, 2 * l + 2)
                        scale(f[1], i, LAST + 1)
                        tokensT(f[0], i)
                        tokensT(f[1], i)
                        route(f, i, 0)
                        route(f, i, 1)
                        gate_up(f[0], i, 0)
                    elif m < LAYERS:
                        gate_up(a[1], i, 0)
                        weigh(a[0], i, 0)
                        weigh(a[1], i, 0)
                        gate_up(a[1], i, 1)
                        gate_up(a[0], i, 1)
                        weigh(a[0], i, 1)
                        move(f[0], i, 2 * m + 2)
                        stats(f[0], i, LAST)
                        weigh(a[1], i, 1)
                        move(f[1], i, 2 * m + 2)
                        stats(f[1], i, LAST)
                        gate_up(a[0], i, 2)
                    else:
                        scale(a[0], i, LAST)
                        gate_up(f[1], i, 2)
                        leave(a[0], i, 0)
                        scale(a[1], i, LAST)
                        leave(a[0], i, 1)
                        leave(a[1], i, 0)
                        leave(a[0], i, 2)
                        leave(a[1], i, 1)
                        finish(f[0], i, 0)
                        stats(a[0], i, LAST + 1)
                        finish(f[0], i, 1)
                        stats(f[0], i + 1, 0)
                        finish(f[1], i, 0)
                        leave(a[1], i, 2)
                        finish(f[1], i, 1)
                        stats(f[1], i + 1, 0)
                        stats(a[1], i, LAST + 1)
                        scale(f[0], i + 1, 0)
                        scale(a[0], i, LAST + 1)
                        enter(f[0], i + 1, 0)
                        scale(f[1], i + 1, 0)
                        enter(f[0], i + 1, 1)
                        enter(f[1], i + 1, 0)
                        enter(f[0], i + 1, 2)
                        enter(f[1], i + 1, 1)
                        stats(f[0], i + 1, 1)
                        enter(f[1], i + 1, 2)
                        tokensT(a[0], i)
                        stats(f[1], i + 1, 1)
                        scale(a[1], i, LAST + 1)
                        scale(f[0], i + 1, 1)
                        scale(f[1], i + 1, 1)
                        tokensT(a[1], i)
                        route(a, i, 0)
                        route(a, i, 1)
                        gate_up(a[0], i, 0)
                        gate_up(a[1], i, 0)
                        positive_keys(f[0], i + 1, 0)
                        positive_queries(f[0], i + 1, 0)
                        positive_keys(f[1], i + 1, 0)
                        masked(f[0], i + 1, 0)
                        positive_queries(f[1], i + 1, 0)
                        masked(f[1], i + 1, 0)
                        weigh(a[1], i, 0)
                        weigh(a[0], i, 0)
                        divided(f[0], i + 1, 0)
                        divided(f[1], i + 1, 0)
                        gate_up(a[1], i, 1)
                        weigh(a[1], i, 1)
                        gate_up(a[0], i, 1)
                        weigh(a[0], i, 1)
                        move(f[0], i + 1, 1)
                        gate_up(a[0], i, 2)
                        move(f[1], i + 1, 1)
                        stats(f[1], i + 1, 2)
                        gate_up(a[1], i, 2)
                        stats(f[0], i + 1, 2)
                        scale(f[1], i + 1, 2)
                        finish(a[0], i, 0)
                        finish(a[0], i, 1)
                        stats(a[0], i + 1, 0)
                        scale(f[0], i + 1, 2)
                        finish(a[1], i, 0)
                        scale(a[0], i + 1, 0)
                        finish(a[1], i, 1)
                        enter(a[0], i + 1, 0)
                        stats(a[1], i + 1, 0)
                        enter(a[0], i + 1, 1)
                        enter(a[0], i + 1, 2)
                        stats(a[0], i + 1, 1)
                        scale(a[1], i + 1, 0)
                        enter(a[1], i + 1, 0)
                        scale(a[0], i + 1, 1)
                        enter(a[1], i + 1, 1)
                        enter(a[1], i + 1, 2)
                        stats(a[1], i + 1, 1)
                        scale(a[1], i + 1, 1)

        @block.tensor
        def _(pe):
            def mm(o, lhsT, rhs, start=True, stop=True):
                return pe.matmul(o, lhsT, rhs, start=start, stop=stop)

            pe.wait_ge(s_k, 16)
            pe.wait_ge(s_par, 16 * 5)
            n_par = 4 * LAYERS + BATCH
            pe.transpose(A.ps[:, 0, 0:n_par], par[:, :], ident[0:n_par, 0:n_par]).then_inc(s_parps, 1)
            pe.wait_ge(s_condT, 1)
            pe.wait_ge(s_wm, 16)
            mm(A.ps[0:BATCH, 0, :], condT[:, :], wm[:, 0:512])
            mm(A.ps[0:BATCH, 1, 0:6 * D - 512], condT[:, :], wm[:, 512:6 * D])
            mm(B.ps[:, 0, 0:BATCH], wm[:, 3 * D:4 * D], condT[:, :])
            mm(B.ps[:, 0, BATCH:2 * BATCH], wm[:, 4 * D:5 * D], condT[:, :]).then_inc(s_modps, 1)
            pe.wait_ge(s_wqkv, 48)
            pe.wait_ge(s_w1, 16)
            pe.wait_ge(s_fold, 2 * LAYERS)

            def fold_weight(n):
                l, k = n // 2, n % 2
                w, width = (wqkv[:, l, :], QKV) if k == 0 else (w1[:, l, :], FF)
                if n >= 4:
                    pe.wait_ge(s_folded, n - 3)
                mm(chains[2 + k].ps[:, l % 2, 0:width], fold[:, n, :], w).then_inc(s_foldps, 1)

            for n in range(4):
                fold_weight(n)
            pe.wait_ge(s_modsb, 12)
            pe.wait_ge(s_c16, 1)
            for s in range(BATCH):
                if s >= 2:
                    pe.wait_ge(s_rowsb, s - 1)
                hot, ps = hot16[:, s * P:(s + 1) * P], chains[s % 2].ps
                mm(ps[:, 0, :], hot, mod16[:, 0:512])
                mm(ps[:, 1, 0:MOD - 512], hot, mod16[:, 512:MOD]).then_inc(s_rowps, 1)
            for n in range(4, 2 * LAYERS):
                fold_weight(n)
            pe.wait_ge(s_folded, 2 * LAYERS)
            pe.wait_ge(s_rowsb, BATCH)
            pe.wait_ge(s_const, 10)

            def transposes(b, i, n):
                norm, src = (n + 1, b.xn) if n < 2 * LAYERS else (LAST + 1, b.z)
                pe.wait_ge(b.s_normed.sem, b.s_normed.value(i, norm + 1))
                for t in range(TILES):
                    last = pe.transpose(b.ps[:, n % 2, t * P:(t + 1) * P], src[:, t, :], ident)
                last.then_inc(b.s_tps.sem, 1)

            def project_keys(b, i, l):
                pe.wait_ge(b.s_xT.sem, b.s_xT.value(i, 2 * l + 1))
                for t in range(TILES):
                    last = mm(b.ps[:, 1, t * 2 * D:(t + 1) * 2 * D], b.xT[:, t * P:(t + 1) * P], wqkv[:, l, D:QKV])
                last.then_inc(b.s_kvps.sem, 1)

            def project_queries(b, i, l):
                mm(b.ps[:, 0, 0:T], wqkv[:, l, 0:D], b.xT[:, :]).then_inc(b.s_qps.sem, 1)

            def sums(b, i, l):
                pe.wait_ge(b.s_kp.sem, b.s_kp.value(i, l + 1))
                for t in range(TILES):
                    last = mm(b.ps[:, 1, 0:VW], b.kp[:, t, :], b.v[:, t, :], start=t == 0, stop=t == TILES - 1)
                last.then_inc(b.s_sumps.sem, 1)

            def attend(b, i, l):
                pe.wait_ge(b.s_qp.sem, b.s_qp.value(i, l + 1))
                pe.wait_ge(b.s_kv.sem, b.s_kv.value(i, l + 1))
                for t in range(TILES):
                    last = mm(b.ps[:, 0, t * 2 * D:t * 2 * D + VW], b.qp[:, t * P:(t + 1) * P], b.kv[:, :])
                last.then_inc(b.s_attps.sem, 1)

            def out_project(b, i, l):
                pe.wait_ge(b.s_att.sem, b.s_att.value(i, 3 * l + 3))
                for t in range(TILES):
                    last = pe.transpose(b.ps[:, 1, t * P:(t + 1) * P], b.att[:, t, :], ident)
                last.then_inc(b.s_atps.sem, 1)

            def out_project2(b, i, l):
                pe.wait_ge(b.s_attT.sem, b.s_attT.value(i, l + 1))
                for t in range(TILES):
                    last = mm(b.ps[:, 0, t * P:(t + 1) * P], b.attT[:, t * P:(t + 1) * P], wo[:, l, :])
                last.then_inc(b.s_wops.sem, 1)

            def expand(b, i, l, k):
                pe.wait_ge(b.s_xT.sem, b.s_xT.value(i, 2 * l + 2))
                for c in (2 * k, 2 * k + 1):
                    last = mm(b.ps[:, k, c % 2 * T:(c % 2 + 1) * T], w1[:, l, c * P:(c + 1) * P], b.xT[:, :])
                last.then_inc(b.s_w1ps.sem, 1)

            def contract(b, i, l):
                pe.wait_ge(b.s_h.sem, b.s_h.value(i, (l + 1) * PAIRS))
                for t in range(TILES):
                    for c in range(CH):
                        last = mm(b.ps[:, 0, t * P:(t + 1) * P], b.h[:, c, t * P:(t + 1) * P], w2[:, l, c, :],
                                  start=c == 0, stop=c == CH - 1)
                last.then_inc(b.s_w2ps.sem, 1)

            def logits(b, i):
                transposes(b, i, 2 * LAYERS)

            def logits2(b, i):
                pe.wait_ge(b.s_xT.sem, b.s_xT.value(i, 2 * LAYERS + 1))
                for t in range(TILES):
                    last = mm(b.ps[:, 1, t * EXPERTS:(t + 1) * EXPERTS], b.xT[:, t * P:(t + 1) * P], wr[:, :])
                last.then_inc(b.s_eps.sem, 1)

            def two(b, bank, w, k):
                for j, c in enumerate(range(2 * k, min(2 * k + 2, CH + 1))):
                    last = mm(b.ps[:, bank, j * T:(j + 1) * T], w[:, c, :], b.xT[:, :])
                last.then_inc(b.s_eps.sem, 1)

            def gate(b, i, k):
                if k == 1:
                    pe.wait_ge(b.s_eact.sem, b.s_eact.of(EXPERT_ACT, "coefT", i))
                elif k == 2:
                    pe.wait_ge(b.s_units.sem, b.s_units.of(EXPERT_UNITS, "product1", i))
                two(b, k % 2, wg, k)

            def up(b, i, k):
                if k == 0:
                    pe.wait_ge(b.s_route.sem, b.s_route.value(i, 1))
                else:
                    pe.wait_ge(b.s_units.sem, b.s_units.of(EXPERT_UNITS, f"weighed{k - 1}", i))
                two(b, 1 - k % 2, wu, k)

            def coef_transposes(b, i):
                pe.wait_ge(b.s_route.sem, b.s_route.value(i, b.s_route.per))
                pe.wait_ge(b.s_units.sem, b.s_units.of(EXPERT_UNITS, "product0", i))
                cps = b.ps[0:S_ROWS, 1, 0:T // 2].bitcast(BF16)
                for t in range(TILES):
                    last = pe.transpose(cps[:, t * P:(t + 1) * P],
                                        b.parts[:, t, :, :].rearrange("p k e -> p (k e)"), ident16[:, :])
                last.then_inc(b.s_eps.sem, 1)

            def spread(b, i, k):
                pe.wait_ge(b.s_eact.sem, b.s_eact.of(EXPERT_ACT, "coefT", i))
                pe.wait_ge(b.s_eact.sem, b.s_eact.of(EXPERT_ACT, f"silu{k}", i))
                for j in range(2):
                    c = 2 * k + j
                    last = mm(b.ps[:, k % 2, j * T:(j + 1) * T], sel16[:, c * P:(c + 1) * P], b.coefT[:, :])
                last.then_inc(b.s_eps.sem, 1)

            def down(b, i):
                pe.wait_ge(b.s_units.sem, b.s_units.of(EXPERT_UNITS, f"product{PAIRS}", i))
                for t in range(TILES):
                    tok = slice(t * P, (t + 1) * P)
                    for c in range(CH + 1):
                        hid = b.h[:, c, tok] if c < CH else b.hs[:, tok]
                        last = mm(b.ps[:, 0, tok], hid, wd[:, c, :], start=c == 0, stop=c == CH)
                last.then_inc(b.s_eps.sem, 1)

            a, _, f, _ = phase(0)
            pe.wait_ge(s_rest, 64)
            transposes(a[0], 0, 0)
            project_keys(a[0], 0, 0)
            project_queries(a[0], 0, 0)
            sums(a[0], 0, 0)
            transposes(a[1], 0, 0)
            attend(a[0], 0, 0)
            project_keys(a[1], 0, 0)
            project_queries(a[1], 0, 0)
            out_project(a[0], 0, 0)
            sums(a[1], 0, 0)
            out_project2(a[0], 0, 0)
            attend(a[1], 0, 0)
            out_project(a[1], 0, 0)
            out_project2(a[1], 0, 0)
            pe.wait_ge(s_wmoe, 16 * 7)
            with pe.Fori(0, STEPS) as i:
                for n in range(1, PHASES):
                    a, l, f, m = phase(n)
                    if n == 1:
                        transposes(f[0], i, 1)
                        expand(f[0], i, 0, 0)
                        expand(f[0], i, 0, 1)
                        transposes(f[1], i, 1)
                        contract(f[0], i, 0)
                        transposes(a[0], i, 0)
                        expand(f[1], i, 0, 0)
                        project_keys(a[0], i, 0)
                        project_queries(a[0], i, 0)
                        transposes(a[1], i, 0)
                        sums(a[0], i, 0)
                        project_keys(a[1], i, 0)
                        attend(a[0], i, 0)
                        expand(f[1], i, 0, 1)
                        project_queries(a[1], i, 0)
                        out_project(a[0], i, 0)
                        sums(a[1], i, 0)
                        out_project2(a[0], i, 0)
                        attend(a[1], i, 0)
                        contract(f[1], i, 0)
                        out_project(a[1], i, 0)
                    elif n < PHASES - 3:
                        transposes(a[0], i, 2 * l)
                        out_project2(f[1], i, m)
                        transposes(f[0], i, 2 * m + 1)
                        project_keys(a[0], i, l)
                        expand(f[0], i, m, 0)
                        expand(f[0], i, m, 1)
                        transposes(a[1], i, 2 * l)
                        project_queries(a[0], i, l)
                        sums(a[0], i, l)
                        transposes(f[1], i, 2 * m + 1)
                        project_keys(a[1], i, l)
                        project_queries(a[1], i, l)
                        expand(f[1], i, m, 0)
                        attend(a[0], i, l)
                        sums(a[1], i, l)
                        contract(f[0], i, m)
                        out_project(a[0], i, l)
                        attend(a[1], i, l)
                        expand(f[1], i, m, 1)
                        out_project2(a[0], i, l)
                        out_project(a[1], i, l)
                        contract(f[1], i, m)
                    elif l < LAYERS:
                        transposes(a[0], i, 2 * l)
                        out_project2(f[1], i, m)
                        transposes(f[0], i, 2 * m + 1)
                        project_keys(a[0], i, l)
                        expand(f[0], i, m, 0)
                        expand(f[0], i, m, 1)
                        transposes(a[1], i, 2 * l)
                        project_queries(a[0], i, l)
                        sums(a[0], i, l)
                        project_keys(a[1], i, l)
                        project_queries(a[1], i, l)
                        attend(a[0], i, l)
                        contract(f[0], i, m)
                        sums(a[1], i, l)
                        transposes(f[1], i, 2 * m + 1)
                        out_project(a[0], i, l)
                        attend(a[1], i, l)
                        out_project2(a[0], i, l)
                        expand(f[1], i, m, 0)
                        expand(f[1], i, m, 1)
                        out_project(a[1], i, l)
                        contract(f[1], i, m)
                        out_project2(a[1], i, l)
                        transposes(a[0], i, 2 * l + 1)
                        expand(a[0], i, l, 0)
                        expand(a[0], i, l, 1)
                        logits(f[0], i)
                        transposes(a[1], i, 2 * l + 1)
                        logits(f[1], i)
                        logits2(f[0], i)
                        gate(f[0], i, 0)
                        logits2(f[1], i)
                    elif m < LAYERS:
                        gate(a[1], i, 0)
                        up(a[1], i, 0)
                        up(a[0], i, 0)
                        expand(f[1], i, m, 0)
                    else:
                        expand(a[1], i, l - 1, 1)
                        coef_transposes(f[0], i)
                        coef_transposes(f[1], i)
                        spread(f[0], i, 0)
                        gate(f[0], i, 1)
                        spread(f[1], i, 0)
                        gate(f[1], i, 1)
                        up(f[0], i, 1)
                        up(f[1], i, 1)
                        spread(f[1], i, 1)
                        spread(f[0], i, 1)
                        contract(a[0], i, l - 1)
                        contract(a[1], i, l - 1)
                        gate(f[0], i, 2)
                        up(f[0], i, 2)
                        gate(f[1], i, 2)
                        up(f[1], i, 2)
                        down(f[0], i)
                        down(f[1], i)
                        logits(a[0], i)
                        logits2(a[0], i)
                        gate(a[0], i, 0)
                        logits(a[1], i)
                        transposes(f[0], i + 1, 0)
                        transposes(f[1], i + 1, 0)
                        logits2(a[1], i)
                        gate(a[1], i, 0)
                        up(a[1], i, 0)
                        up(a[0], i, 0)
                        project_keys(f[0], i + 1, 0)
                        project_queries(f[0], i + 1, 0)
                        project_keys(f[1], i + 1, 0)
                        coef_transposes(a[1], i)
                        sums(f[0], i + 1, 0)
                        coef_transposes(a[0], i)
                        project_queries(f[1], i + 1, 0)
                        sums(f[1], i + 1, 0)
                        spread(a[1], i, 0)
                        spread(a[0], i, 0)
                        gate(a[1], i, 1)
                        attend(f[0], i + 1, 0)
                        attend(f[1], i + 1, 0)
                        up(a[1], i, 1)
                        gate(a[0], i, 1)
                        spread(a[1], i, 1)
                        up(a[0], i, 1)
                        out_project(f[0], i + 1, 0)
                        spread(a[0], i, 1)
                        gate(a[1], i, 2)
                        out_project(f[1], i + 1, 0)
                        out_project2(f[0], i + 1, 0)
                        gate(a[0], i, 2)
                        up(a[0], i, 2)
                        out_project2(f[1], i + 1, 0)
                        up(a[1], i, 2)
                        down(a[0], i)
                        down(a[1], i)


_INS = ["attn_x_in", "attn_Wq", "attn_bq", "attn_Wk", "attn_bk", "attn_Wv", "attn_bv", "attn_Wo", "attn_bo",
        "attn_W1", "attn_b1", "attn_W2", "attn_b2", "attn_ln1_s", "attn_ln1_b", "attn_ln2_s", "attn_ln2_b",
        "attn_lnf_s", "attn_lnf_b", "ffn_router", "ffn_experts_gate", "ffn_experts_up", "ffn_experts_down",
        "ffn_shared_gate", "ffn_shared_up", "ffn_shared_down", "c", "wmod"]


def build(nc, inputs):
    arrays, args = {}, []
    for name in _INS:
        arrays["in_" + name] = np.ascontiguousarray(inputs["L0_" + name])
    arrays["in_consts"] = constants()
    arrays["in_selectors"] = selectors()
    for name, a in arrays.items():
        args.append(nc.dram_tensor(name, a.shape, mybir.dt.from_np(a.dtype), kind="ExternalInput").ap())
    args.append(nc.dram_tensor("out", (BATCH, T, D), F32, kind="ExternalOutput").ap())
    program(nc, *args)
    return arrays


def kernel(**inputs):
    from concourse.bacc import Bacc
    from concourse.bass_utils import run_bass_kernel_spmd

    nc = Bacc("TRN2", target_bir_lowering=False, num_devices=1)
    arrays = build(nc, inputs)
    return run_bass_kernel_spmd(nc, [arrays], core_ids=[0]).results[0]["out"]
```

```python
from contextlib import ExitStack

import numpy as np

import concourse.bass as bass
from concourse import mybir
from concourse.alu_op_type import AluOpType as ALU

F32 = mybir.dt.float32
F32R = mybir.dt.float32r
ACT = mybir.ActivationFunctionType
AXX = mybir.AxisListType.X

BATCH, T, D = 16, 256, 128
LAYERS, HEADS, FF = 4, 16, 512
DK = D // HEADS
EXPERTS, DE, TOP = 8, 64, 2
P = 128
CHAINS = 4
TILES = T // P
STEPS = BATCH // CHAINS
CH = FF // P
PAIRS = CH // 2
VW = D + HEADS
QKV = 3 * D
MOD = 5 * D
EPS = 1e-5
EPS_ATTN = 1e-6
NORMS = 2 * LAYERS + 3
LAST = 2 * LAYERS + 1
EXPERT_PS = ("logits", "gate0", "up0", "coefT", "spread0", "gate1", "up1", "spread1", "gate2", "up2", "down")
EXPERT_ACT = ("exp", "silu0", "coefT", "silu1", "silu2")
EXPERT_UNITS = ("product0", "weighed0", "product1", "weighed1", "product2")
MOD_STEPS = 8
ROUTE_STEPS = 14
PHASES = 2 * LAYERS + 2

C_ID = 0
C_MASK = C_ID + P
C_TRI = C_MASK + VW
C_POS = C_TRI + EXPERTS * EXPERTS
C_BASE = C_POS + T // P * D
C_ALL = C_BASE + P
PARTS = 2
S_ROWS = PARTS * EXPERTS
SPREAD = (2, 2, 4, 8)


def constants():
    k = np.zeros((P, C_ALL), np.float32)
    p = np.arange(P)
    k[:, C_ID:C_ID + P] = np.eye(P)
    k[:, C_MASK:C_MASK + D] = p[:, None] // DK == p[None, :] // DK
    k[:, C_MASK + D:C_MASK + VW] = p[:, None] // DK == np.arange(HEADS)[None, :]
    e = np.arange(EXPERTS)
    k[:, C_TRI:C_TRI + EXPERTS ** 2] = (e[None, :] < e[:, None]).reshape(1, -1)
    half = D // 2
    freq = np.exp(np.arange(half, dtype=np.float32) * np.float32(-np.log(10000.0) / (half - 1)))
    pos = (np.arange(T, dtype=np.float32) + np.float32(1))[:, None] * freq[None, :]
    pos = np.concatenate([np.sin(pos), np.cos(pos)], axis=-1)
    k[:, C_POS:C_POS + T // P * D] = pos.reshape(T // P, P, D).transpose(1, 0, 2).reshape(P, -1)
    base = np.eye(P)
    base[P - 1, :] = -1
    k[:, C_BASE:C_BASE + P] = base
    return k


def selectors():
    k = np.zeros((S_ROWS, CH * P), np.float32)
    for c in range(CH):
        for m in range(P):
            k[2 * c + m // DE + EXPERTS * np.arange(PARTS), c * P + m] = 1
    return k


class Signal:

    def __init__(self, sem, per):
        self.sem, self.per = sem, per

    def value(self, i, n):
        return i * self.per + n

    def of(self, names, name, i):
        return self.value(i, names.index(name) + 1)


def program(nc, x_in, Wq, bq, Wk, bk, Wv, bv, Wo, bo, W1, b1, W2, b2, ln1_s, ln1_b, ln2_s, ln2_b, lnf_s, lnf_b,
            router, e_gate, e_up, e_down, s_gate, s_up, s_down, cond, wmod, consts, select, out, rows):
    nc.disable_value_cache = True
    ctx = ExitStack()
    with ctx:
        def sb(name, shape, dt=F32):
            return ctx.enter_context(nc.sbuf_tensor(name, shape, dt))

        def sem(name):
            return ctx.enter_context(nc.semaphore(name))

        def flat(ap):
            return ap.rearrange("p a b -> p (a b)")

        K = sb("K", [P, C_ALL])
        ident, base = K[:, C_ID:C_ID + P], K[:, C_BASE:C_BASE + P]
        headmask = K[:, C_MASK:C_MASK + VW]
        tri = K[:, C_TRI:C_TRI + EXPERTS ** 2].rearrange("p (j k) -> p j k", k=EXPERTS)
        pos = K[:, C_POS:C_POS + TILES * D].rearrange("p (t f) -> p t f", f=D)
        sel_hi = sb("sel_hi", [S_ROWS, CH * P], F32R)
        sel = sb("sel", [S_ROWS, CH * P])
        X = sb("X", [P, BATCH * TILES * D])
        par = sb("par", [4 * LAYERS, D])
        parT = sb("parT", [P, 4 * LAYERS])
        c_in = sb("c_in", [BATCH, D])
        condT = sb("condT", [P, BATCH])
        wqkv_hi, wqkv_lo = sb("wqkv_hi", [P, LAYERS, QKV], F32R), sb("wqkv_lo", [P, LAYERS, QKV], F32R)
        w1_hi, w1_lo = sb("w1_hi", [P, LAYERS, FF], F32R), sb("w1_lo", [P, LAYERS, FF], F32R)
        w2 = sb("w2", [P, LAYERS, CH, D])
        wo = sb("wo", [P, LAYERS, D])
        bo_all = sb("bo_all", [P, LAYERS, D])
        b2_all = sb("b2_all", [P, LAYERS, D])
        fold = sb("fold", [P, 2 * LAYERS, P])
        wm = sb("wm", [P, 6 * D])
        M = sb("M", [P, BATCH, MOD])
        H = sb("H", [P, CHAINS * CH * T])
        bias = H[:, 0:LAYERS * (QKV + FF)].rearrange("p (l n) -> p l n", n=QKV + FF)
        last_rows = flat(M[:, BATCH - SPREAD[-1]:, :])
        wqkv = last_rows[:, 0:LAYERS * QKV].rearrange("p (l n) -> p l n", n=QKV)
        w1 = last_rows[:, LAYERS * QKV:LAYERS * (QKV + FF)].rearrange("p (l n) -> p l n", n=FF)
        mod = flat(M[:, :, :])[0:BATCH, BATCH * MOD - 6 * D:]
        modp = flat(M[:, :, :])[0:BATCH, BATCH * MOD - 6 * D - MOD:BATCH * MOD - 6 * D]
        gates = H[0:BATCH, LAYERS * (QKV + FF):]
        sgn, lnf = gates[:, 0:2 * D], gates[:, 2 * D:4 * D]
        shiftT = sb("shiftT", [P, BATCH])
        scaleT = sb("scaleT", [P, BATCH])
        wr = sb("wr", [P, EXPERTS])
        wg = sb("wg", [P, CH + 1, P])
        wu = sb("wu", [P, CH + 1, P])
        wd = sb("wd", [P, CH + 1, D])
        rowsum = sb("rowsum", [P, LAYERS * CH])
        rowmean = sb("rowmean", [P, LAYERS])
        neghalf = sb("neghalf", [P, TILES])
        epsilon = sb("epsilon", [P, TILES])

        class Chain:
            pass

        chains = []
        for c in range(CHAINS):
            b = Chain()
            b.c = c
            n = "ABCD"[c]
            b.x = sb("x" + n, [P, TILES, D])
            b.stat = sb("stat" + n, [P, TILES, 6])
            b.mv = sb("mv" + n, [P, TILES, 2])
            b.ms = sb("ms" + n, [P, TILES])
            b.negmean = sb("negmean" + n, [P, TILES])
            b.ve = sb("ve" + n, [P, TILES])
            b.rstd = sb("rstd" + n, [P, TILES])
            b.xn = sb("xn" + n, [P, TILES, D])
            b.gu = sb("gu" + n, [P, 2, T])
            b.z = b.gu[:, 0, :].rearrange("p (t f) -> p t f", f=D)
            b.attT = b.gu[:, 1, :]
            b.zi = sb("zi" + n, [P, TILES, D])
            b.x_hi = sb("xhi" + n, [P, T], F32R)
            b.x_lo = sb("xlo" + n, [P, T], F32R)
            b.eqk = sb("eqk" + n, [P, 2, T])
            b.eq, b.ek = b.eqk[:, 0, :], b.eqk[:, 1, :].rearrange("p (t f) -> p t f", f=D)
            b.qp = sb("qp" + n, [P, T])
            b.kp = sb("kp" + n, [P, TILES, D])
            b.v = sb("v" + n, [P, TILES, VW])
            b.kv = sb("kv" + n, [P, VW])
            b.den = sb("den" + n, [P, TILES, HEADS])
            b.rden = sb("rden" + n, [P, TILES, HEADS])
            b.att = sb("att" + n, [P, TILES, D])
            b.y = b.att
            b.h = H[:, c * CH * T:(c + 1) * CH * T].rearrange("p (c t) -> p c t", t=T)
            b.hs = b.qp
            b.xT = b.kp[:, :, :].rearrange("p t f -> p (t f)")
            b.lg = sb("lg" + n, [P, TILES, EXPERTS])
            b.mx = sb("mx" + n, [P, TILES])
            b.ls = sb("ls" + n, [P, TILES, EXPERTS])
            b.ex = sb("ex" + n, [P, TILES, EXPERTS])
            b.gt = sb("gt" + n, [P, TILES, EXPERTS, EXPERTS])
            b.tie = sb("tie" + n, [P, TILES, EXPERTS, EXPERTS])
            b.rank = sb("rank" + n, [P, TILES, EXPERTS])
            b.sum = sb("sum" + n, [P, TILES])
            b.rsum = sb("rsum" + n, [P, TILES])
            b.coef = sb("coef" + n, [P, TILES, EXPERTS])
            b.parts = sb("parts" + n, [P, TILES, PARTS, EXPERTS], F32R)
            b.coefT = sb("coefT" + n, [S_ROWS, T], F32R)
            b.ps = ctx.enter_context(nc.psum_tensor("ps" + n, [P, 2, 512], F32))

            def sig(name, per, n=n):
                return Signal(sem(name + n), per)

            b.s_moved = sig("moved", 2 * LAYERS + 2)
            b.s_moments = sig("moments", 2)
            b.s_centred = sig("centred", 2)
            b.s_squares = sig("squares", LAST)
            b.s_rstd = sig("rstd", 2 * NORMS)
            b.s_normed = sig("normed", NORMS)
            b.s_biased = sig("biased", 2 * LAYERS + 2)
            b.s_tps = sig("tps", 2 * LAYERS + 1)
            b.s_xT = sig("xT", 2 * LAYERS + 1)
            b.s_x_lo = sig("xlo", 2 * LAYERS)
            b.s_qkvps = sig("qkvps", 2 * LAYERS)
            b.s_v = sig("v", LAYERS)
            b.s_eq = sig("eq", LAYERS)
            b.s_pos = sig("pos", 2 * LAYERS)
            b.s_sumps = sig("sumps", LAYERS)
            b.s_kv = sig("kv", LAYERS)
            b.s_attps = sig("attps", LAYERS)
            b.s_att = sig("att", 3 * LAYERS)
            b.s_atps = sig("atps", LAYERS)
            b.s_attT = sig("attT", LAYERS)
            b.s_wops = sig("wops", LAYERS)
            b.s_w1ps = sig("w1ps", PAIRS * LAYERS)
            b.s_h = sig("h", PAIRS * LAYERS)
            b.s_w2ps = sig("w2ps", LAYERS)
            b.s_in = sig("in", 1)
            b.s_mod = sig("mod", 2)
            b.s_route = sig("route", ROUTE_STEPS)
            b.s_eps = sig("eps", len(EXPERT_PS))
            b.s_eact = sig("eact", len(EXPERT_ACT))
            b.s_units = sig("units", len(EXPERT_UNITS))
            b.s_out = sig("out", 1)
            chains.append(b)
        AB, CD = chains[:2], chains[2:]
        A, B = AB

        s_k, s_sel, s_par, s_bias, s_lnf, s_wm = sem("k"), sem("sel"), sem("par"), sem("biasin"), sem("lnf"), sem("wm")
        s_xfirst, s_saved = sem("xfirst"), sem("saved")
        s_spread = [sem(f"spread{n}") for n in range(len(SPREAD))]
        s_wqkv, s_w1, s_rest, s_wmoe = sem("wqkv"), sem("w1in"), sem("wrest"), sem("wmoe")
        s_x = sem("xin")
        s_stored = sem("stored")
        s_const = sem("const")
        s_zero = sem("zero")
        s_ones = sem("ones")
        s_parps = sem("parps")
        s_parT = sem("parT")
        s_condT = sem("condT")
        s_modps = sem("modps")
        s_modsb = sem("modsb")
        s_fold = sem("fold")
        s_foldps = sem("foldps")
        s_folded = sem("folded")
        s_high = sem("high")
        s_low = sem("low")
        s_lessmean = sem("lessmean")
        s_w2 = sem("w2")

        block = ctx.enter_context(nc.Block())

        Xv = X[:, :].rearrange("p (n f) -> p n f", f=D)

        def seq_of(b, i):
            return (i % STEPS) * CHAINS + b.c

        def x_tile(b, i, t):
            return X[:, bass.ds(seq_of(b, i) * TILES * D + t * D, D)]

        def x_tiles(b, i):
            return X[:, bass.ds(seq_of(b, i) * TILES * D, TILES * D)].rearrange("p (t f) -> p t f", f=D)

        def mod_row(b, i, k):
            r = M[:, bass.ds(seq_of(b, i), 1), k * D:(k + 1) * D]
            return r.to_broadcast([P, TILES, D])

        def phase(n):
            first, second = (AB, CD) if n % 2 == 0 else (CD, AB)
            return first, n // 2, second, (n - 1) // 2

        @block.sync
        def _(sync):
            sync.dma_start(c_in[:, :], cond).then_inc(s_k, 16)
            sync.dma_start(K[:, :], consts).then_inc(s_k, 16)
            sync.dma_start(wm[:, :], wmod).then_inc(s_wm, 16)
            for n, a in enumerate((lnf_s, lnf_b)):
                sync.dma_start(lnf[:, n * D:(n + 1) * D],
                               a.rearrange("(a n) -> a n", a=1).to_broadcast([BATCH, D])).then_inc(s_lnf, 16)
            sync.dma_start(sel[:, :], select).then_inc(s_sel, 16)
            sync.wait_ge(s_zero, 1)
            for n, a in enumerate((bq, bk, bv)):
                sync.dma_start(bias[P - 1:P, :, n * D:(n + 1) * D],
                               a.rearrange("(a l) n -> a l n", a=1)).then_inc(s_bias, 16)
            sync.dma_start(bias[P - 1:P, :, QKV:], b1.rearrange("(a l) n -> a l n", a=1)).then_inc(s_bias, 16)
            sync.wait_ge(s_modsb, MOD_STEPS)
            sync.dma_start(rows, modp[:, :]).then_inc(s_saved, 16)
            sync.wait_ge(s_saved, 16)
            tiles_in = x_in.rearrange("b (t p) f -> p (b t) f", p=P)
            k = CHAINS * TILES
            first = 0
            for n, spread in zip(SPREAD, s_spread):
                if spread is s_spread[-1]:
                    sync.dma_start(Xv[:, k:, :], tiles_in[:, k:, :]).then_inc(s_x, 16)
                    sync.wait_ge(s_low, 2 * LAYERS)
                sync.dma_start(M[:, first:first + n, :], rows[first:first + n, :].rearrange("(a s) n -> a s n", a=1)
                               .to_broadcast([P, n, MOD])).then_inc(spread, 16)
                first += n
            out_tiles = out.rearrange("b (t p) f -> b p t f", p=P)
            with sync.Fori(0, STEPS) as i:
                for b in chains:
                    sync.wait_ge(b.s_out.sem, b.s_out.value(i, 1))
                    sync.dma_start(out_tiles[bass.ds(seq_of(b, i), 1), :, :, :].rearrange("a p t f -> p (a t) f"),
                                   x_tiles(b, i)).then_inc(s_stored, 16)
            sync.wait_ge(s_stored, 16 * STEPS * CHAINS)

        @block.scalar
        def _(act):
            act.dma_start(Xv[:, 0:CHAINS * TILES, :], x_in.rearrange("b (t p) f -> p (b t) f", p=P)[:, 0:CHAINS * TILES, :])\
                .then_inc(s_xfirst, 16)
            for n, a in enumerate((Wq, Wk, Wv)):
                act.dma_start(wqkv[:, :, n * D:(n + 1) * D], a.rearrange("l k n -> k l n")).then_inc(s_wqkv, 16)
            act.dma_start(w1[:, :, :], W1.rearrange("l k n -> k l n")).then_inc(s_w1, 16)

            act.wait_ge(s_parps, 1)
            act.activation(condT[:, :], A.ps[:, 0, 0:BATCH], ACT.Silu).then_inc(s_condT, 1)

            def less_w2_means(first, end):
                for l in range(first, end):
                    unused = flat(chains[l].eqk[:, :, :])
                    for c in range(CH):
                        k = l * CH + c
                        last = act.activation(unused[:, c * D:(c + 1) * D], w2[:, l, c, :], ACT.Copy, scale=-1.0 / D,
                                              accum_out=rowsum[:, k:k + 1])
                    last.then_inc(s_w2, 1)
                    act.wait_ge(s_w2, 2 * l + 1)
                    for c in range(CH):
                        k = l * CH + c
                        last = act.activation(w2[:, l, c, :], w2[:, l, c, :], ACT.Identity, bias=rowsum[:, k:k + 1])
                    last.then_inc(s_w2, 1)

            def high(first, end):
                for n in range(first, end):
                    l, k = n // 2, n % 2
                    act.wait_ge(s_folded, n + 1)
                    act.activation((wqkv_hi, w1_hi)[k][:, l, :], (wqkv, w1)[k][:, l, :], ACT.Copy).then_inc(s_high, 1)

            def transposed(b, i, n):
                act.wait_ge(b.s_tps.sem, b.s_tps.value(i, n + 1))
                act.activation(b.x_hi[:, :], b.ps[:, n % 2, 0:T], ACT.Copy).then_inc(b.s_xT.sem, 1)

            def centre(b, i):
                act.wait_ge(b.s_moved.sem, b.s_moved.value(i, 1))
                for t in range(TILES):
                    last = act.activation(b.zi[:, t, :], b.x[:, t, :], ACT.Copy, scale=-1.0 / D,
                                          accum_out=b.negmean[:, t:t + 1])
                last.then_inc(b.s_centred.sem, 1)
                act.wait_ge(b.s_centred.sem, b.s_centred.value(i, 1))
                for t in range(TILES):
                    last = act.activation(b.x[:, t, :], b.x[:, t, :], ACT.Identity, bias=b.negmean[:, t:t + 1])
                last.then_inc(b.s_centred.sem, 1)

            def squares(b, i, n):
                if n == 1:
                    act.wait_ge(b.s_centred.sem, b.s_centred.value(i, 2))
                else:
                    act.wait_ge(b.s_moved.sem, b.s_moved.value(i, n))
                for t in range(TILES):
                    unused = b.zi[:, t, :] if n == 1 else b.eq[:, t * P:(t + 1) * P]
                    last = act.activation(unused, b.x[:, t, :], ACT.Square, scale=float(D) ** -0.5,
                                          accum_out=b.ms[:, t:t + 1])
                last.then_inc(b.s_squares.sem, 1)

            def key_exps(b, i, l):
                act.wait_ge(b.s_qkvps.sem, b.s_qkvps.value(i, 2 * l + 1))
                both = b.ps[:, 1, :].rearrange("p (t n) -> p t n", n=2 * D)
                act.activation(b.ek, both[:, :, 0:D], ACT.Exp, bias=-1.0)
                act.activation(b.v[:, :, 0:D], both[:, :, D:], ACT.Copy).then_inc(b.s_v.sem, 1)

            def query_exps(b, i, l):
                act.wait_ge(b.s_qkvps.sem, b.s_qkvps.value(i, 2 * l + 2))
                act.activation(b.eq, b.ps[:, 0, 0:T], ACT.Exp, bias=-1.0).then_inc(b.s_eq.sem, 1)

            def att_transposed(b, i, l):
                act.wait_ge(b.s_atps.sem, b.s_atps.value(i, l + 1))
                act.activation(b.attT, b.ps[:, 1, 0:T], ACT.Copy).then_inc(b.s_attT.sem, 1)

            def relu(b, i, l, k):
                act.wait_ge(b.s_w1ps.sem, b.s_w1ps.value(i, l * PAIRS + k + 1))
                act.activation(b.h[:, 2 * k:2 * k + 2, :], b.ps[:, k, :].rearrange("p (c t) -> p c t", t=T),
                               ACT.Relu).then_inc(b.s_h.sem, 1)

            def router_exp(b, i):
                act.wait_ge(b.s_route.sem, b.s_route.value(i, 3))
                act.activation(b.ex[:, :, :], b.ls[:, :, :], ACT.Exp).then_inc(b.s_eact.sem, 1)

            def coefs(b, i):
                act.wait_ge(b.s_eps.sem, b.s_eps.of(EXPERT_PS, "coefT", i))
                act.activation(b.coefT[:, :], b.ps[0:S_ROWS, 1, 0:T], ACT.Copy)\
                    .then_inc(b.s_eact.sem, 1)

            def silu(b, i, k):
                act.wait_ge(b.s_eps.sem, b.s_eps.of(EXPERT_PS, f"gate{k}", i))
                if k > 0:
                    act.wait_ge(b.s_units.sem, b.s_units.of(EXPERT_UNITS, f"product{k - 1}", i))
                width = 2 * T if k < PAIRS else T
                act.activation(b.eqk[:, :, :].rearrange("p a t -> p (a t)")[:, 0:width], b.ps[:, k % 2, 0:width],
                               ACT.Silu).then_inc(b.s_eact.sem, 1)

            a, _, f, _ = phase(0)
            act.wait_ge(s_rest, 64)
            less_w2_means(0, 1)
            high(0, 1)
            less_w2_means(1, 2)
            high(1, 2)
            centre(a[0], 0)
            squares(a[0], 0, 1)
            centre(a[1], 0)
            squares(a[1], 0, 1)
            transposed(a[0], 0, 0)
            transposed(a[1], 0, 0)
            high(2, 5)
            key_exps(a[0], 0, 0)
            query_exps(a[0], 0, 0)
            key_exps(a[1], 0, 0)
            query_exps(a[1], 0, 0)
            high(5, 2 * LAYERS)
            less_w2_means(2, 3)
            att_transposed(a[0], 0, 0)
            att_transposed(a[1], 0, 0)
            centre(f[0], 0)
            squares(f[0], 0, 1)
            squares(a[0], 0, 2)
            centre(f[1], 0)
            squares(f[1], 0, 1)
            squares(a[1], 0, 2)
            less_w2_means(3, 4)
            with act.Fori(0, STEPS) as i:
                for n in range(1, PHASES):
                    a, l, f, m = phase(n)
                    if n == 1:
                        transposed(a[1], i, 0)
                        transposed(f[0], i, 1)
                        transposed(a[0], i, 0)
                        transposed(f[1], i, 1)
                        key_exps(a[1], i, 0)
                        key_exps(a[0], i, 0)
                        query_exps(a[0], i, 0)
                        query_exps(a[1], i, 0)
                        relu(f[0], i, 0, 0)
                        relu(f[0], i, 0, 1)
                        relu(f[1], i, m, 0)
                        relu(f[1], i, m, 1)
                        att_transposed(a[0], i, l)
                        squares(f[0], i, 2 * m + 3)
                        squares(a[0], i, 2 * l + 2)
                        att_transposed(a[1], i, l)
                        transposed(f[0], i, 2 * m + 2)
                    elif n < PHASES - 3:
                        squares(a[1], i, 2 * l + 1)
                        transposed(f[0], i, 2 * m + 1)
                        key_exps(a[0], i, l)
                        squares(f[1], i, 2 * m + 2)
                        transposed(a[1], i, 2 * l)
                        relu(f[0], i, m, 0)
                        query_exps(a[0], i, l)
                        relu(f[0], i, m, 1)
                        key_exps(a[1], i, l)
                        query_exps(a[1], i, l)
                        transposed(f[1], i, 2 * m + 1)
                        squares(f[0], i, 2 * m + 3)
                        att_transposed(a[0], i, l)
                        relu(f[1], i, m, 0)
                        relu(f[1], i, m, 1)
                        squares(a[0], i, 2 * l + 2)
                        att_transposed(a[1], i, l)
                        transposed(f[0], i, 2 * m + 2)
                    elif l < LAYERS:
                        transposed(f[0], i, 2 * m + 1)
                        squares(a[1], i, 2 * l + 1)
                        key_exps(a[0], i, l)
                        relu(f[0], i, m, 0)
                    elif m < LAYERS:
                        relu(a[0], i, l - 1, 1)
                        squares(a[1], i, 2 * l)
                        query_exps(f[0], i, m)
                        transposed(f[1], i, 2 * m)
                        transposed(a[1], i, 2 * l - 1)
                        squares(a[0], i, 2 * l + 1)
                        key_exps(f[1], i, m)
                        query_exps(f[1], i, m)
                        att_transposed(f[0], i, m)
                        relu(a[1], i, l - 1, 0)
                        relu(a[1], i, l - 1, 1)
                        squares(f[0], i, 2 * m + 2)
                        squares(a[1], i, 2 * l + 1)
                        att_transposed(f[1], i, m)
                    else:
                        transposed(a[0], i, 2 * l - 1)
                        squares(a[1], i, 2 * l)
                        transposed(a[1], i, 2 * l - 1)
                        relu(a[1], i, l - 1, 0)
                        relu(a[1], i, l - 1, 1)
                        router_exp(f[0], i)
                        router_exp(f[1], i)
                        silu(f[0], i, 0)
                        relu(a[0], i, l - 1, 0)
                        relu(a[0], i, l - 1, 1)
                        silu(f[1], i, 0)
                        squares(a[1], i, LAST)
                        coefs(f[1], i)
                        coefs(f[0], i)
                        silu(f[1], i, 1)
                        squares(a[0], i, LAST)
                        silu(f[0], i, 1)
                        silu(f[1], i, 2)
                        centre(f[0], i + 1)
                        squares(f[0], i + 1, 1)
                        silu(f[0], i, 2)
                        centre(f[1], i + 1)
                        squares(f[1], i + 1, 1)
                        transposed(f[1], i + 1, 0)
                        transposed(f[0], i + 1, 0)
                        key_exps(f[1], i + 1, 0)
                        router_exp(a[0], i)
                        router_exp(a[1], i)
                        silu(a[1], i, 0)
                        silu(a[0], i, 0)
                        query_exps(f[1], i + 1, 0)
                        coefs(a[1], i)
                        key_exps(f[0], i + 1, 0)
                        query_exps(f[0], i + 1, 0)
                        coefs(a[0], i)
                        silu(a[1], i, 1)
                        silu(a[0], i, 1)
                        att_transposed(f[0], i + 1, 0)
                        att_transposed(f[1], i + 1, 0)
                        silu(a[1], i, 2)
                        centre(a[1], i + 1)
                        squares(a[1], i + 1, 1)
                        silu(a[0], i, 2)
                        squares(f[1], i + 1, 2)
                        squares(f[0], i + 1, 2)
                        centre(a[0], i + 1)
                        squares(a[0], i + 1, 1)

        @block.gpsimd
        def _(pool):
            for n, a in enumerate((ln1_s, ln1_b, ln2_s, ln2_b)):
                pool.dma_start(par[n * LAYERS:(n + 1) * LAYERS, :], a).then_inc(s_par, 16)
            pool.memset(neghalf[:, :], -0.5).then_inc(s_const, 1)
            pool.memset(epsilon[:, :], EPS).then_inc(s_const, 1)
            for b in chains:
                pool.memset(b.xn[:, :, D - 1:D], 1.0).then_inc(s_const, 1)
                pool.memset(b.v[:, :, D:], 1.0).then_inc(s_const, 1)
            pool.dma_start(wo[:, :, :], Wo.rearrange("l k n -> k l n")).then_inc(s_rest, 16)
            pool.dma_start(w2[:, :, :, :].rearrange("p l c n -> p (l c) n"),
                           W2.rearrange("l (c p) n -> p (l c) n", p=P)).then_inc(s_rest, 16)
            for w, a in ((bo_all, bo), (b2_all, b2)):
                pool.dma_start(w[:, :, :].rearrange("p l n -> p (l n)"),
                               a.rearrange("(a l) n -> a (l n)", a=1).to_broadcast([P, LAYERS * D])).then_inc(s_rest, 16)
            pool.wait_ge(s_const, 10)

            def moe_weights():
                pool.dma_start(wr[:, :], router).then_inc(s_wmoe, 16)
                for w, e, s in ((wg, e_gate, s_gate), (wu, e_up, s_up)):
                    pool.dma_start(w[:, 0:CH, :].rearrange("p c (e d) -> p (c e) d", d=DE),
                                   e.rearrange("e h d -> h e d")).then_inc(s_wmoe, 16)
                    pool.dma_start(w[:, CH, :], s).then_inc(s_wmoe, 16)
                pool.dma_start(wd[:, 0:CH, :], e_down.rearrange("(c e) d n -> (e d) c n", e=2)).then_inc(s_wmoe, 16)
                pool.dma_start(wd[:, CH, :], s_down).then_inc(s_wmoe, 16)

            def low(first, end):
                for n in range(first, end):
                    l, k = n // 2, n % 2
                    pool.wait_ge(s_high, n + 1)
                    pool.tensor_tensor((wqkv_lo, w1_lo)[k][:, l, :], (wqkv, w1)[k][:, l, :],
                                       (wqkv_hi, w1_hi)[k][:, l, :], ALU.subtract).then_inc(s_low, 1)

            def rstd(b, i, n):
                if 0 < n <= LAST:
                    pool.wait_ge(b.s_squares.sem, b.s_squares.value(i, n))
                    var = b.ms[:, :]
                else:
                    pool.wait_ge(b.s_moments.sem, b.s_moments.value(i, 1 if n == 0 else 2))
                    var = b.mv[:, :, 1]
                pool.tensor_tensor(b.ve[:, :], var, epsilon[:, :], ALU.add).then_inc(b.s_rstd.sem, 1)
                pool.wait_ge(b.s_rstd.sem, b.s_rstd.value(i, 2 * n + 1))
                pool.tensor_tensor(b.rstd[:, :], b.ve[:, :], neghalf[:, :], ALU.pow).then_inc(b.s_rstd.sem, 1)

            def add_bias(b, i, n):
                l, k = (n - 1) // 2, (n - 1) % 2
                w = (bo_all, b2_all)[k]
                pool.wait_ge(b.s_normed.sem, b.s_normed.value(i, n + 1))
                pool.tensor_tensor(b.x[:, :, :], b.x[:, :, :], w[:, l:l + 1, :].to_broadcast([P, TILES, D]), ALU.add)\
                    .then_inc(b.s_biased.sem, 1)

            def shift_in(b, i):
                pool.tensor_tensor(b.x[:, :, :], mod_row(b, i, 1), pos, ALU.add).then_inc(b.s_biased.sem, 1)

            def shift_out(b, i):
                pool.tensor_tensor(b.zi[:, :, :], mod_row(b, i, 3), x_tiles(b, i), ALU.add).then_inc(b.s_biased.sem, 1)

            a, _, f, _ = phase(0)
            rstd(a[0], 0, 0)
            rstd(a[1], 0, 0)
            rstd(f[0], 0, 0)
            rstd(f[1], 0, 0)
            pool.wait_ge(s_k, 32)
            pool.wait_ge(s_spread[0], 16)
            shift_in(a[0], 0)
            shift_in(a[1], 0)
            low(0, 1)
            rstd(a[0], 0, 1)
            rstd(a[1], 0, 1)
            low(1, 2)
            pool.wait_ge(s_spread[1], 16)
            pool.wait_ge(s_xfirst, 16)
            shift_in(f[0], 0)
            shift_in(f[1], 0)
            low(2, 3)
            pool.wait_ge(s_lessmean, 6)
            add_bias(a[0], 0, 1)
            add_bias(a[1], 0, 1)
            low(3, 5)
            rstd(f[0], 0, 1)
            rstd(a[0], 0, 2)
            rstd(f[1], 0, 1)
            rstd(a[1], 0, 2)
            low(5, 2 * LAYERS)
            moe_weights()
            with pool.Fori(0, STEPS) as i:
                for n in range(1, PHASES):
                    a, l, f, m = phase(n)
                    if n == 1:
                        pool.wait_ge(s_lessmean, 9)
                        add_bias(a[0], i, 2 * l + 1)
                        add_bias(f[1], i, 2 * m + 2)
                    elif n < PHASES - 3:
                        add_bias(a[0], i, 2 * l)
                        add_bias(f[1], i, 2 * m + 1)
                        rstd(a[0], i, 2 * l + 1)
                        rstd(f[0], i, 2 * m + 2)
                        rstd(a[1], i, 2 * l + 1)
                        rstd(f[1], i, 2 * m + 2)
                        add_bias(f[1], i, 2 * m + 2)
                        add_bias(a[0], i, 2 * l + 1)
                    elif l < LAYERS:
                        pool.wait_ge(s_spread[2], 16)
                        pool.wait_ge(s_spread[3], 16)
                        pool.wait_ge(s_x, 16)
                        add_bias(a[0], i, 2 * l)
                        rstd(a[0], i, 2 * l + 1)
                        add_bias(f[1], i, 2 * m + 1)
                        rstd(f[0], i, 2 * m + 2)
                        rstd(a[1], i, 2 * l + 1)
                        add_bias(a[0], i, 2 * l + 1)
                        add_bias(f[0], i, 2 * m + 2)
                        rstd(f[1], i, 2 * m + 2)
                        add_bias(a[1], i, 2 * l + 1)
                    elif m < LAYERS:
                        rstd(a[0], i, 2 * l + 1)
                        shift_out(a[0], i)
                        rstd(a[0], i, LAST + 1)
                        add_bias(a[1], i, 2 * l)
                        rstd(f[0], i, 2 * m + 2)
                        rstd(a[1], i, 2 * l + 1)
                        shift_out(a[1], i)
                        rstd(a[0], i + 1, 0)
                        rstd(f[1], i, 2 * m + 2)
                        rstd(a[1], i, LAST + 1)
                    else:
                        shift_in(f[0], i + 1)
                        rstd(f[1], i + 1, 0)
                        add_bias(a[1], i, 2 * l)
                        add_bias(a[0], i, 2 * l)
                        rstd(a[1], i, LAST)
                        shift_out(a[1], i)
                        rstd(a[0], i, LAST)
                        shift_out(a[0], i)
                        rstd(a[1], i, LAST + 1)
                        shift_in(f[1], i + 1)
                        shift_in(a[1], i + 1)
                        rstd(a[0], i, LAST + 1)
                        rstd(f[1], i + 1, 1)
                        rstd(f[0], i + 1, 1)
                        rstd(a[0], i + 1, 0)
                        add_bias(f[0], i + 1, 1)
                        shift_in(a[0], i + 1)
                        rstd(a[1], i + 1, 0)
                        add_bias(f[1], i + 1, 1)
                        rstd(f[1], i + 1, 2)
                        rstd(a[1], i + 1, 1)
                        rstd(f[0], i + 1, 2)
                        rstd(a[0], i + 1, 1)

        @block.vector
        def _(dve):
            dve.memset(bias[:, :, :], 0.0).then_inc(s_zero, 1)

            def fold_matrices():
                dve.wait_ge(s_parps, 2)
                dve.tensor_copy(parT[:, :], B.ps[:, 1, 0:4 * LAYERS]).then_inc(s_parT, 1)
                dve.wait_ge(s_parT, 1)
                for n in range(2 * LAYERS):
                    l, k = n // 2, n % 2
                    sc = parT[:, 2 * k * LAYERS + l:2 * k * LAYERS + l + 1]
                    sh = parT[:, (2 * k + 1) * LAYERS + l:(2 * k + 1) * LAYERS + l + 1]
                    dve.tensor_scalar(fold[:, n, 0:P - 1], base[:, 0:P - 1], sc, None, ALU.mult)
                    dve.tensor_copy(fold[:, n, P - 1:P], sh).then_inc(s_fold, 1)

            steps = [0]

            def done(ins):
                ins.then_inc(s_modsb, 1)
                steps[0] += 1
                dve.wait_ge(s_modsb, steps[0])

            def modulation():
                dve.wait_ge(s_modps, 1)
                done(dve.tensor_copy(mod[:, :], A.ps[0:BATCH, :, :].rearrange("p k n -> p (k n)")[:, 0:6 * D]))
                dve.tensor_copy(shiftT[:, :], B.ps[:, 0, 0:BATCH])
                done(dve.tensor_scalar(scaleT[:, :], B.ps[:, 0, BATCH:2 * BATCH], 1.0, None, ALU.add))
                root = float(D) ** 0.5
                dve.tensor_scalar(modp[:, 0:D], mod[:, D:2 * D], 1.0, root, ALU.add, ALU.mult)
                done(dve.tensor_scalar(modp[:, D:2 * D], mod[:, 0:D], root, None, ALU.mult))
                g = mod[:, :].rearrange("b (k n) -> b k n", n=3 * D)[:, :, 2 * D:]
                s = sgn[:, :].rearrange("b (k n) -> b k n", n=D)
                done(dve.tensor_scalar(s, g, 0.0, 2.0, ALU.is_ge, ALU.mult))
                done(dve.tensor_scalar(s, s, -1.0, None, ALU.add))
                done(dve.tensor_tensor(g, g, s, ALU.mult))
                done(dve.scalar_tensor_tensor(s, g, 0.25, s, ALU.max, ALU.mult))
                dve.wait_ge(s_lnf, 32)
                dve.tensor_tensor(modp[:, 2 * D:3 * D], sgn[:, 0:D], lnf[:, 0:D], ALU.mult)
                dve.tensor_tensor(modp[:, 3 * D:4 * D], sgn[:, 0:D], lnf[:, D:2 * D], ALU.mult)
                done(dve.tensor_copy(modp[:, 4 * D:5 * D], sgn[:, D:2 * D]))
                assert steps[0] == MOD_STEPS

            def spreading_ones():
                dve.wait_ge(s_sel, 16)
                dve.tensor_copy(sel_hi[:, :], sel[:, :]).then_inc(s_ones, 1)

            def less_means(weights, n):
                for w in weights:
                    mean = rowmean[:, 0:w.shape[1]]
                    if n > 0:
                        dve.wait_ge(s_lessmean, n)
                    dve.tensor_reduce(mean, w, AXX, ALU.add).then_inc(s_lessmean, 1)
                    dve.wait_ge(s_lessmean, n + 1)
                    dve.tensor_scalar(mean, mean, 1.0 / D, None, ALU.mult).then_inc(s_lessmean, 1)
                    dve.wait_ge(s_lessmean, n + 2)
                    dve.tensor_tensor(w, w, mean.unsqueeze(2).to_broadcast(list(w.shape)), ALU.subtract)\
                        .then_inc(s_lessmean, 1)
                    n += 3

            def folded(first, end):
                if first == 0:
                    dve.wait_ge(s_bias, 64)
                    dve.tensor_scalar(bias[:, :, 0:2 * D], bias[:, :, 0:2 * D], ident[:, P - 1:P], None, ALU.add)\
                        .then_inc(s_parT, 1)
                    dve.wait_ge(s_parT, 2)
                for n in range(first, end):
                    l, k = n // 2, n % 2
                    w, part = (wqkv[:, l, :], bias[:, l, 0:QKV]) if k == 0 else (w1[:, l, :], bias[:, l, QKV:])
                    dve.wait_ge(s_foldps, n + 1)
                    dve.tensor_tensor(w, chains[2 + k].ps[:, l % 2, 0:w.shape[-1]], part, ALU.add).then_inc(s_folded, 1)

            def source(b, i, n):
                if n == 0:
                    return lambda t: x_tile(b, i, t)
                return (lambda t: b.y[:, t, :]) if n == LAST + 1 else (lambda t: b.x[:, t, :])

            def stats(b, i, n):
                src = source(b, i, n)
                if n > 0:
                    dve.wait_ge(b.s_moved.sem, b.s_moved.value(i, n))
                for t in range(TILES):
                    dve.bn_stats(b.stat[:, t, :], src(t))
                dve.drain()
                for t in range(TILES):
                    last = dve.bn_aggr(b.mv[:, t, :], b.stat[:, t, :])
                last.then_inc(b.s_moments.sem, 1)

            def scale(b, i, n):
                dve.wait_ge(b.s_rstd.sem, b.s_rstd.value(i, 2 * n + 2))
                if 0 < n <= LAST:
                    dst, width = (b.xn, D - 1) if n < LAST else (b.z, D)
                    dve.tensor_tensor(dst[:, :, 0:width], b.x[:, :, 0:width],
                                      b.rstd[:, :].unsqueeze(2).to_broadcast([P, TILES, width]), ALU.mult)\
                        .then_inc(b.s_normed.sem, 1)
                    return
                src, dst = source(b, i, n), b.zi if n == 0 else b.z
                for t in range(TILES):
                    last = dve.tensor_scalar(dst[:, t, :], src(t), b.mv[:, t, 0:1], b.rstd[:, t:t + 1],
                                             ALU.subtract, ALU.mult)
                last.then_inc(b.s_normed.sem, 1)

            def enter(b, i, k):
                if k == 0:
                    dve.wait_ge(b.s_normed.sem, b.s_normed.value(i, 1))
                    dve.tensor_tensor(b.zi[:, :, :], b.zi[:, :, :], mod_row(b, i, 0), ALU.mult).then_inc(b.s_in.sem, 1)
                else:
                    dve.wait_ge(b.s_in.sem, b.s_in.value(i, 1))
                    dve.wait_ge(b.s_biased.sem, b.s_biased.value(i, 1))
                    dve.tensor_tensor(b.x[:, :, :], b.zi[:, :, :], b.x[:, :, :], ALU.add).then_inc(b.s_moved.sem, 1)

            def low_part(b, i, n):
                dve.wait_ge(b.s_xT.sem, b.s_xT.value(i, n + 1))
                dve.tensor_tensor(b.x_lo[:, :], b.ps[:, n % 2, 0:T], b.x_hi[:, :], ALU.subtract)\
                    .then_inc(b.s_x_lo.sem, 1)

            def positive_keys(b, i, l):
                dve.wait_ge(b.s_v.sem, b.s_v.value(i, l + 1))
                keys = b.ps[:, 1, :].rearrange("p (t n) -> p t n", n=2 * D)[:, :, 0:D]
                dve.scalar_tensor_tensor(b.kp[:, :, :], b.ek, 1.0, keys, ALU.min, ALU.max).then_inc(b.s_pos.sem, 1)

            def positive_queries(b, i, l):
                dve.wait_ge(b.s_eq.sem, b.s_eq.value(i, l + 1))
                dve.scalar_tensor_tensor(b.qp[:, :], b.eq, 1.0, b.ps[:, 0, 0:T], ALU.min, ALU.max)\
                    .then_inc(b.s_pos.sem, 1)

            def masked(b, i, l):
                dve.wait_ge(b.s_sumps.sem, b.s_sumps.value(i, l + 1))
                dve.tensor_tensor(b.kv[:, :], b.ps[:, 1, 0:VW], headmask, ALU.mult).then_inc(b.s_kv.sem, 1)

            def divided(b, i, l):
                both = b.ps[:, 0, :].rearrange("p (t n) -> p t n", n=2 * D)
                dve.wait_ge(b.s_attps.sem, b.s_attps.value(i, l + 1))
                dve.tensor_scalar(b.den[:, :, :], both[:, :, D:VW], EPS_ATTN, None, ALU.add).then_inc(b.s_att.sem, 1)
                dve.wait_ge(b.s_att.sem, b.s_att.value(i, 3 * l + 1))
                dve.reciprocal(b.rden[:, :, :], b.den[:, :, :]).then_inc(b.s_att.sem, 1)
                dve.wait_ge(b.s_att.sem, b.s_att.value(i, 3 * l + 2))
                dve.tensor_tensor(b.att[:, :, :].rearrange("p t (h k) -> p t h k", k=DK),
                                  both[:, :, 0:D].rearrange("p t (h k) -> p t h k", k=DK),
                                  b.rden[:, :, :].unsqueeze(3).to_broadcast([P, TILES, HEADS, DK]), ALU.mult)\
                    .then_inc(b.s_att.sem, 1)

            def move(b, i, n):
                ps = (b.s_wops, b.s_w2ps)[(n - 1) % 2]
                dve.wait_ge(ps.sem, ps.value(i, (n - 1) // 2 + 1))
                dve.wait_ge(b.s_biased.sem, b.s_biased.value(i, n + 1))
                dve.tensor_tensor(b.x[:, :, :], b.ps[:, 0, 0:T].rearrange("p (t f) -> p t f", f=D), b.x[:, :, :],
                                  ALU.add).then_inc(b.s_moved.sem, 1)

            def leave(b, i, k):
                if k == 0:
                    dve.wait_ge(b.s_normed.sem, b.s_normed.value(i, LAST + 1))
                    dve.tensor_tensor(b.z[:, :, :], b.z[:, :, :], mod_row(b, i, 2), ALU.mult).then_inc(b.s_mod.sem, 1)
                else:
                    dve.wait_ge(b.s_mod.sem, b.s_mod.value(i, 1))
                    dve.wait_ge(b.s_biased.sem, b.s_biased.value(i, b.s_biased.per))
                    dve.tensor_tensor(b.y[:, :, :], b.z[:, :, :], b.zi[:, :, :], ALU.add).then_inc(b.s_moved.sem, 1)

            def tokensT(b, i):
                dve.wait_ge(b.s_tps.sem, b.s_tps.value(i, 2 * LAYERS + 1))
                s = seq_of(b, i)
                dve.tensor_scalar(b.xT[:, :], b.ps[:, 0, 0:T], scaleT[:, bass.ds(s, 1)],
                                  shiftT[:, bass.ds(s, 1)], ALU.mult, ALU.add).then_inc(b.s_xT.sem, 1)

            def route(pair, i, part):
                n = [0 if part == 0 else 3]

                def step(op):
                    for b in pair:
                        op(b).then_inc(b.s_route.sem, 1)
                    n[0] += 1

                def then(op):
                    k = n[0]
                    for b in pair:
                        dve.wait_ge(b.s_route.sem, b.s_route.value(i, k))
                        op(b).then_inc(b.s_route.sem, 1)
                    n[0] += 1

                if part == 0:
                    for b in pair:
                        dve.wait_ge(b.s_eps.sem, b.s_eps.of(EXPERT_PS, "logits", i))
                        dve.tensor_copy(b.lg[:, :, :], b.ps[:, 1, 0:TILES * EXPERTS].rearrange(
                            "p (t e) -> p t e", e=EXPERTS)).then_inc(b.s_route.sem, 1)
                    n[0] += 1
                    then(lambda b: dve.tensor_reduce(b.mx[:, :], b.lg[:, :, :], AXX, ALU.max))
                    then(lambda b: dve.tensor_tensor(b.ls[:, :, :], b.lg[:, :, :],
                                                     b.mx[:, :].unsqueeze(2).to_broadcast([P, TILES, EXPERTS]),
                                                     ALU.subtract))
                    return
                four = [P, TILES, EXPERTS, EXPERTS]

                def other(b):
                    return b.lg[:, :, :].unsqueeze(2).to_broadcast(four)

                def mine(b):
                    return b.lg[:, :, :].unsqueeze(3).to_broadcast(four)

                step(lambda b: dve.tensor_tensor(b.tie[:, :, :, :], other(b), mine(b), ALU.is_equal))
                step(lambda b: dve.tensor_tensor(b.gt[:, :, :, :], other(b), mine(b), ALU.is_gt))
                then(lambda b: dve.tensor_tensor(b.tie[:, :, :, :], b.tie[:, :, :, :],
                                                 tri.unsqueeze(1).to_broadcast(four), ALU.mult))
                then(lambda b: dve.tensor_tensor(b.gt[:, :, :, :], b.gt[:, :, :, :], b.tie[:, :, :, :], ALU.add))
                then(lambda b: dve.tensor_reduce(b.rank[:, :, :], b.gt[:, :, :, :], AXX, ALU.add))
                for b in pair:
                    dve.wait_ge(b.s_eact.sem, b.s_eact.of(EXPERT_ACT, "exp", i))
                    dve.tensor_reduce(b.sum[:, :], b.ex[:, :, :], AXX, ALU.add).then_inc(b.s_route.sem, 1)
                n[0] += 1
                then(lambda b: dve.scalar_tensor_tensor(b.coef[:, :, :], b.rank[:, :, :], float(TOP), b.ex[:, :, :],
                                                        ALU.is_lt, ALU.mult))
                step(lambda b: dve.reciprocal(b.rsum[:, :], b.sum[:, :]))
                then(lambda b: dve.tensor_tensor(b.coef[:, :, :], b.coef[:, :, :],
                                                 b.rsum[:, :].unsqueeze(2).to_broadcast([P, TILES, EXPERTS]),
                                                 ALU.mult))
                then(lambda b: dve.tensor_copy(b.parts[:, :, 0, :], b.coef[:, :, :]))
                then(lambda b: dve.tensor_tensor(b.parts[:, :, 1, :], b.coef[:, :, :], b.parts[:, :, 0, :],
                                                 ALU.subtract))
                assert n[0] == ROUTE_STEPS

            def gate_up(b, i, k):
                dve.wait_ge(b.s_eact.sem, b.s_eact.of(EXPERT_ACT, f"silu{k}", i))
                dve.wait_ge(b.s_eps.sem, b.s_eps.of(EXPERT_PS, f"up{k}", i))
                if k < PAIRS:
                    if k > 0:
                        dve.wait_ge(b.s_units.sem, b.s_units.of(EXPERT_UNITS, f"weighed{k - 1}", i))
                    dve.tensor_tensor(flat(b.gu[:, :, :]), flat(b.eqk[:, :, :]), b.ps[:, 1 - k % 2, :], ALU.mult)\
                        .then_inc(b.s_units.sem, 1)
                else:
                    dve.tensor_tensor(b.hs[:, :], b.eqk[:, 0, :], b.ps[:, 1 - k % 2, 0:T], ALU.mult)\
                        .then_inc(b.s_units.sem, 1)

            def weigh(b, i, k):
                dve.wait_ge(b.s_units.sem, b.s_units.of(EXPERT_UNITS, f"product{k}", i))
                dve.wait_ge(b.s_eps.sem, b.s_eps.of(EXPERT_PS, f"spread{k}", i))
                dve.tensor_tensor(flat(b.h[:, 2 * k:2 * k + 2, :]), flat(b.gu[:, :, :]), b.ps[:, k % 2, :], ALU.mult)\
                    .then_inc(b.s_units.sem, 1)

            def finish(b, i, k):
                if k == 0:
                    dve.wait_ge(b.s_eps.sem, b.s_eps.of(EXPERT_PS, "down", i))
                    dve.tensor_tensor(b.z[:, :, :], b.ps[:, 0, 0:T].rearrange("p (t f) -> p t f", f=D),
                                      mod_row(b, i, 4), ALU.mult).then_inc(b.s_mod.sem, 1)
                else:
                    dve.wait_ge(b.s_mod.sem, b.s_mod.value(i, 2))
                    dve.tensor_tensor(x_tiles(b, i), b.z[:, :, :], b.y[:, :, :], ALU.add).then_inc(b.s_out.sem, 1)

            a, _, f, _ = phase(0)
            dve.wait_ge(s_xfirst, 16)
            stats(a[0], 0, 0)
            stats(a[1], 0, 0)
            stats(f[0], 0, 0)
            stats(f[1], 0, 0)
            modulation()
            fold_matrices()
            dve.wait_ge(s_const, 10)
            scale(a[0], 0, 0)
            scale(a[1], 0, 0)
            folded(0, 4)
            scale(f[0], 0, 0)
            scale(f[1], 0, 0)
            dve.wait_ge(s_spread[0], 16)
            enter(a[0], 0, 0)
            enter(a[1], 0, 0)
            enter(a[0], 0, 1)
            enter(a[1], 0, 1)
            folded(4, 2 * LAYERS)
            scale(a[0], 0, 1)
            scale(a[1], 0, 1)
            low_part(a[0], 0, 0)
            low_part(a[1], 0, 0)
            dve.wait_ge(s_rest, 64)
            less_means((wo[:, :, :],), 0)
            positive_keys(a[0], 0, 0)
            positive_queries(a[0], 0, 0)
            less_means((bo_all[:, :, :],), 3)
            positive_keys(a[1], 0, 0)
            positive_queries(a[1], 0, 0)
            masked(a[0], 0, 0)
            masked(a[1], 0, 0)
            dve.wait_ge(s_spread[1], 16)
            enter(f[0], 0, 0)
            enter(f[1], 0, 0)
            divided(a[0], 0, 0)
            enter(f[0], 0, 1)
            divided(a[1], 0, 0)
            enter(f[1], 0, 1)
            less_means((b2_all[:, :, :],), 6)
            move(a[0], 0, 1)
            move(a[1], 0, 1)
            scale(f[0], 0, 1)
            scale(f[1], 0, 1)
            scale(a[0], 0, 2)
            scale(a[1], 0, 2)
            spreading_ones()
            with dve.Fori(0, STEPS) as i:
                for n in range(1, PHASES):
                    a, l, f, m = phase(n)
                    if n == 1:
                        low_part(a[1], i, 0)
                        low_part(a[0], i, 0)
                        low_part(f[0], i, 1)
                        low_part(f[1], i, 1)
                        positive_keys(a[0], i, 0)
                        positive_queries(a[0], i, 0)
                        masked(a[0], i, 0)
                        divided(a[0], i, l)
                        positive_keys(a[1], i, l)
                        move(f[0], i, 2 * m + 2)
                        positive_queries(a[1], i, l)
                    elif n < PHASES - 3:
                        masked(f[1], i, m)
                        move(f[0], i, 2 * m + 1)
                        divided(f[1], i, m)
                        scale(a[0], i, 2 * l + 1)
                        scale(f[0], i, 2 * m + 2)
                        move(a[1], i, 2 * l)
                        low_part(a[0], i, 2 * l)
                        low_part(f[0], i, 2 * m + 1)
                        move(f[1], i, 2 * m + 1)
                        scale(a[1], i, 2 * l + 1)
                        positive_keys(a[0], i, l)
                        low_part(a[1], i, 2 * l)
                        scale(f[1], i, 2 * m + 2)
                        positive_queries(a[0], i, l)
                        masked(a[0], i, l)
                        positive_keys(a[1], i, l)
                        divided(a[0], i, l)
                        low_part(f[1], i, 2 * m + 1)
                        positive_queries(a[1], i, l)
                        move(f[0], i, 2 * m + 2)
                    elif l < LAYERS:
                        dve.wait_ge(s_spread[2], 16)
                        dve.wait_ge(s_spread[3], 16)
                        dve.wait_ge(s_x, 16)
                        masked(f[1], i, m)
                        move(f[0], i, 2 * m + 1)
                        divided(f[1], i, m)
                        scale(a[0], i, 2 * l + 1)
                        scale(f[0], i, 2 * m + 2)
                        move(a[1], i, 2 * l)
                        low_part(a[0], i, 2 * l)
                        low_part(f[0], i, 2 * m + 1)
                        move(f[1], i, 2 * m + 1)
                        positive_keys(a[0], i, l)
                        scale(a[1], i, 2 * l + 1)
                        positive_queries(a[0], i, l)
                        scale(f[1], i, 2 * m + 2)
                        masked(a[0], i, l)
                        low_part(a[1], i, 2 * l)
                        move(f[0], i, 2 * m + 2)
                        low_part(f[1], i, 2 * m + 1)
                        divided(a[0], i, l)
                        positive_keys(a[1], i, l)
                        scale(f[0], i, 2 * m + 3)
                        positive_queries(a[1], i, l)
                        leave(f[0], i, 0)
                        masked(a[1], i, l)
                        leave(f[0], i, 1)
                        stats(f[0], i, LAST + 1)
                        move(a[0], i, 2 * l + 1)
                        divided(a[1], i, l)
                        scale(f[0], i, LAST + 1)
                        move(f[1], i, 2 * m + 2)
                        stats(f[0], i + 1, 0)
                        scale(a[0], i, 2 * l + 2)
                        tokensT(f[0], i)
                        scale(f[1], i, 2 * m + 3)
                        move(a[1], i, 2 * l + 1)
                        leave(f[1], i, 0)
                        leave(f[1], i, 1)
                        low_part(a[0], i, 2 * l + 1)
                        stats(f[1], i, LAST + 1)
                    elif m < LAYERS:
                        scale(f[1], i, 2 * m + 2)
                        scale(a[0], i + 1, 0)
                        scale(a[1], i, LAST + 1)
                        low_part(f[1], i, 2 * m + 1)
                        enter(a[0], i + 1, 0)
                        tokensT(a[1], i)
                        stats(a[1], i + 1, 0)
                        route(a, i, 0)
                        route(a, i, 1)
                        gate_up(a[1], i, 0)
                        move(f[1], i, 2 * m + 2)
                        scale(a[1], i + 1, 0)
                        enter(a[0], i + 1, 1)
                        gate_up(a[0], i, 0)
                        enter(a[1], i + 1, 0)
                        scale(f[1], i, LAST)
                        weigh(a[1], i, 0)
                        leave(f[1], i, 0)
                        move(f[0], i, 2 * m + 2)
                        leave(f[1], i, 1)
                        weigh(a[0], i, 0)
                        gate_up(a[1], i, 1)
                        stats(f[1], i, LAST + 1)
                        weigh(a[1], i, 1)
                        gate_up(a[0], i, 1)
                        scale(f[0], i, LAST)
                        scale(f[1], i, LAST + 1)
                        weigh(a[0], i, 1)
                        gate_up(a[1], i, 2)
                        leave(f[0], i, 0)
                        enter(a[1], i + 1, 1)
                        leave(f[0], i, 1)
                        stats(f[0], i, LAST + 1)
                        gate_up(a[0], i, 2)
                        tokensT(f[1], i)
                        scale(f[0], i, LAST + 1)
                        stats(f[0], i + 1, 0)
                        finish(a[1], i, 0)
                        scale(a[1], i + 1, 1)
                        finish(a[1], i, 1)
                        finish(a[0], i, 0)
                        scale(a[0], i + 1, 1)
                        low_part(a[1], i + 1, 0)
                        tokensT(f[0], i)
                        finish(a[0], i, 1)
                        low_part(a[0], i + 1, 0)
                        route(f, i, 0)
                        route(f, i, 1)
                        gate_up(f[1], i, 0)
                        positive_keys(a[1], i + 1, 0)
                        gate_up(f[0], i, 0)
                        stats(f[1], i + 1, 0)
                        positive_keys(a[0], i + 1, 0)
                        weigh(f[1], i, 0)
                        positive_queries(a[1], i + 1, 0)
                        masked(a[1], i + 1, 0)
                        positive_queries(a[0], i + 1, 0)
                        masked(a[0], i + 1, 0)
                        weigh(f[0], i, 0)
                        scale(f[1], i + 1, 0)
                        divided(a[0], i + 1, 0)
                        gate_up(f[1], i, 1)
                        divided(a[1], i + 1, 0)
                        weigh(f[1], i, 1)
                        enter(f[1], i + 1, 0)
                    else:
                        gate_up(a[0], i, 1)
                        enter(a[1], i + 1, 1)
                        weigh(a[0], i, 1)
                        gate_up(a[1], i, 2)
                        scale(a[0], i + 1, 0)
                        move(f[1], i + 1, 1)
                        move(f[0], i + 1, 1)
                        enter(a[0], i + 1, 0)
                        gate_up(a[0], i, 2)
                        enter(a[0], i + 1, 1)
                        scale(f[1], i + 1, 2)
                        finish(a[1], i, 0)
                        scale(a[1], i + 1, 1)
                        finish(a[1], i, 1)
                        scale(f[0], i + 1, 2)
                        finish(a[0], i, 0)
                        scale(a[0], i + 1, 1)
                        finish(a[0], i, 1)

        @block.tensor
        def _(pe):
            def mm(o, lhsT, rhs, start=True, stop=True):
                return pe.matmul(o, lhsT, rhs, start=start, stop=stop)

            pe.wait_ge(s_k, 32)
            pe.transpose(A.ps[:, 0, 0:BATCH], c_in[:, :], ident[0:BATCH, 0:BATCH]).then_inc(s_parps, 1)
            pe.wait_ge(s_condT, 1)
            pe.wait_ge(s_wm, 16)
            mm(A.ps[0:BATCH, 0, :], condT[:, :], wm[:, 0:512])
            mm(A.ps[0:BATCH, 1, 0:6 * D - 512], condT[:, :], wm[:, 512:6 * D])
            mm(B.ps[:, 0, 0:BATCH], wm[:, 3 * D:4 * D], condT[:, :])
            mm(B.ps[:, 0, BATCH:2 * BATCH], wm[:, 4 * D:5 * D], condT[:, :]).then_inc(s_modps, 1)
            pe.wait_ge(s_par, 16 * 4)
            pe.transpose(B.ps[:, 1, 0:4 * LAYERS], par[:, :], ident[0:4 * LAYERS, 0:4 * LAYERS]).then_inc(s_parps, 1)

            def fold_weights(first, end):
                for n in range(first, end):
                    l, k = n // 2, n % 2
                    w, width = (wqkv[:, l, :], QKV) if k == 0 else (w1[:, l, :], FF)
                    pe.wait_ge((s_wqkv, s_w1)[k], (48, 16)[k])
                    pe.wait_ge(s_fold, n + 1)
                    if n >= 4:
                        pe.wait_ge(s_folded, n - 3)
                    mm(chains[2 + k].ps[:, l % 2, 0:width], fold[:, n, :], w).then_inc(s_foldps, 1)

            fold_weights(0, 4)
            pe.wait_ge(s_low, 1)
            pe.wait_ge(s_const, 10)

            def transposes(b, i, n):
                norm, src = (n + 1, b.xn) if n < 2 * LAYERS else (LAST + 1, b.z)
                pe.wait_ge(b.s_normed.sem, b.s_normed.value(i, norm + 1))
                for t in range(TILES):
                    last = pe.transpose(b.ps[:, n % 2, t * P:(t + 1) * P], src[:, t, :], ident)
                last.then_inc(b.s_tps.sem, 1)

            def exact(b, o, w_hi, w_lo):
                mm(o, w_hi, b.x_hi[:, :], stop=False)
                mm(o, w_lo, b.x_hi[:, :], start=False, stop=False)
                return mm(o, w_hi, b.x_lo[:, :], start=False)

            def project_keys(b, i, l):
                pe.wait_ge(b.s_xT.sem, b.s_xT.value(i, 2 * l + 1))
                for t in range(TILES):
                    o, tok = b.ps[:, 1, t * 2 * D:(t + 1) * 2 * D], slice(t * P, (t + 1) * P)
                    mm(o, b.x_hi[:, tok], wqkv_hi[:, l, D:QKV], stop=False)
                    mm(o, b.x_hi[:, tok], wqkv_lo[:, l, D:QKV], start=False, stop=False)
                    if t == 0:
                        pe.wait_ge(b.s_x_lo.sem, b.s_x_lo.value(i, 2 * l + 1))
                    last = mm(o, b.x_lo[:, tok], wqkv_hi[:, l, D:QKV], start=False)
                last.then_inc(b.s_qkvps.sem, 1)

            def project_queries(b, i, l):
                exact(b, b.ps[:, 0, 0:T], wqkv_hi[:, l, 0:D], wqkv_lo[:, l, 0:D]).then_inc(b.s_qkvps.sem, 1)

            def sums(b, i, l):
                pe.wait_ge(b.s_pos.sem, b.s_pos.value(i, 2 * l + 1))
                for t in range(TILES):
                    last = mm(b.ps[:, 1, 0:VW], b.kp[:, t, :], b.v[:, t, :], start=t == 0, stop=t == TILES - 1)
                last.then_inc(b.s_sumps.sem, 1)

            def attend(b, i, l):
                pe.wait_ge(b.s_pos.sem, b.s_pos.value(i, 2 * l + 2))
                pe.wait_ge(b.s_kv.sem, b.s_kv.value(i, l + 1))
                for t in range(TILES):
                    last = mm(b.ps[:, 0, t * 2 * D:t * 2 * D + VW], b.qp[:, t * P:(t + 1) * P], b.kv[:, :])
                last.then_inc(b.s_attps.sem, 1)

            def out_project(b, i, l):
                pe.wait_ge(b.s_att.sem, b.s_att.value(i, 3 * l + 3))
                for t in range(TILES):
                    last = pe.transpose(b.ps[:, 1, t * P:(t + 1) * P], b.att[:, t, :], ident)
                last.then_inc(b.s_atps.sem, 1)

            def out_project2(b, i, l):
                pe.wait_ge(b.s_attT.sem, b.s_attT.value(i, l + 1))
                for t in range(TILES):
                    last = mm(b.ps[:, 0, t * P:(t + 1) * P], b.attT[:, t * P:(t + 1) * P], wo[:, l, :])
                last.then_inc(b.s_wops.sem, 1)

            def expand(b, i, l, k):
                pe.wait_ge(b.s_xT.sem, b.s_xT.value(i, 2 * l + 2))
                pe.wait_ge(b.s_x_lo.sem, b.s_x_lo.value(i, 2 * l + 2))
                for c in (2 * k, 2 * k + 1):
                    last = exact(b, b.ps[:, k, c % 2 * T:(c % 2 + 1) * T], w1_hi[:, l, c * P:(c + 1) * P],
                                 w1_lo[:, l, c * P:(c + 1) * P])
                last.then_inc(b.s_w1ps.sem, 1)

            def contract(b, i, l):
                pe.wait_ge(b.s_h.sem, b.s_h.value(i, (l + 1) * PAIRS))
                for t in range(TILES):
                    for c in range(CH):
                        last = mm(b.ps[:, 0, t * P:(t + 1) * P], b.h[:, c, t * P:(t + 1) * P], w2[:, l, c, :],
                                  start=c == 0, stop=c == CH - 1)
                last.then_inc(b.s_w2ps.sem, 1)

            def logits(b, i):
                transposes(b, i, 2 * LAYERS)

            def logits2(b, i):
                pe.wait_ge(b.s_xT.sem, b.s_xT.value(i, 2 * LAYERS + 1))
                for t in range(TILES):
                    last = mm(b.ps[:, 1, t * EXPERTS:(t + 1) * EXPERTS], b.xT[:, t * P:(t + 1) * P], wr[:, :])
                last.then_inc(b.s_eps.sem, 1)

            def two(b, bank, w, k):
                for j, c in enumerate(range(2 * k, min(2 * k + 2, CH + 1))):
                    last = mm(b.ps[:, bank, j * T:(j + 1) * T], w[:, c, :], b.xT[:, :])
                last.then_inc(b.s_eps.sem, 1)

            def gate(b, i, k):
                if k == 1:
                    pe.wait_ge(b.s_eact.sem, b.s_eact.of(EXPERT_ACT, "coefT", i))
                elif k == 2:
                    pe.wait_ge(b.s_units.sem, b.s_units.of(EXPERT_UNITS, "product1", i))
                two(b, k % 2, wg, k)

            def up(b, i, k):
                if k == 0:
                    pe.wait_ge(b.s_route.sem, b.s_route.value(i, 1))
                else:
                    pe.wait_ge(b.s_units.sem, b.s_units.of(EXPERT_UNITS, f"weighed{k - 1}", i))
                two(b, 1 - k % 2, wu, k)

            def coef_transposes(b, i):
                pe.wait_ge(b.s_route.sem, b.s_route.value(i, b.s_route.per))
                pe.wait_ge(b.s_units.sem, b.s_units.of(EXPERT_UNITS, "product0", i))
                for t in range(TILES):
                    last = pe.transpose(b.ps[0:S_ROWS, 1, t * P:(t + 1) * P],
                                        b.parts[:, t, :, :].rearrange("p k e -> p (k e)").bitcast(F32), ident)
                last.then_inc(b.s_eps.sem, 1)

            def spread(b, i, k):
                pe.wait_ge(b.s_eact.sem, b.s_eact.of(EXPERT_ACT, "coefT", i))
                pe.wait_ge(b.s_eact.sem, b.s_eact.of(EXPERT_ACT, f"silu{k}", i))
                for j in range(2):
                    c = 2 * k + j
                    last = mm(b.ps[:, k % 2, j * T:(j + 1) * T], sel_hi[:, c * P:(c + 1) * P], b.coefT[:, :])
                last.then_inc(b.s_eps.sem, 1)

            def down(b, i):
                pe.wait_ge(b.s_units.sem, b.s_units.of(EXPERT_UNITS, f"product{PAIRS}", i))
                for t in range(TILES):
                    tok = slice(t * P, (t + 1) * P)
                    for c in range(CH + 1):
                        hid = b.h[:, c, tok] if c < CH else b.hs[:, tok]
                        last = mm(b.ps[:, 0, tok], hid, wd[:, c, :], start=c == 0, stop=c == CH)
                last.then_inc(b.s_eps.sem, 1)

            a, _, f, _ = phase(0)
            fold_weights(4, 2 * LAYERS)
            transposes(a[0], 0, 0)
            transposes(a[1], 0, 0)
            project_keys(a[0], 0, 0)
            project_queries(a[0], 0, 0)
            project_keys(a[1], 0, 0)
            project_queries(a[1], 0, 0)
            sums(a[0], 0, 0)
            sums(a[1], 0, 0)
            attend(a[0], 0, 0)
            attend(a[1], 0, 0)
            out_project(a[0], 0, 0)
            pe.wait_ge(s_lessmean, 3)
            out_project2(a[0], 0, 0)
            out_project(a[1], 0, 0)
            out_project2(a[1], 0, 0)
            pe.wait_ge(s_low, 2)
            pe.wait_ge(s_folded, 2 * LAYERS)
            with pe.Fori(0, STEPS) as i:
                for n in range(1, PHASES):
                    a, l, f, m = phase(n)
                    if n == 1:
                        transposes(a[1], i, 0)
                        transposes(f[0], i, 1)
                        transposes(a[0], i, 0)
                        transposes(f[1], i, 1)
                        project_keys(a[1], i, 0)
                        project_queries(a[1], i, 0)
                        project_keys(a[0], i, 0)
                        expand(f[0], i, 0, 0)
                        expand(f[0], i, 0, 1)
                        project_queries(a[0], i, 0)
                        expand(f[1], i, m, 0)
                        sums(a[0], i, 0)
                        expand(f[1], i, m, 1)
                        attend(a[0], i, 0)
                        pe.wait_ge(s_w2, 2 * LAYERS)
                        contract(f[0], i, 0)
                        out_project(a[0], i, l)
                        sums(a[1], i, l)
                    elif n < PHASES - 3:
                        pe.wait_ge(s_low, 2 * LAYERS)
                        out_project2(f[0], i, m)
                        attend(f[1], i, m)
                        contract(a[1], i, l - 1)
                        out_project(f[1], i, m)
                        transposes(a[0], i, 2 * l)
                        transposes(f[0], i, 2 * m + 1)
                        out_project2(f[1], i, m)
                        project_keys(a[0], i, l)
                        project_queries(a[0], i, l)
                        expand(f[0], i, m, 0)
                        transposes(a[1], i, 2 * l)
                        expand(f[0], i, m, 1)
                        sums(a[0], i, l)
                        project_keys(a[1], i, l)
                        project_queries(a[1], i, l)
                        transposes(f[1], i, 2 * m + 1)
                        attend(a[0], i, l)
                        contract(f[0], i, m)
                        out_project(a[0], i, l)
                        expand(f[1], i, m, 0)
                        sums(a[1], i, l)
                        expand(f[1], i, m, 1)
                    elif l < LAYERS:
                        pe.wait_ge(s_wmoe, 16 * 7)
                        pe.wait_ge(s_ones, 1)
                        out_project2(f[0], i, m)
                        attend(f[1], i, m)
                        contract(a[1], i, l - 1)
                        out_project(f[1], i, m)
                        transposes(a[0], i, 2 * l)
                        transposes(f[0], i, 2 * m + 1)
                        out_project2(f[1], i, m)
                        project_keys(a[0], i, l)
                        expand(f[0], i, m, 0)
                        expand(f[0], i, m, 1)
                        project_queries(a[0], i, l)
                        sums(a[0], i, l)
                        transposes(a[1], i, 2 * l)
                        contract(f[0], i, m)
                        transposes(f[1], i, 2 * m + 1)
                        attend(a[0], i, l)
                        project_keys(a[1], i, l)
                        project_queries(a[1], i, l)
                        expand(f[1], i, m, 0)
                        out_project(a[0], i, l)
                        sums(a[1], i, l)
                        expand(f[1], i, m, 1)
                    elif m < LAYERS:
                        out_project2(f[0], i, m)
                        attend(f[1], i, m)
                        contract(a[1], i, l - 1)
                        out_project(f[1], i, m)
                        logits(a[0], i)
                        out_project2(f[1], i, m)
                        transposes(f[0], i, 2 * m + 1)
                        logits2(a[0], i)
                        gate(a[0], i, 0)
                        expand(f[0], i, m, 0)
                        transposes(f[1], i, 2 * m + 1)
                        expand(f[0], i, m, 1)
                        logits(a[1], i)
                        expand(f[1], i, m, 0)
                        expand(f[1], i, m, 1)
                        logits2(a[1], i)
                        gate(a[1], i, 0)
                        up(a[1], i, 0)
                        contract(f[1], i, m)
                        up(a[0], i, 0)
                        contract(f[0], i, m)
                        coef_transposes(a[1], i)
                        spread(a[1], i, 0)
                        coef_transposes(a[0], i)
                        gate(a[1], i, 1)
                        spread(a[0], i, 0)
                        up(a[1], i, 1)
                        spread(a[1], i, 1)
                        gate(a[0], i, 1)
                        up(a[0], i, 1)
                        spread(a[0], i, 1)
                        gate(a[1], i, 2)
                        up(a[1], i, 2)
                        logits(f[1], i)
                        gate(a[0], i, 2)
                        up(a[0], i, 2)
                        down(a[1], i)
                        down(a[0], i)
                        logits(f[0], i)
                        transposes(a[1], i + 1, 0)
                        logits2(f[1], i)
                        transposes(a[0], i + 1, 0)
                        project_keys(a[1], i + 1, 0)
                        logits2(f[0], i)
                        gate(f[1], i, 0)
                        gate(f[0], i, 0)
                        up(f[1], i, 0)
                        project_queries(a[1], i + 1, 0)
                    else:
                        up(a[0], i, 0)
                        project_keys(f[0], i + 1, 0)
                        project_queries(f[0], i + 1, 0)
                        coef_transposes(a[1], i)
                        sums(f[1], i + 1, 0)
                        coef_transposes(a[0], i)
                        spread(a[1], i, 0)
                        gate(a[1], i, 1)
                        sums(f[0], i + 1, 0)
                        spread(a[0], i, 0)
                        up(a[1], i, 1)
                        attend(f[0], i + 1, 0)
                        attend(f[1], i + 1, 0)
                        gate(a[0], i, 1)
                        up(a[0], i, 1)
                        spread(a[1], i, 1)
                        gate(a[1], i, 2)
                        out_project(f[0], i + 1, 0)
                        out_project(f[1], i + 1, 0)
                        spread(a[0], i, 1)
                        out_project2(f[0], i + 1, 0)
                        up(a[1], i, 2)
                        out_project2(f[1], i + 1, 0)
                        gate(a[0], i, 2)
                        up(a[0], i, 2)
                        down(a[1], i)
                        down(a[0], i)


_INS = ["attn_x_in", "attn_Wq", "attn_bq", "attn_Wk", "attn_bk", "attn_Wv", "attn_bv", "attn_Wo", "attn_bo",
        "attn_W1", "attn_b1", "attn_W2", "attn_b2", "attn_ln1_s", "attn_ln1_b", "attn_ln2_s", "attn_ln2_b",
        "attn_lnf_s", "attn_lnf_b", "ffn_router", "ffn_experts_gate", "ffn_experts_up", "ffn_experts_down",
        "ffn_shared_gate", "ffn_shared_up", "ffn_shared_down", "c", "wmod"]


def build(nc, inputs):
    arrays, args = {}, []
    for name in _INS:
        arrays["in_" + name] = np.ascontiguousarray(inputs["L0_" + name])
    arrays["in_consts"] = constants()
    arrays["in_selectors"] = selectors()
    for name, a in arrays.items():
        args.append(nc.dram_tensor(name, a.shape, mybir.dt.from_np(a.dtype), kind="ExternalInput").ap())
    args.append(nc.dram_tensor("out", (BATCH, T, D), F32, kind="ExternalOutput").ap())
    args.append(nc.dram_tensor("modulation_rows", (BATCH, MOD), F32, kind="Internal").ap())
    program(nc, *args)
    return arrays


def kernel(**inputs):
    from concourse.bacc import Bacc
    from concourse.bass_utils import run_bass_kernel_spmd

    nc = Bacc("TRN2", target_bir_lowering=False, num_devices=1)
    arrays = build(nc, inputs)
    return run_bass_kernel_spmd(nc, [arrays], core_ids=[0]).results[0]["out"]
```
